# Optimizing a Trainium2 kernel written in Bass

```python
import numpy as np
import jax
import jax.numpy as jnp

def _softmax(x, axis=-1):
    return jax.nn.softmax(x, axis=axis)

def _gelu(x):
    return jax.nn.gelu(x, approximate=True)

def _silu(x):
    return jax.nn.silu(x)

def _sigmoid(x):
    return jax.nn.sigmoid(x)

def _layernorm(x, axis=-1, eps=1e-05):
    m = jnp.mean(x, axis=axis, keepdims=True)
    v = jnp.var(x, axis=axis, keepdims=True)
    return (x - m) / jnp.sqrt(v + eps)

def _scatter_add(tgt, idx, src, axis=0):
    return tgt.at[idx].add(src)

def _segment_sum(src, seg, n):
    return jax.ops.segment_sum(src, seg, n)
kernel_name = 'mk_audio_tower_d2_tok_audfeat512_r4_4d01a3'

def setup_inputs(seed: int=0):
    np.random.seed(seed)
    _w = jnp.asarray

    def _rec_inputs():
        import jax
        import jax.numpy as jnp
        _rk = jax.random.key(seed)
        x = -0.000392918 + 0.999932 * jax.random.normal(jax.random.fold_in(_rk, 1), (16, 750, 128), jnp.float32)
        return x
    x = _rec_inputs()

    def _L0_tok_setup():
        import jax, jax.numpy as jnp
        import numpy as np
        from jax import lax
        B, T, D = (32, 256, 128)
        UNITS, WINDOW = (128, 3)
        key = jax.random.key(seed)
        k1, k2 = jax.random.split(key)
        x = jax.random.normal(k1, (B, T, D), dtype=jnp.float32)
        kernel = jax.random.normal(k2, (WINDOW, D, UNITS * 3), dtype=jnp.float32) * 0.05
        return {'x': x, 'kernel': kernel}
    _L0_tok_all = _L0_tok_setup()
    _L0_tok_in = {k: v for k, v in _L0_tok_all.items() if k in ('kernel',)}
    del _L0_tok_all

    def _L0_attn_setup():
        import jax, jax.numpy as jnp
        import numpy as np
        NUM_HEADS = 8
        key = jax.random.key(seed)
        k1, k2, k3 = jax.random.split(key, 3)
        B, N, C = (4, 512, 128)
        x = jax.random.normal(k1, (B, N, C), dtype=jnp.float32)
        q_w = jax.random.normal(k2, (C, C), dtype=jnp.float32) * 0.02
        kv_w = jax.random.normal(k3, (2 * C, C), dtype=jnp.float32) * 0.02
        return {'x': x, 'q_w': q_w, 'kv_w': kv_w}
    _L0_attn_all = _L0_attn_setup()
    _L0_attn_in = {k: v for k, v in _L0_attn_all.items() if k in ('q_w', 'kv_w')}
    del _L0_attn_all

    def _L0_ffn_setup():
        import jax, jax.numpy as jnp
        import numpy as np
        B, L, H, E, F, C = (8, 2048, 128, 8, 256, 2)
        key = jax.random.key(seed)
        ks = jax.random.split(key, 4)
        x = jax.random.normal(ks[0], (B, L, H), jnp.float32)
        Wg = jax.random.normal(ks[1], (H, E), jnp.float32) * H ** (-0.5)
        W1 = jax.random.normal(ks[2], (E, H, F), jnp.float32) * H ** (-0.5)
        b1 = jnp.zeros((E, F), jnp.float32)
        W2 = jax.random.normal(ks[3], (E, F, H), jnp.float32) * F ** (-0.5)
        b2 = jnp.zeros((E, H), jnp.float32)
        return {'x': x, 'Wg': Wg, 'W1': W1, 'b1': b1, 'W2': W2, 'b2': b2}
    _L0_ffn_all = _L0_ffn_setup()
    _L0_ffn_in = {k: v for k, v in _L0_ffn_all.items() if k in ('Wg', 'W1', 'b1', 'W2', 'b2')}
    del _L0_ffn_all

    def _L1_attn_setup():
        import jax, jax.numpy as jnp
        import numpy as np
        DIM = 128
        HEADS = 8
        DIM_HEAD = 64
        SLICE = 32
        INNER = HEADS * DIM_HEAD
        key = jax.random.key(seed)
        ks = jax.random.split(key, 8)
        B, N = (8, 2048)
        s = 0.02
        return {'x': jax.random.normal(ks[0], (B, N, DIM), dtype=jnp.float32), 'W_in': jax.random.normal(ks[1], (DIM, INNER), dtype=jnp.float32) * s, 'b_in': jnp.zeros((INNER,), dtype=jnp.float32), 'Wq': jax.random.normal(ks[2], (DIM_HEAD, SLICE), dtype=jnp.float32) * s, 'Wk': jax.random.normal(ks[3], (DIM_HEAD, SLICE), dtype=jnp.float32) * s, 'Wv': jax.random.normal(ks[4], (DIM_HEAD, DIM_HEAD), dtype=jnp.float32) * s, 'W_out': jax.random.normal(ks[5], (INNER, DIM), dtype=jnp.float32) * s, 'b_out': jnp.zeros((DIM,), dtype=jnp.float32)}
    _L1_attn_all = _L1_attn_setup()
    _L1_attn_in = {k: v for k, v in _L1_attn_all.items() if k in ('W_in', 'b_in', 'Wq', 'Wk', 'Wv', 'W_out', 'b_out')}
    del _L1_attn_all

    def _L1_ffn_setup():
        import jax, jax.numpy as jnp
        import numpy as np
        B, S, D, F, E, NS, K = (2, 512, 128, 512, 8, 2, 2)
        key = jax.random.key(seed)
        ks = jax.random.split(key, 6)
        scale = 0.02

        def p(k, shape):
            return jax.random.normal(k, shape, jnp.float32) * scale
        return {'x': jax.random.normal(ks[0], (B, S, D), jnp.float32), 'gate_w': p(ks[1], (E, D)), 'gate_b': jnp.zeros((E,), jnp.float32), 'sw1': p(ks[2], (NS, F, D)), 'sb1': jnp.zeros((NS, F), jnp.float32), 'sw2': p(ks[3], (NS, D, F)), 'sb2': jnp.zeros((NS, D), jnp.float32), 'rw1': p(ks[4], (E, F, D)), 'rb1': jnp.zeros((E, F), jnp.float32), 'rw2': p(ks[5], (E, D, F)), 'rb2': jnp.zeros((E, D), jnp.float32)}
    _L1_ffn_all = _L1_ffn_setup()
    _L1_ffn_in = {k: v for k, v in _L1_ffn_all.items() if k in ('gate_w', 'gate_b', 'sw1', 'sb1', 'sw2', 'sb2', 'rw1', 'rb1', 'rw2', 'rb2')}
    del _L1_ffn_all
    return {'x': x, 'L0_tok_kernel': _L0_tok_in['kernel'], 'L0_attn_q_w': _L0_attn_in['q_w'], 'L0_attn_kv_w': _L0_attn_in['kv_w'], 'L0_ffn_Wg': _L0_ffn_in['Wg'], 'L0_ffn_W1': _L0_ffn_in['W1'], 'L0_ffn_b1': _L0_ffn_in['b1'], 'L0_ffn_W2': _L0_ffn_in['W2'], 'L0_ffn_b2': _L0_ffn_in['b2'], 'L1_attn_W_in': _L1_attn_in['W_in'], 'L1_attn_b_in': _L1_attn_in['b_in'], 'L1_attn_Wq': _L1_attn_in['Wq'], 'L1_attn_Wk': _L1_attn_in['Wk'], 'L1_attn_Wv': _L1_attn_in['Wv'], 'L1_attn_W_out': _L1_attn_in['W_out'], 'L1_attn_b_out': _L1_attn_in['b_out'], 'L1_ffn_gate_w': _L1_ffn_in['gate_w'], 'L1_ffn_gate_b': _L1_ffn_in['gate_b'], 'L1_ffn_sw1': _L1_ffn_in['sw1'], 'L1_ffn_sb1': _L1_ffn_in['sb1'], 'L1_ffn_sw2': _L1_ffn_in['sw2'], 'L1_ffn_sb2': _L1_ffn_in['sb2'], 'L1_ffn_rw1': _L1_ffn_in['rw1'], 'L1_ffn_rb1': _L1_ffn_in['rb1'], 'L1_ffn_rw2': _L1_ffn_in['rw2'], 'L1_ffn_rb2': _L1_ffn_in['rb2']}

def reference(x, L0_tok_kernel, L0_attn_q_w, L0_attn_kv_w, L0_ffn_Wg, L0_ffn_W1, L0_ffn_b1, L0_ffn_W2, L0_ffn_b2, L1_attn_W_in, L1_attn_b_in, L1_attn_Wq, L1_attn_Wk, L1_attn_Wv, L1_attn_W_out, L1_attn_b_out, L1_ffn_gate_w, L1_ffn_gate_b, L1_ffn_sw1, L1_ffn_sb1, L1_ffn_sw2, L1_ffn_sb2, L1_ffn_rw1, L1_ffn_rb1, L1_ffn_rw2, L1_ffn_rb2):
    import jax
    import jax.numpy as jnp

    def _L0_tok_ref(x, kernel):
        import jax, jax.numpy as jnp
        import numpy as np
        from jax import lax
        B, T, D = (32, 256, 128)
        UNITS, WINDOW = (128, 3)
        units = kernel.shape[2] // 3
        conv = lax.conv_general_dilated(x, kernel, window_strides=(1,), padding='VALID', dimension_numbers=('NWC', 'WIO', 'NWC'))
        Z = conv[..., :units]
        F = conv[..., units:2 * units]
        O = conv[..., 2 * units:]
        z = jnp.tanh(Z)
        f = jax.nn.sigmoid(F)
        o = jax.nn.sigmoid(O)

        def step(c, zfo):
            z_t, f_t, o_t = zfo
            c_t = f_t * c + (1.0 - f_t) * z_t
            return (c_t, o_t * c_t)
        c0 = jnp.zeros((x.shape[0], units), dtype=x.dtype)
        zf = (z.transpose(1, 0, 2), f.transpose(1, 0, 2), o.transpose(1, 0, 2))
        _, hs = lax.scan(step, c0, zf)
        return hs.transpose(1, 0, 2)

    def _L0_attn_ref(x, q_w, kv_w):
        import jax, jax.numpy as jnp
        import numpy as np
        NUM_HEADS = 8
        B, N, C = x.shape
        H = NUM_HEADS
        D = C // H
        halfB = B // 2
        q = (x @ q_w.T).reshape(B, N, H, D)
        kv = (x @ kv_w.T).reshape(B, N, 2, H, D)
        k, v = (kv[:, :, 0], kv[:, :, 1])
        k = jnp.concatenate([k[halfB:], k[:halfB]], axis=0)
        v = jnp.concatenate([v[halfB:], v[:halfB]], axis=0)
        scores = jnp.einsum('bnhd,bmhd->bhnm', q, k) / jnp.sqrt(jnp.float32(C))
        prob = jax.nn.softmax(scores, axis=-1)
        out = jnp.einsum('bhnm,bmhd->bndh', prob, v).reshape(B, N, C)
        return out

    def _L0_ffn_ref(x, Wg, W1, b1, W2, b2):
        import jax, jax.numpy as jnp
        import numpy as np
        B, L, H, E, F, C = (8, 2048, 128, 8, 256, 2)
        b, l, h = x.shape
        e = Wg.shape[1]
        k = min(max(int(l * C / e), 1), l)
        S = jax.nn.softmax(x @ Wg, axis=-1)
        St = jnp.swapaxes(S, 1, 2)
        G, I = jax.lax.top_k(St, k)
        ex = jnp.take_along_axis(x[:, None], I[..., None], axis=2)
        hmid = jax.nn.gelu(jnp.einsum('bekh,ehf->bekf', ex, W1) + b1[None, :, None, :], approximate=False)
        out = jnp.einsum('bekf,efh->bekh', hmid, W2) + b2[None, :, None, :]
        vals = G[..., None] * out
        new_x = jnp.zeros_like(x).at[jnp.arange(b)[:, None, None], I].add(vals)
        return new_x

    def _L1_attn_ref(x, W_in, b_in, Wq, Wk, Wv, W_out, b_out):
        import jax, jax.numpy as jnp
        import numpy as np
        DIM = 128
        HEADS = 8
        DIM_HEAD = 64
        SLICE = 32
        INNER = HEADS * DIM_HEAD
        B, N, C = x.shape
        x_mid = (x @ W_in + b_in).reshape(B, N, HEADS, DIM_HEAD).transpose(0, 2, 1, 3)
        q = x_mid @ Wq
        k = x_mid @ Wk
        v = x_mid @ Wv
        q = jax.nn.softmax(q, axis=-1)
        k = jax.nn.softmax(k, axis=-2)
        kv = jnp.einsum('bhns,bhnc->bhsc', k, v)
        qkv = jnp.einsum('bhns,bhsc->bhnc', q, kv)
        qkv = qkv.transpose(0, 2, 1, 3).reshape(B, N, INNER)
        return qkv @ W_out + b_out

    def _L1_ffn_ref(x, gate_w, gate_b, sw1, sb1, sw2, sb2, rw1, rb1, rw2, rb2):
        import jax, jax.numpy as jnp
        import numpy as np
        B, S, D, F, E, NS, K = (2, 512, 128, 512, 8, 2, 2)
        b, s, d = x.shape
        t = x.reshape(-1, d)
        T = t.shape[0]
        hs = jax.nn.gelu(jnp.einsum('td,nfd->ntf', t, sw1) + sb1[:, None, :], approximate=False)
        shared = jnp.einsum('ntf,ndf->td', hs, sw2) + sb2.sum(axis=0)
        logits = t @ gate_w.T + gate_b
        probs = jax.nn.softmax(logits, axis=-1)
        top_v, top_i = jax.lax.top_k(probs, K)
        cw = jnp.zeros_like(probs).at[jnp.arange(T)[:, None], top_i].add(top_v)
        hr = jax.nn.gelu(jnp.einsum('td,efd->etf', t, rw1) + rb1[:, None, :], approximate=False)
        oe = jnp.einsum('etf,edf->etd', hr, rw2) + rb2[:, None, :]
        routed = jnp.einsum('etd,te->td', oe, cw)
        return (shared + routed).reshape(b, s, d)
    h = _L0_tok_ref(x, L0_tok_kernel)
    h = h + _L0_attn_ref(_layernorm(h, axis=-1), L0_attn_q_w, L0_attn_kv_w)
    h = h + _L0_ffn_ref(_layernorm(h, axis=-1), L0_ffn_Wg, L0_ffn_W1, L0_ffn_b1, L0_ffn_W2, L0_ffn_b2)
    h = h + _L1_attn_ref(_layernorm(h, axis=-1), L1_attn_W_in, L1_attn_b_in, L1_attn_Wq, L1_attn_Wk, L1_attn_Wv, L1_attn_W_out, L1_attn_b_out)
    h = h + _L1_ffn_ref(_layernorm(h, axis=-1), L1_ffn_gate_w, L1_ffn_gate_b, L1_ffn_sw1, L1_ffn_sb1, L1_ffn_sw2, L1_ffn_sb2, L1_ffn_rw1, L1_ffn_rb1, L1_ffn_rw2, L1_ffn_rb2)
    return h

_drawn_inputs = setup_inputs


def setup_inputs(seed=0):
    import zlib

    import numpy as np

    out = dict(_drawn_inputs(seed))
    spreads = {'L0_ffn_b1': (0.0, 0.1),
     'L0_ffn_b2': (0.0, 0.1),
     'L1_attn_b_in': (0.0, 0.409),
     'L1_attn_b_out': (0.0, 0.1),
     'L1_ffn_gate_b': (0.0, 0.1),
     'L1_ffn_sb1': (0.0, 0.1),
     'L1_ffn_sb2': (0.0, 0.1),
     'L1_ffn_rb1': (0.0, 0.55),
     'L1_ffn_rb2': (0.0, 0.1)}
    factors = {'L0_attn_q_w': 2.767,
     'L1_attn_W_in': 7.863,
     'L1_attn_Wq': 8.0,
     'L1_attn_Wk': 8.0,
     'L1_attn_Wv': 2.792,
     'L1_attn_W_out': 3.076}
    for name, (base, spread) in spreads.items():
        noise = np.random.default_rng([zlib.crc32(name.encode()), seed]).standard_normal(out[name].shape)
        drawn = base * np.exp(spread * noise) if base else spread * noise
        out[name] = jnp.asarray(drawn.astype(out[name].dtype))
    for name, factor in factors.items():
        out[name] = (out[name] * factor).astype(out[name].dtype)
    return out
```

```python
from contextlib import ExitStack

import concourse.bass as bass
from concourse import mybir

F32 = mybir.dt.float32
F32R = mybir.dt.float32r
U32 = mybir.dt.uint32
ALU = mybir.AluOpType
ACT = mybir.ActivationFunctionType
AX = mybir.AxisListType

P = 128
B = 16
T_IN = 750
WINDOW = 3
T = T_IN - WINDOW + 1
HALF = T // 2
TILES = -(-T // P)
ROWS = [min(P, T - P * c) for c in range(TILES)]
LAST = ROWS[-1]
HALVES = [slice(0, HALF), slice(HALF, T)]
EPS = 1e-5


def steps(eng, n, peel, body):
    assert (n - 2 * peel) % 2 == 0
    for k in range(peel):
        body(k, k % 2)
    with eng.Fori(0, (n - 2 * peel) // 2) as i:
        for q in range(2):
            body(i * 2 + (peel + q), (peel + q) % 2)
    for k in range(n - peel, n):
        body(k, k % 2)


def at_least(k, low):
    return not isinstance(k, int) or k >= low


def before(k, high):
    return not isinstance(k, int) or k < high


def semaphores(nc, ctx, tag=""):
    made = []

    def clear():
        with nc.Block() as block:
            @block.sync
            def _(sp):
                for s in made:
                    sp.sem_clear(s)
        for s in made:
            nc.release_semaphore(s)

    def sem(name):
        made.append(nc.alloc_semaphore(f"{name}{tag}"))
        return made[-1]

    ctx.callback(clear)
    return sem


class Shared:
    pass

def steps3(eng, n, low, high, body):
    assert (n - low - high) % 3 == 0
    for k in range(low):
        body(k, k % 3)
    with eng.Fori(0, (n - low - high) // 3) as i:
        for q in range(3):
            body(i * 3 + (low + q), (low + q) % 3)
    for k in range(n - high, n):
        body(k, k % 3)


def row_statistics(nc, g, tag):
    N = B * TILES
    STEP = 8
    with ExitStack() as ctx:
        def sb(name, shape):
            return ctx.enter_context(nc.sbuf_tensor(f"{name}_{tag}", shape, F32))
        stats = sb("stats", [P, N, 6])
        diff, spread, std = sb("diff", [P, N]), sb("spread", [P, N]), sb("std", [P, N])
        sem = semaphores(nc, ctx, "_" + tag)
        stats_done, sums_done, std_done = sem("stats_done"), sem("sums_done"), sem("std_done")
        eps = sb("eps", [P, 1])
        half = P // 2
        with nc.Block() as block:
            @block.vector
            def _(dve):
                dve.memset(eps[:, :], EPS)
                with dve.Fori(0, N // STEP) as i:
                    for q in range(STEP):
                        dve.bn_stats(stats[:, bass.ds(i * STEP + q, 1), :].rearrange("p o s -> p (o s)"),
                                     g.h[:, bass.ds(i * STEP + q, 1), :].rearrange("p o d -> p (o d)")
                                     ).then_inc(stats_done, 1)
                dve.wait_ge(stats_done, N)
                dve.tensor_tensor(diff[:, :], stats[:, :, 1], stats[:, :, 4], ALU.subtract)
                dve.tensor_tensor(g.mean[:, :], stats[:, :, 1], stats[:, :, 4], ALU.add)
                dve.tensor_tensor(spread[:, :], stats[:, :, 2], stats[:, :, 5], ALU.add).then_inc(sums_done, 1)
                dve.wait_ge(sums_done, 1)
                dve.tensor_scalar(g.mean[:, :], g.mean[:, :], 0.5, None, ALU.mult)
                dve.tensor_tensor(diff[:, :], diff[:, :], diff[:, :], ALU.mult).then_inc(sums_done, 1)
                dve.wait_ge(sums_done, 2)
                dve.scalar_tensor_tensor(out=spread[:, :], in0=diff[:, :], scalar=half / 2.0, in1=spread[:, :],
                                         op0=ALU.mult, op1=ALU.add).then_inc(sums_done, 1)
                dve.wait_ge(std_done, 1)
                dve.reciprocal(g.rstd[:, :], std[:, :])

            @block.scalar
            def _(act):
                act.wait_ge(sums_done, 3)
                act.activation(std[:, :], spread[:, :], ACT.Sqrt, bias=eps[:, :], scale=1.0 / P
                               ).then_inc(std_done, 1)


def normalize(pool, g, rows, b, centred, n):
    tiles = bass.ds(b * TILES, TILES)
    mean = g.mean[:, tiles].unsqueeze(2).broadcast_to([P, TILES, P])
    rstd = g.rstd[:, tiles].unsqueeze(2).broadcast_to([P, TILES, P])
    pool.tensor_tensor(rows, g.h[:, tiles, :], mean, ALU.subtract).then_inc(centred, 1)
    pool.wait_ge(centred, n)
    return pool.tensor_tensor(rows, rows, rstd, ALU.mult)


def split_weights(nc, g, jobs, tag):
    CHUNK = 4
    pieces = []
    for hi, lo, view, turned in jobs:
        for k in range(0, view.shape[1], CHUNK):
            n = min(CHUNK, view.shape[1] - k)
            pieces.append((hi[:, k:k + n, :], None if lo is None else lo[:, k:k + n, :], view[:, k:k + n, :], turned))
    turns = [sum(p[3] for p in pieces[:j + 1]) for j in range(len(pieces))]
    with ExitStack() as ctx:
        sem = semaphores(nc, ctx, "_" + tag)

        raw = ctx.enter_context(nc.sbuf_tensor(f"raw_{tag}", [P, 2, CHUNK, P], F32))
        turn = [ctx.enter_context(nc.psum_tensor(f"wturn{j}_{tag}", [P, CHUNK, P], F32)) for j in range(2)]
        loaded = [sem("w_in0"), sem("w_in1")]
        turned_n, hi_n, lo_n = sem("w_turned"), sem("w_hi"), sem("w_lo")

        def block_of(j):
            hi, lo, view, turned = pieces[j]
            rows, n, cols = view.shape
            return turn[j % 2][0:cols, 0:n, 0:rows] if turned else raw[0:rows, j % 2, 0:n, 0:cols]

        with nc.Block() as block:
            @block.sync
            def _(sp):
                for j, (hi, lo, view, turned) in enumerate(pieces):
                    rows, n, cols = view.shape
                    if j >= 2:
                        sp.wait_ge(lo_n, j - 1)
                    sp.dma_start(raw[0:rows, j % 2, 0:n, 0:cols], view).then_inc(loaded[j % 2], 16)

            @block.tensor
            def _(pe):
                for j, (hi, lo, view, turned) in enumerate(pieces):
                    rows, n, cols = view.shape
                    if not turned:
                        continue
                    pe.wait_ge(loaded[j % 2], 16 * (j // 2 + 1))
                    if j >= 2:
                        pe.wait_ge(lo_n, j - 1)
                    for c in range(n):
                        last = pe.transpose(turn[j % 2][0:cols, c, 0:rows], raw[0:rows, j % 2, c, 0:cols],
                                            g.ident[0:rows, 0:rows])
                    last.then_inc(turned_n, 1)

            def wait_for(eng, j):
                if pieces[j][3]:
                    eng.wait_ge(turned_n, turns[j])
                else:
                    eng.wait_ge(loaded[j % 2], 16 * (j // 2 + 1))

            @block.scalar
            def _(act):
                for j, (hi, lo, view, turned) in enumerate(pieces):
                    if lo is not None:
                        wait_for(act, j)
                        act.copy(hi, block_of(j)).then_inc(hi_n, 1)

            @block.vector
            def _(dve):
                rounded = 0
                for j, (hi, lo, view, turned) in enumerate(pieces):
                    if lo is None:
                        wait_for(dve, j)
                        dve.tensor_copy(hi, block_of(j)).then_inc(lo_n, 1)
                    else:
                        rounded += 1
                        dve.wait_ge(hi_n, rounded)
                        dve.tensor_tensor(lo, block_of(j), hi.bitcast(F32), ALU.subtract).then_inc(lo_n, 1)


def turn_tiles(pe, g, turn, rows):
    for c, n in enumerate(ROWS):
        last = pe.transpose(turn[:, c // 4, (c % 4) * P:(c % 4) * P + n], rows[0:n, c, :], g.ident[0:n, 0:n])
    return last


def round_cols(act, hi, turn):
    act.copy(hi[:, 0:512], turn[:, 0, :])
    return act.copy(hi[:, 512:T], turn[:, 1, 0:T - 512])


def split_cols(dve, lo, hi, turn):
    dve.tensor_tensor(lo[:, 0:512], turn[:, 0, :], hi[:, 0:512].bitcast(F32), ALU.subtract)
    return dve.tensor_tensor(lo[:, 512:T], turn[:, 1, 0:T - 512], hi[:, 512:T].bitcast(F32), ALU.subtract)


def constants(nc, ctx, g):
    g.ident = ctx.enter_context(nc.sbuf_tensor("ident", [P, P], F32))
    made = ctx.enter_context(nc.semaphore("ident_zeroed"))
    with nc.Block() as block:
        @block.gpsimd
        def _(pool):
            pool.memset(g.ident[:], 0.0).then_inc(made, 1)
            pool.wait_ge(made, 1)
            pool.affine_select(out=g.ident[:], in_=g.ident[:], compare_op=ALU.not_equal, fill=1.0, base=0,
                               pattern=[[-1, P]], channel_multiplier=1)

        @block.vector
        def _(dve):
            dve.memset(g.h[:, :, :], 0.0)


def quasi_recurrent(nc, g, x, w):
    GATES = 3
    with ExitStack() as ctx:
        def sb(name, shape, dt=F32):
            return ctx.enter_context(nc.sbuf_tensor(name, shape, dt))

        sem = semaphores(nc, ctx)

        x_rows = sb("x_rows", [P, 2, TILES, P])
        x_hi = sb("x_hi", [P, 2, T_IN], F32R)
        x_lo = sb("x_lo", [P, 2, T_IN], F32R)
        w_raw = sb("w_raw", [P, WINDOW, GATES * P])
        w_hi = sb("w_hi", [P, WINDOW, GATES * P], F32R)
        w_lo = sb("w_lo", [P, WINDOW, GATES * P], F32R)
        gates = sb("gates", [P, 2, GATES, T])
        fresh = sb("fresh", [P, 2, T])
        cell = sb("cell", [P, 2, T])
        hid = sb("hid", [P, 2, T])
        turn_in = ctx.enter_context(nc.psum_tensor("turn_in", [P, 2, 512], F32))
        conv = [ctx.enter_context(nc.psum_tensor(f"conv{k}", [P, 2, 512], F32)) for k in range(2)]
        turn_out = ctx.enter_context(nc.psum_tensor("turn_out", [P, 2, 512], F32))
        x_loaded = [sem("x_loaded0"), sem("x_loaded1")]
        w_loaded, w_rounded, w_split = sem("w_loaded"), sem("w_rounded"), sem("w_split")
        x_turned, x_rounded, x_split = sem("x_turned"), sem("x_rounded"), sem("x_split")
        conv_done, gate_done = sem("conv_done"), sem("gate_done")
        fresh_done, cell_done, hid_done = sem("fresh_done"), sem("cell_done"), sem("hid_done")
        h_turned, h_kept = sem("h_turned"), sem("h_kept")
        full_in = T_IN // P
        rows_in = [min(P, T_IN - P * c) for c in range(full_in + 1)]

        with nc.Block() as block:
            @block.sync
            def _(sp):
                sp.dma_start(w_raw[:, :, :], w.rearrange("k d n -> d k n")).then_inc(w_loaded, 16)

                def load(b, slot):
                    if at_least(b, 2):
                        sp.wait_ge(x_turned, b - 1)
                    sp.dma_start(x_rows[:, slot, 0:full_in, :],
                                 x[bass.ds(b, 1), 0:full_in * P, :].rearrange("o (c p) d -> (o p) c d", p=P)
                                 ).then_inc(x_loaded[slot], 16)
                    sp.dma_start(x_rows[0:rows_in[-1], slot, full_in, :],
                                 x[bass.ds(b, 1), full_in * P:T_IN, :].rearrange("o p d -> (o p) d")
                                 ).then_inc(x_loaded[slot], 16)
                steps(sp, B, 2, load)

            @block.tensor
            def _(pe):
                def turn(b, slot):
                    half = b // 2 if isinstance(b, int) else None
                    pe.wait_ge(x_loaded[slot], 32 * (half + 1) if half is not None else (b - slot) * 16 + 32)
                    if at_least(b, 1):
                        pe.wait_ge(x_split, b)
                    for c, n in enumerate(rows_in):
                        last = pe.transpose(turn_in[:, c // 4, (c % 4) * P:(c % 4) * P + n], x_rows[0:n, slot, c, :],
                                            g.ident[0:n, 0:n])
                    last.then_inc(x_turned, 1)

                def convolve(b, slot):
                    pe.wait_ge(x_split, b + 1)
                    for gate in range(GATES):
                        if at_least(b, 1) or gate == 2:
                            pe.wait_ge(gate_done, b * GATES + (0, -1, 1)[gate])
                        out = conv[gate % 2]
                        for h, cols in enumerate(HALVES):
                            for k in range(WINDOW):
                                for j, (a, m) in enumerate([(w_hi, x_hi), (w_hi, x_lo), (w_lo, x_hi)]):
                                    last = pe.matmul(out[:, h, 0:HALF], a[:, k, gate * P:(gate + 1) * P],
                                                     m[:, slot, cols.start + k:cols.stop + k],
                                                     start=(k == 0 and j == 0), stop=(k == WINDOW - 1 and j == 2))
                        last.then_inc(conv_done, 1)

                def turn_back(b, slot):
                    pe.wait_ge(hid_done, b + 1)
                    if at_least(b, 1):
                        pe.wait_ge(h_kept, b)
                    for c, n in enumerate(ROWS):
                        last = pe.transpose(turn_out[0:n, c // 4, (c % 4) * P:(c % 4) * P + P],
                                            hid[:, slot, c * P:c * P + n], g.ident[:, :])
                    last.then_inc(h_turned, 1)

                def step(b, slot):
                    if before(b, B - 1):
                        turn(b + 1, 1 - slot)
                    convolve(b, slot)
                    if at_least(b, 1):
                        turn_back(b - 1, 1 - slot)

                pe.wait_ge(w_split, 1)
                turn(0, 0)
                steps(pe, B, 2, step)
                turn_back(B - 1, (B - 1) % 2)

            @block.scalar
            def _(act):
                act.wait_ge(w_loaded, 16)
                act.copy(w_hi[:, :, :], w_raw[:, :, :]).then_inc(w_rounded, 1)

                def round_x(b, slot):
                    act.wait_ge(x_turned, b + 1)
                    if at_least(b, 2):
                        act.wait_ge(conv_done, b * GATES - GATES)
                    act.copy(x_hi[:, slot, 0:512], turn_in[:, 0, :]).then_inc(x_rounded, 1)
                    act.copy(x_hi[:, slot, 512:T_IN], turn_in[:, 1, 0:T_IN - 512]).then_inc(x_rounded, 1)

                def open_gates(b, slot):
                    for gate, func in enumerate([ACT.Tanh, ACT.Sigmoid, ACT.Sigmoid]):
                        act.wait_ge(conv_done, b * GATES + (gate + 1))
                        if at_least(b, 2) and gate == 0:
                            act.wait_ge(hid_done, b - 1)
                        act.activation(gates[:, slot, gate, :].rearrange("p (h n) -> p h n", h=2),
                                       conv[gate % 2][:, :, 0:HALF], func).then_inc(gate_done, 1)

                def keep(b, slot):
                    act.wait_ge(h_turned, b + 1)
                    act.copy(g.h[:, bass.ds(b * TILES, 4), :], turn_out[:, 0, :].rearrange("p (c d) -> p c d", c=4))
                    act.copy(g.h[:, bass.ds(b * TILES + 4, 1), :], turn_out[:, 1:2, 0:P])
                    act.copy(g.h[0:LAST, bass.ds(b * TILES + 5, 1), :], turn_out[0:LAST, 1:2, P:2 * P]
                             ).then_inc(h_kept, 1)

                def step(b, slot):
                    if before(b, B - 1):
                        round_x(b + 1, 1 - slot)
                    open_gates(b, slot)
                    if at_least(b, 1):
                        keep(b - 1, 1 - slot)
                round_x(0, 0)
                steps(act, B, 2, step)
                keep(B - 1, (B - 1) % 2)

            @block.vector
            def _(dve):
                dve.wait_ge(w_rounded, 1)
                dve.tensor_tensor(w_lo[:, :, :], w_raw[:, :, :], w_hi[:, :, :].bitcast(F32), ALU.subtract
                                  ).then_inc(w_split, 1)

                def split_x(b, slot):
                    dve.wait_ge(x_rounded, b * 2 + 2)
                    if at_least(b, 2):
                        dve.wait_ge(conv_done, b * GATES - GATES)
                    dve.tensor_tensor(x_lo[:, slot, 0:512], turn_in[:, 0, :], x_hi[:, slot, 0:512].bitcast(F32),
                                      ALU.subtract)
                    dve.tensor_tensor(x_lo[:, slot, 512:T_IN], turn_in[:, 1, 0:T_IN - 512],
                                      x_hi[:, slot, 512:T_IN].bitcast(F32), ALU.subtract).then_inc(x_split, 1)

                def recur(b, slot):
                    dve.wait_ge(gate_done, b * GATES + 2)
                    dve.scalar_tensor_tensor(out=fresh[:, slot, :], in0=gates[:, slot, 1, :], scalar=1.0,
                                             in1=gates[:, slot, 0, :], op0=ALU.subtract, op1=ALU.mult
                                             ).then_inc(fresh_done, 1)
                    dve.wait_ge(fresh_done, b + 1)
                    dve.tensor_tensor_scan(cell[:, slot, :], gates[:, slot, 1, :], fresh[:, slot, :], 0.0,
                                           ALU.mult, ALU.subtract).then_inc(cell_done, 1)
                    dve.wait_ge(cell_done, b + 1)
                    dve.wait_ge(gate_done, b * GATES + 3)
                    if at_least(b, 2):
                        dve.wait_ge(h_turned, b - 1)
                    dve.tensor_tensor(hid[:, slot, :], gates[:, slot, 2, :], cell[:, slot, :], ALU.mult
                                      ).then_inc(hid_done, 1)

                def step(b, slot):
                    if before(b, B - 1):
                        split_x(b + 1, 1 - slot)
                    recur(b, slot)
                split_x(0, 0)
                steps(dve, B, 2, step)


HEADS = 8
DH = P // HEADS
GROUPS = 2
GH = HEADS // GROUPS
UNITS = B * GROUPS
VCOLS = DH + 1
LANE = 32


def attention_inputs(nc, g, w, q_parts, k_parts, v_rows):
    SCALE = float(P) ** -0.5
    with ExitStack() as ctx:
        def sb(name, shape, dt=F32):
            return ctx.enter_context(nc.sbuf_tensor(name, shape, dt))

        sem = semaphores(nc, ctx)

        w_hi = sb("qkv_hi", [P, 3, P], F32R)
        w_lo = sb("qkv_lo", [P, 3, P], F32R)
        split_weights(nc, g, [(w_hi[:, 0:1, :], w_lo[:, 0:1, :], w["L0_attn_q_w"].rearrange("o (i k) -> o i k", i=1), True),
                              (w_hi[:, 1:3, :], w_lo[:, 1:3, :],
                               w["L0_attn_kv_w"].rearrange("(j o) k -> o j k", j=2), True)], "qkv")
        rows = sb("y_rows", [P, 2, TILES, P])
        y_hi = sb("y_hi", [P, 2, T], F32R)
        y_lo = sb("y_lo", [P, 2, T], F32R)
        out_hi = [sb(f"{s}_hi", [P, 2, T], F32R) for s in "qk"]
        out_lo = [sb(f"{s}_lo", [P, 2, T], F32R) for s in "qk"]
        v_out = sb("v_out", [P, 2, GROUPS, TILES, GH, VCOLS])
        turn = ctx.enter_context(nc.psum_tensor("y_turn", [P, 2, 512], F32))
        proj = [ctx.enter_context(nc.psum_tensor(f"{s}_proj", [P, 2, 512], F32)) for s in "qk"]
        v_proj = ctx.enter_context(nc.psum_tensor("v_proj", [P, 2, 512], F32))
        centred, ready, turned = sem("centred"), sem("y_ready"), sem("y_turned")
        rounded, split = sem("y_rounded"), sem("y_split")
        done, v_done = [sem("q_done"), sem("k_done")], sem("v_done")
        hi_done, lo_done, v_kept = [sem("q_hi_done"), sem("k_hi_done")], [sem("q_lo_done"), sem("k_lo_done")], sem("v_kept")
        stored, ones_set = [sem("qkv_stored0"), sem("qkv_stored1")], sem("ones_set")
        STORES = 10

        with nc.Block() as block:
            @block.gpsimd
            def _(pool):
                pool.memset(v_out[:, :, :, :, :, :], 1.0).then_inc(ones_set, 1)

                def norm(b, slot):
                    if at_least(b, 2):
                        pool.wait_ge(turned, b - 1)
                    normalize(pool, g, rows[:, slot, :, :], b, centred, b + 1).then_inc(ready, 1)
                steps(pool, B, 2, norm)

            @block.tensor
            def _(pe):
                def turn_rows(b, slot):
                    pe.wait_ge(ready, b + 1)
                    if at_least(b, 1):
                        pe.wait_ge(split, b)
                    for c, n in enumerate(ROWS):
                        last = pe.transpose(turn[:, c // 4, (c % 4) * P:(c % 4) * P + n], rows[0:n, slot, c, :],
                                            g.ident[0:n, 0:n])
                    last.then_inc(turned, 1)

                def project(b, slot):
                    pe.wait_ge(split, b + 1)
                    for j in range(2):
                        if at_least(b, 1):
                            pe.wait_ge(lo_done[j], b)
                        for h, cols in enumerate(HALVES):
                            for k, (a, m) in enumerate([(w_hi, y_hi), (w_hi, y_lo), (w_lo, y_hi)]):
                                last = pe.matmul(proj[j][:, h, 0:HALF], a[:, j, :], m[:, slot, cols],
                                                 start=(k == 0), stop=(k == 2))
                        last.then_inc(done[j], 1)
                    if at_least(b, 1):
                        pe.wait_ge(v_kept, b)
                    for c, n in enumerate(ROWS):
                        for k, (a, m) in enumerate([(y_hi, w_hi), (y_hi, w_lo), (y_lo, w_hi)]):
                            last = pe.matmul(v_proj[0:n, c // 4, (c % 4) * P:(c % 4 + 1) * P],
                                             a[:, slot, c * P:c * P + n], m[:, 2, :], start=(k == 0), stop=(k == 2))
                    last.then_inc(v_done, 1)

                def step(b, slot):
                    if before(b, B - 1):
                        turn_rows(b + 1, 1 - slot)
                    project(b, slot)
                turn_rows(0, 0)
                steps(pe, B, 2, step)

            @block.scalar
            def _(act):
                def round_y(b, slot):
                    act.wait_ge(turned, b + 1)
                    if at_least(b, 2):
                        act.wait_ge(v_done, b - 1)
                    act.copy(y_hi[:, slot, 0:512], turn[:, 0, :])
                    act.copy(y_hi[:, slot, 512:T], turn[:, 1, 0:T - 512]).then_inc(rounded, 1)

                def keep(b, slot):
                    if at_least(b, 2):
                        act.wait_ge(stored[slot], (b - slot) * (8 * STORES))
                    for j in range(2):
                        act.wait_ge(done[j], b + 1)
                        act.mul(out_hi[j][:, slot, :].rearrange("p (h n) -> p h n", h=2), proj[j][:, :, 0:HALF],
                                SCALE if j == 0 else 1.0).then_inc(hi_done[j], 1)
                    act.wait_ge(v_done, b + 1)
                    if not at_least(b, 1):
                        act.wait_ge(ones_set, 1)
                    for c, n in enumerate(ROWS):
                        last = act.copy(v_out[0:n, slot, :, c, :, 0:DH],
                                        v_proj[0:n, c // 4, (c % 4) * P:(c % 4 + 1) * P]
                                        .rearrange("p (a k d) -> p a k d", a=GROUPS, k=GH))
                    last.then_inc(v_kept, 1)

                def step(b, slot):
                    if before(b, B - 1):
                        round_y(b + 1, 1 - slot)
                    keep(b, slot)
                round_y(0, 0)
                steps(act, B, 2, step)

            @block.vector
            def _(dve):
                def split_y(b, slot):
                    dve.wait_ge(rounded, b + 1)
                    dve.tensor_tensor(y_lo[:, slot, 0:512], turn[:, 0, :], y_hi[:, slot, 0:512].bitcast(F32),
                                      ALU.subtract)
                    dve.tensor_tensor(y_lo[:, slot, 512:T], turn[:, 1, 0:T - 512],
                                      y_hi[:, slot, 512:T].bitcast(F32), ALU.subtract).then_inc(split, 1)

                def low(b, slot):
                    for j in range(2):
                        dve.wait_ge(hi_done[j], b + 1)
                        dve.scalar_tensor_tensor(
                            out=out_lo[j][:, slot, :].rearrange("p (h n) -> p h n", h=2), in0=proj[j][:, :, 0:HALF],
                            scalar=SCALE if j == 0 else 1.0,
                            in1=out_hi[j][:, slot, :].bitcast(F32).rearrange("p (h n) -> p h n", h=2),
                            op0=ALU.mult, op1=ALU.subtract).then_inc(lo_done[j], 1)

                def step(b, slot):
                    if before(b, B - 1):
                        split_y(b + 1, 1 - slot)
                    low(b, slot)
                split_y(0, 0)
                steps(dve, B, 2, step)

            @block.sync
            def _(sp):
                def save(b, slot):
                    asker = (b + B // 2) % B
                    for j, (dram, batch) in enumerate([(q_parts, b), (k_parts, asker)]):
                        sp.wait_ge(lo_done[j], b + 1)
                        for part, src in enumerate([out_hi[j], out_lo[j]]):
                            for grp in range(GROUPS):
                                sp.dma_start(dram[bass.ds(batch * GROUPS + grp, 1), part, :, :]
                                             .rearrange("o p n -> (o p) n"),
                                             src[grp * 64:grp * 64 + 64, slot, :].bitcast(F32)).then_inc(stored[slot], 16)
                    sp.wait_ge(v_kept, b + 1)
                    for grp in range(GROUPS):
                        sp.dma_start(v_rows[bass.ds(asker * GROUPS + grp, 1), :, :].rearrange("o p n -> (o p) n"),
                                     v_out[:, slot, grp, :, :, :].rearrange("p c k d -> p (c k d)")
                                     ).then_inc(stored[slot], 16)
                steps(sp, B, 2, save)
                for slot in range(2):
                    sp.wait_ge(stored[slot], 16 * STORES * (B // 2))


def cross_attention(nc, g, w):
    row_statistics(nc, g, "n0")
    with ExitStack() as ctx:
        q_parts = nc.dram_tensor("q_parts", (UNITS, 2, GH * DH, T), F32, kind="Internal").ap()
        k_parts = nc.dram_tensor("k_parts", (UNITS, 2, GH * DH, T), F32, kind="Internal").ap()
        v_rows = nc.dram_tensor("v_rows", (UNITS, P, TILES * GH * VCOLS), F32, kind="Internal").ap()
        attention_inputs(nc, g, w, q_parts, k_parts, v_rows)

        def sb(name, shape, dt=F32):
            return ctx.enter_context(nc.sbuf_tensor(name, shape, dt))

        sem = semaphores(nc, ctx)

        SLOTS = 3
        PAD = TILES * P
        PARTS_ROWS = 4 * DH
        MAX_ROW = P - 1
        STEPS = 2 * (TILES // 2)
        MAXES = GH * TILES * 2
        SHARE = MAXES // STEPS
        RING = 3
        q_stack = [sb(f"q_stack{k}", [P, GH, PAD], F32R) for k in range(SLOTS)]
        k_stack = [sb(f"k_stack{k}", [P, GH, PAD], F32R) for k in range(SLOTS)]
        v_sb = [sb(f"v_sb{k}", [P, TILES, GH, VCOLS]) for k in range(SLOTS)]
        probs = sb("probs", [P, 2, GH, 2, HALF])
        part_max = sb("part_max", [P, GH, TILES, 2])
        neg_max = sb("neg_max", [P, GH * TILES])
        max_rows = sb("max_rows", [GH * TILES, P], F32R)
        o_cols = sb("o_cols", [P, T])
        ones = sb("ones", [1, GH, T])
        inv = sb("inv", [P, TILES, GH])
        o_rows = sb("o_rows", [P, TILES, GH, DH])
        score = [ctx.enter_context(nc.psum_tensor(f"score{k}", [P, 2, 512], F32)) for k in range(2)]
        ring = [ctx.enter_context(nc.psum_tensor(f"to_dve{k}", [P, 512], F32)) for k in range(RING)]
        o_sum = ctx.enter_context(nc.psum_tensor("o_sum", [P, 512], F32))
        qk_loaded = [sem(f"qk_loaded{k}") for k in range(SLOTS)]
        v_loaded = [sem(f"v_loaded{k}") for k in range(SLOTS)]
        row_loaded, padded, ones_made, ones_placed, zeroed = (
            sem("row_loaded"), sem("padded"), sem("ones_made"), sem("ones_placed"), sem("zeroed"))
        filled, used = sem("ring_filled"), sem("ring_used")
        negated, rows_ready = sem("negated"), sem("rows_ready")
        score_done, prob_done, pv_done = sem("score_done"), sem("prob_done"), sem("pv_done")
        o_copied, inverted, scaled, added = sem("o_copied"), sem("inverted"), sem("scaled"), sem("added")
        QK_LOADS = 8
        PARTS = [(0, 4), (4, 2)]

        def plan(u):
            def probes(ahead, k):
                if not before(u, UNITS - ahead):
                    return []
                return [("probe", ahead, i) for i in range(k * SHARE, (k + 1) * SHARE)]
            out = []
            for s in range(STEPS):
                items = probes(1, s + 1) if s < STEPS - 1 else probes(2, 0)
                if s in (2, 3) and at_least(u, 1):
                    items.append(("out", -1, s - 2))
                if s == STEPS - 1 and before(u, UNITS - 1):
                    items.insert(min(len(items), SHARE // 2), ("max", 1, 0))
                out.append(items)
            return out
        opening = [("probe", 0, i) for i in range(MAXES)] + [("max", 0, 0)] + [("probe", 1, i) for i in range(SHARE)]
        closing = [("out", 0, part) for part in range(2)]
        PER_UNIT = MAXES + 3
        firsts = [len(opening)]
        for u in range(UNITS):
            firsts.append(firsts[-1] + sum(len(items) for items in plan(u)))
        assert PER_UNIT % RING == 0 and all(firsts[u] == firsts[1] + (u - 1) * PER_UNIT for u in range(1, UNITS - 1))

        def number(u, s, k):
            at = sum(len(items) for items in plan(u)[:s]) + k
            if isinstance(u, int):
                return firsts[u] + at, (firsts[u] + at) % RING
            at += firsts[1] - PER_UNIT
            return u * PER_UNIT + at, at % RING

        with nc.Block() as block:
            @block.gpsimd
            def _(pool):
                pool.memset(ones[:, :, :], 1.0).then_inc(ones_made, 1)
                pool.wait_ge(ones_made, 1)
                for k in range(SLOTS):
                    pool.memset(k_stack[k][0:PARTS_ROWS, :, T:PAD].bitcast(F32), 0.0).then_inc(padded, 1)
                    pool.wait_ge(padded, 3 * k + 1)
                    pool.memset(k_stack[k][PARTS_ROWS:P, :, :].bitcast(F32), 0.0).then_inc(padded, 1)
                    pool.wait_ge(padded, 3 * k + 2)
                    pool.memset(q_stack[k][PARTS_ROWS:P, :, :].bitcast(F32), 0.0).then_inc(padded, 1)
                    pool.wait_ge(padded, 3 * k + 3)

                def add(u, part):
                    pool.wait_ge(scaled, u * 3 + (1, 3)[part])
                    first, count = PARTS[part]
                    for c0, n, rows in [(0, 4, P)] if part == 0 else [(4, 1, P), (5, 1, LAST)]:
                        h = g.h[0:rows, bass.ds((u // GROUPS) * TILES + c0, n), :].rearrange(
                            "p c (d k) -> p c k d", k=HEADS)[:, :, bass.ds((u % GROUPS) * GH, GH), :]
                        last = pool.tensor_tensor(h, h, o_rows[0:rows, c0:c0 + n, :, :], ALU.add)
                    last.then_inc(added, 1)
                with pool.Fori(0, UNITS) as u:
                    add(u, 0)
                    add(u, 1)

            @block.sync
            def _(sp):
                def load_qk(u, slot):
                    if at_least(u, SLOTS):
                        sp.wait_ge(score_done, u * (STEPS * GH) - (SLOTS - 1) * STEPS * GH)
                    for stack, dram, parts in [(q_stack, q_parts, (0, 1, 0, 1)), (k_stack, k_parts, (0, 1, 1, 0))]:
                        for r, part in enumerate(parts):
                            sp.dma_start(stack[slot][r * DH:(r + 1) * DH, :, 0:T].bitcast(F32),
                                         dram[bass.ds(u, 1), part, :, :].rearrange("o (k d) n -> (o d) k n", k=GH)
                                         ).then_inc(qk_loaded[slot], 16)

                def load_v(u, slot):
                    if at_least(u, SLOTS):
                        sp.wait_ge(pv_done, u * STEPS - (SLOTS - 1) * STEPS)
                    sp.dma_start(v_sb[slot][:, :, :, :].rearrange("p c k d -> p (c k d)"),
                                 v_rows[bass.ds(u, 1), :, :].rearrange("o p n -> (o p) n")).then_inc(v_loaded[slot], 16)

                def place_row(u, slot):
                    sp.wait_ge(rows_ready, u + 1)
                    sp.dma_start(q_stack[slot][MAX_ROW:P, :, :].bitcast(F32).rearrange("o k (c p) -> o (k c) p", p=P),
                                 max_rows[:, :].bitcast(F32)).then_inc(row_loaded, 16)

                def step(u, slot):
                    if before(u, UNITS - 2):
                        load_qk(u + 2, (slot + 2) % SLOTS)
                        load_v(u + 2, (slot + 2) % SLOTS)
                    if before(u, UNITS - 1):
                        place_row(u + 1, (slot + 1) % SLOTS)
                for k in range(SLOTS):
                    sp.wait_ge(padded, 3 * k + 2)
                    sp.dma_start(k_stack[k][MAX_ROW:P, :, 0:T].bitcast(F32), ones[:, :, :]).then_inc(ones_placed, 16)
                sp.wait_ge(padded, 3 * SLOTS)
                for u in range(2):
                    load_qk(u, u)
                    load_v(u, u)
                place_row(0, 0)
                steps3(sp, UNITS, 2, 3, step)

            @block.tensor
            def _(pe):
                def await_qk(u, slot):
                    if isinstance(u, int):
                        pe.wait_ge(qk_loaded[slot], 16 * QK_LOADS * (u // SLOTS + 1))
                    else:
                        pe.wait_ge(qk_loaded[slot], (u // SLOTS) * (16 * QK_LOADS) + 16 * QK_LOADS)

                def hand_over(u, slot, item, at, bank):
                    kind, ahead, i = item
                    unit, its_slot = u + ahead, (slot + ahead) % SLOTS
                    if kind == "probe" and i == 0:
                        await_qk(unit, its_slot)
                    if kind == "max":
                        pe.wait_ge(negated, unit + 1)
                    if kind == "out" and i == 0:
                        pe.wait_ge(o_copied, unit * 2 + 2)
                    if at_least(at, RING):
                        pe.wait_ge(used, at - (RING - 1))
                    if kind == "probe":
                        head, c, half = i // (2 * TILES), (i // 2) % TILES, i % 2
                        last = pe.matmul(ring[bank][0:ROWS[c], 0:HALF],
                                         q_stack[its_slot][0:MAX_ROW, head, c * P:c * P + ROWS[c]],
                                         k_stack[its_slot][0:MAX_ROW, head, HALVES[half]], start=True, stop=True)
                    elif kind == "max":
                        last = pe.transpose(ring[bank][0:GH * TILES, 0:P], neg_max[:, :], g.ident[:, :])
                    else:
                        first, n = PARTS[i]
                        for c in range(first, first + n):
                            last = pe.transpose(ring[bank][0:ROWS[c], (c - first) * P:(c - first + 1) * P],
                                                o_cols[:, c * P:c * P + ROWS[c]], g.ident[:, :])
                    last.then_inc(filled, 1)

                def score_one(u, slot, s, head):
                    e = s * GH + head
                    half, pair = divmod(s, TILES // 2)
                    if at_least(u, 1) or e >= 2:
                        pe.wait_ge(prob_done, u * (STEPS * GH) + (e - 1))
                    for m in range(2):
                        c = 2 * pair + m
                        last = pe.matmul(score[e % 2][:, m, 0:HALF], k_stack[slot][:, head, c * P:(c + 1) * P],
                                         q_stack[slot][:, head, HALVES[half]], start=True, stop=True)
                    last.then_inc(score_done, 1)

                def sum_one(u, slot, s, m):
                    half, pair = divmod(s, TILES // 2)
                    c = 2 * pair + m
                    if s == 0 and m == 0:
                        pe.wait_ge(v_loaded[slot], 16 * (u // SLOTS + 1) if isinstance(u, int) else
                                   (u // SLOTS) * 16 + 16)
                    if m == 0:
                        pe.wait_ge(prob_done, u * (STEPS * GH) + (s + 1) * GH)
                        if pair == 0 and (at_least(u, 1) or half):
                            pe.wait_ge(o_copied, u * 2 + half)
                    for head in range(GH):
                        last = pe.matmul(o_sum[head * LANE:head * LANE + VCOLS, 0:HALF],
                                         v_sb[slot][0:ROWS[c], c, head, :], probs[0:ROWS[c], s % 2, head, m, :],
                                         start=(c == 0), stop=(c == TILES - 1))
                    if m == 1:
                        last.then_inc(pv_done, 1)

                def step(u, slot):
                    pe.wait_ge(row_loaded, u * 16 + 16)
                    items = plan(u)
                    for s in range(STEPS):
                        todo = [(item, *number(u, s, k)) for k, item in enumerate(items[s])]

                        def some(share):
                            for item, at, bank in todo[:share]:
                                hand_over(u, slot, item, at, bank)
                            del todo[:share]

                        def sums(m):
                            if s:
                                sum_one(u, slot, s - 1, m)
                            elif at_least(u, 1):
                                sum_one(u - 1, (slot + 2) % SLOTS, STEPS - 1, m)
                        score_one(u, slot, s, 0)
                        some(2)
                        score_one(u, slot, s, 1)
                        some(1)
                        sums(0)
                        some(2)
                        score_one(u, slot, s, 2)
                        some(1)
                        sums(1)
                        some(1)
                        score_one(u, slot, s, 3)
                        some(len(todo))

                pe.wait_ge(ones_placed, 16 * SLOTS)
                pe.wait_ge(zeroed, 2)
                for k, item in enumerate(opening):
                    hand_over(0, 0, item, k, k % RING)
                steps3(pe, UNITS, 2, 3, step)
                for m in range(2):
                    sum_one(UNITS - 1, (UNITS - 1) % SLOTS, STEPS - 1, m)
                for k, item in enumerate(closing):
                    hand_over(UNITS - 1, 0, item, firsts[UNITS] + k, (firsts[UNITS] + k) % RING)

            @block.vector
            def _(dve):
                def take(u, item, at, bank):
                    kind, ahead, i = item
                    unit = u + ahead
                    dve.wait_ge(filled, at + 1)
                    if kind == "probe":
                        head, c, half = i // (2 * TILES), (i // 2) % TILES, i % 2
                        if i == 0 and at_least(unit, 1):
                            dve.wait_ge(negated, unit)
                        dve.tensor_reduce(part_max[0:ROWS[c], head, c, half:half + 1], ring[bank][0:ROWS[c], 0:HALF],
                                          AX.X, ALU.max).then_inc(used, 1)
                        if i == MAXES - 1:
                            dve.wait_ge(used, at + 1)
                            dve.tensor_reduce(neg_max[:, :], part_max[:, :, :, :].rearrange("p k c h -> p (k c) h"),
                                              AX.X, ALU.max, negate=True).then_inc(negated, 1)
                    elif kind == "max":
                        if at_least(unit, 1):
                            dve.wait_ge(row_loaded, unit * 16)
                        dve.tensor_copy(max_rows[:, :], ring[bank][0:GH * TILES, 0:P]).then_inc(rows_ready, 1)
                        dve.wait_ge(rows_ready, unit + 1)
                        dve.sem_inc(used, 1)
                    else:
                        for j, (c0, n, rows) in enumerate([(0, 4, P)] if i == 0 else [(4, 1, P), (5, 1, LAST)]):
                            first = PARTS[i][0]
                            o = ring[bank][0:rows, (c0 - first) * P:(c0 - first + n) * P].rearrange(
                                "p (c k e) -> p c k e", k=GH, e=LANE)
                            dve.reciprocal(inv[0:rows, c0:c0 + n, :], o[:, :, :, DH]).then_inc(inverted, 1)
                            dve.wait_ge(inverted, unit * 3 + (i + j + 1))
                            if at_least(unit, 1) and j == 0:
                                dve.wait_ge(added, unit * 2 + (i - 1))
                            dve.tensor_tensor(o_rows[0:rows, c0:c0 + n, :, :], o[:, :, :, 0:DH],
                                              inv[0:rows, c0:c0 + n, :].unsqueeze(3).broadcast_to([rows, n, GH, DH]),
                                              ALU.mult).then_inc(scaled, 1)
                        dve.wait_ge(scaled, unit * 3 + (1, 3)[i])
                        dve.sem_inc(used, 1)

                def step(u, slot):
                    for s, items in enumerate(plan(u)):
                        for k, item in enumerate(items):
                            take(u, item, *number(u, s, k))

                dve.memset(part_max[:, :, :, :], 0.0).then_inc(zeroed, 1)
                dve.memset(o_sum[:, :], 0.0).then_inc(zeroed, 1)
                dve.wait_ge(zeroed, 2)
                for k, item in enumerate(opening):
                    take(0, item, k, k % RING)
                steps3(dve, UNITS, 2, 3, step)
                for k, item in enumerate(closing):
                    take(UNITS - 1, item, firsts[UNITS] + k, (firsts[UNITS] + k) % RING)

            @block.scalar
            def _(act):
                def copy_o(u, half):
                    act.wait_ge(pv_done, u * STEPS + (half + 1) * (STEPS // 2))
                    if half == 0 and at_least(u, 1):
                        act.wait_ge(filled, number(u, 3, len(plan(u)[3]) - 1)[0] + 1)
                    act.copy(o_cols[:, HALVES[half]], o_sum[:, 0:HALF]).then_inc(o_copied, 1)

                def step(u, slot):
                    for s in range(STEPS):
                        for head in range(GH):
                            e = s * GH + head
                            act.wait_ge(score_done, u * (STEPS * GH) + (e + 1))
                            if at_least(u, 1) or s >= 2:
                                act.wait_ge(pv_done, u * STEPS + (s - 1))
                            act.activation(probs[:, s % 2, head, :, :], score[e % 2][:, :, 0:HALF], ACT.Exp
                                           ).then_inc(prob_done, 1)
                            if head == 0 and s == 1 and at_least(u, 1):
                                copy_o(u - 1, 1)
                            if head == 0 and s == 4:
                                copy_o(u, 0)
                steps3(act, UNITS, 2, 3, step)
                copy_o(UNITS - 1, 1)


E_N = 8


def router_logits(nc, g, wg_hi, wg_lo, bias, logits, tag):
    with ExitStack() as ctx:
        def sb(name, shape, dt=F32):
            return ctx.enter_context(nc.sbuf_tensor(f"{name}_{tag}", shape, dt))

        sem = semaphores(nc, ctx, "_" + tag)

        rows = sb("r_rows", [P, 2, TILES, P])
        y_hi = sb("r_hi", [P, 2, T], F32R)
        y_lo = sb("r_lo", [P, 2, T], F32R)
        turn = [ctx.enter_context(nc.psum_tensor(f"r_turn{k}_{tag}", [P, 2, 512], F32)) for k in range(2)]
        out = [ctx.enter_context(nc.psum_tensor(f"r_out{k}_{tag}", [P, TILES, E_N], F32)) for k in range(2)]
        centred, ready, turned, rounded, split, done, kept, cleared = (
            sem(s) for s in ("r_centred", "r_ready", "r_turned", "r_rounded", "r_split", "r_done", "r_kept",
                             "r_cleared"))
        with nc.Block() as block:
            @block.gpsimd
            def _(pool):
                def norm(b, slot):
                    if at_least(b, 2):
                        pool.wait_ge(turned, b - 1)
                    normalize(pool, g, rows[:, slot, :, :], b, centred, b + 1).then_inc(ready, 1)
                steps(pool, B, 2, norm)

            @block.tensor
            def _(pe):
                def turn_rows(b, slot):
                    pe.wait_ge(ready, b + 1)
                    if at_least(b, 2):
                        pe.wait_ge(split, b - 1)
                    turn_tiles(pe, g, turn[slot], rows[:, slot, :, :]).then_inc(turned, 1)

                def project(b, slot):
                    pe.wait_ge(split, b + 1)
                    if at_least(b, 2):
                        pe.wait_ge(kept, b - 1)
                    for c, n in enumerate(ROWS):
                        for k, (a, m) in enumerate([(y_hi, wg_hi), (y_hi, wg_lo), (y_lo, wg_hi)]):
                            last = pe.matmul(out[slot][0:n, c, :], a[:, slot, c * P:c * P + n], m[:, 0, :],
                                             start=(k == 0), stop=(k == 2))
                    last.then_inc(done, 1)

                def step(b, slot):
                    if before(b, B - 1):
                        turn_rows(b + 1, 1 - slot)
                    project(b, slot)
                turn_rows(0, 0)
                steps(pe, B, 2, step)

            @block.scalar
            def _(act):
                def round_y(b, slot):
                    act.wait_ge(turned, b + 1)
                    if at_least(b, 2):
                        act.wait_ge(done, b - 1)
                    round_cols(act, y_hi[:, slot, :], turn[slot]).then_inc(rounded, 1)
                steps(act, B, 2, round_y)

            @block.vector
            def _(dve):
                dve.memset(logits[:, :, :, :], 0.0).then_inc(cleared, 1)
                dve.wait_ge(cleared, 1)

                def split_y(b, slot):
                    dve.wait_ge(rounded, b + 1)
                    split_cols(dve, y_lo[:, slot, :], y_hi[:, slot, :], turn[slot]).then_inc(split, 1)

                def keep(b, slot):
                    dve.wait_ge(done, b + 1)
                    for c0, c1, n in [(0, TILES - 1, P), (TILES - 1, TILES, LAST)]:
                        dst = logits[0:n, c0:c1, bass.ds(b, 1), :].rearrange("p c o e -> p c (o e)")
                        if bias is None:
                            last = dve.tensor_copy(dst, out[slot][0:n, c0:c1, :])
                        else:
                            last = dve.tensor_tensor(dst, out[slot][0:n, c0:c1, :],
                                                     bias[0:n, :].unsqueeze(1).broadcast_to([n, c1 - c0, E_N]), ALU.add)
                    last.then_inc(kept, 1)

                def step(b, slot):
                    if before(b, B - 1):
                        split_y(b + 1, 1 - slot)
                    keep(b, slot)
                split_y(0, 0)
                steps(dve, B, 2, step)


def route(nc, g, logits, gate, gate_cols, k_tokens, k_experts, tag):
    N = B * TILES
    with ExitStack() as ctx:
        def sb(name, shape, dt=F32):
            return ctx.enter_context(nc.sbuf_tensor(f"{name}_{tag}", shape, dt))

        peak = sb("peak", [P, N])
        probs = logits
        total = sb("total", [P, N])
        turn = ctx.enter_context(nc.psum_tensor(f"g_turn_{tag}", [P, 2, 512], F32))
        back = ctx.enter_context(nc.psum_tensor(f"g_back_{tag}", [P, 2, 512], F32))
        work = sb("work", [P, T])
        cols = sb("cols", [P, T])
        best = sb("best", [P, 8])
        wins = sb("wins", [P, N, E_N])
        beats = sb("beats", [P, N, E_N])
        sem = semaphores(nc, ctx, "_" + tag)
        chain, exped, turned, copied, back_done = (
            sem(s) for s in ("g_chain", "g_exped", "g_turned", "g_copied", "g_back_done"))
        flat = logits[:, :, :, :].rearrange("p c b e -> p (c b) e")

        def spread(a):
            return a[:, :].unsqueeze(2).broadcast_to([P, N, E_N])

        chosen = gate if k_experts else probs
        with nc.Block() as block:
            @block.vector
            def _(dve):
                count = [0]

                def then(ins):
                    count[0] += 1
                    ins.then_inc(chain, 1)
                    dve.wait_ge(chain, count[0])

                then(dve.tensor_reduce(peak[:, :], flat, AX.X, ALU.max))
                then(dve.tensor_tensor(flat, flat, spread(peak), ALU.subtract))
                dve.wait_ge(exped, 1)
                then(dve.tensor_reduce(total[:, :], flat, AX.X, ALU.add))
                then(dve.reciprocal(total[:, :], total[:, :]))
                then(dve.tensor_tensor(flat, flat, spread(total), ALU.mult))
                if k_experts:
                    then(dve.memset(wins[:, :, :], 0.0))
                    then(dve.memset(beats[:, :, :], 0.0))
                    for e in range(E_N):
                        one = flat[:, :, e:e + 1]
                        if e:
                            then(dve.tensor_tensor(beats[:, :, 0:e], one.broadcast_to([P, N, e]), flat[:, :, 0:e],
                                                   ALU.is_gt))
                        if e < E_N - 1:
                            then(dve.tensor_tensor(beats[:, :, e + 1:E_N], one.broadcast_to([P, N, E_N - 1 - e]),
                                                   flat[:, :, e + 1:E_N], ALU.is_ge))
                        if e:
                            then(dve.tensor_tensor(wins[:, :, 0:e], wins[:, :, 0:e], beats[:, :, 0:e], ALU.add))
                        if e < E_N - 1:
                            then(dve.tensor_tensor(wins[:, :, e + 1:E_N], wins[:, :, e + 1:E_N],
                                                   beats[:, :, e + 1:E_N], ALU.add))
                    then(dve.scalar_tensor_tensor(out=gate[:, :, :].rearrange("p c (b e) -> p (c b) e", e=E_N),
                                                  in0=wins[:, :, :], scalar=k_experts - 0.5, in1=flat,
                                                  op0=ALU.is_lt, op1=ALU.mult))
                dve.sem_inc(copied, 1)
                dve.wait_ge(turned, 1)
                if k_experts:
                    dve.tensor_copy(gate_cols[:, 0:512], turn[:, 0, :])
                    dve.tensor_copy(gate_cols[:, 512:T], turn[:, 1, 0:T - 512]).then_inc(chain, 1)
                    return
                for dst in (work, cols):
                    then(dve.tensor_copy(dst[:, 0:512], turn[:, 0, :]))
                    then(dve.tensor_copy(dst[:, 512:T], turn[:, 1, 0:T - 512]))
                rounds = -(-k_tokens // 8)
                for r in range(rounds):
                    then(dve.max(best[:, :], work[:, :]))
                    left = k_tokens - 8 * r
                    if left < 8:
                        then(dve.memset(best[:, left:8], -1.0))
                    then(dve.match_replace(work[:, :], best[:, :], work[:, :], -1.0))
                then(dve.scalar_tensor_tensor(out=gate_cols[:, :], in0=work[:, :], scalar=0.0, in1=cols[:, :],
                                              op0=ALU.is_lt, op1=ALU.mult))
                dve.sem_inc(copied, 1)
                dve.wait_ge(back_done, 1)
                for c, n in enumerate(ROWS):
                    dve.tensor_copy(gate[0:n, c, :], back[0:n, c // 4, (c % 4) * P:(c % 4 + 1) * P])

            @block.scalar
            def _(act):
                act.wait_ge(chain, 2)
                act.activation(flat, flat, ACT.Exp).then_inc(exped, 1)

            @block.tensor
            def _(pe):
                pe.wait_ge(copied, 1)
                src = gate[:, :, :] if k_experts else probs[:, :, :, :].rearrange("p c b e -> p c (b e)")
                turn_tiles(pe, g, turn, src).then_inc(turned, 1)
                if not k_experts:
                    pe.wait_ge(copied, 2)
                    for c, n in enumerate(ROWS):
                        last = pe.transpose(back[0:n, c // 4, (c % 4) * P:(c % 4 + 1) * P],
                                            gate_cols[:, c * P:c * P + n], g.ident[:, :])
                    last.then_inc(back_done, 1)


def gated_ffn(nc, g, w1_hi, w1_lo, b1, w2, blocks, shared, gate, gate_cols, b2_rows, plain_bias, tag):
    experts = w2.shape[1] // blocks
    with ExitStack() as ctx:
        def sb(name, shape, dt=F32):
            return ctx.enter_context(nc.sbuf_tensor(f"{name}_{tag}", shape, dt))

        sem = semaphores(nc, ctx, "_" + tag)

        rows = sb("f_rows", [P, 2, TILES, P])
        y_hi = sb("f_hi", [P, 2, T], F32R)
        y_lo = sb("f_lo", [P, 2, T], F32R)
        hid = sb("f_hid", [P, 2, blocks, T])
        turn = ctx.enter_context(nc.psum_tensor(f"f_turn_{tag}", [P, 2, 512], F32))
        up = [ctx.enter_context(nc.psum_tensor(f"f_up{k}_{tag}", [P, 2, 512], F32)) for k in range(2)]
        down = ctx.enter_context(nc.psum_tensor(f"f_down_{tag}", [P, 2, 512], F32))
        centred, ready, turned, rounded, split, up_done, act_done, down_done, down_used, added = (
            sem(s) for s in ("f_centred", "f_ready", "f_turned", "f_rounded", "f_split", "up_done", "act_done",
                             "down_done", "down_used", "f_added"))
        UP = experts * blocks
        DOWN = experts + 1
        with nc.Block() as block:
            @block.gpsimd
            def _(pool):
                def norm(b, slot):
                    if at_least(b, 2):
                        pool.wait_ge(turned, b - 1)
                    normalize(pool, g, rows[:, slot, :, :], b, centred, b + 1).then_inc(ready, 1)
                steps(pool, B, 2, norm)

            @block.tensor
            def _(pe):
                def turn_rows(b, slot):
                    pe.wait_ge(ready, b + 1)
                    if at_least(b, 1):
                        pe.wait_ge(split, b)
                    turn_tiles(pe, g, turn, rows[:, slot, :, :]).then_inc(turned, 1)

                def widen(b, slot, x):
                    for j in range(blocks):
                        k = x * blocks + j
                        if at_least(b, 1) or k >= 2:
                            pe.wait_ge(act_done, b * UP + (k - 1))
                        for h, cols in enumerate(HALVES):
                            for i, (a, m) in enumerate([(w1_hi, y_hi), (w1_hi, y_lo), (w1_lo, y_hi)]):
                                last = pe.matmul(up[k % 2][:, h, 0:HALF], a[:, k, :], m[:, slot, cols],
                                                 start=(i == 0), stop=(i == 2))
                        last.then_inc(up_done, 1)

                def tile_out(c):
                    return down[0:ROWS[c], c // 4, (c % 4) * P:(c % 4 + 1) * P]

                def narrow(b, x):
                    pe.wait_ge(act_done, b * UP + (x + 1) * blocks)
                    if at_least(b, 1) or x:
                        pe.wait_ge(down_used, b * DOWN + x)
                    for c, n in enumerate(ROWS):
                        for j in range(blocks):
                            last = pe.matmul(tile_out(c), hid[:, x % 2, j, c * P:c * P + n],
                                             w2[:, x * blocks + j, :], start=(j == 0), stop=(j == blocks - 1))
                    last.then_inc(down_done, 1)

                def biases(b):
                    pe.wait_ge(down_used, b * DOWN + experts)
                    for c, n in enumerate(ROWS):
                        last = pe.matmul(tile_out(c), gate_cols[:, c * P:c * P + n],
                                         b2_rows[:, bass.ds(b, 1), :].rearrange("p o d -> p (o d)"),
                                         start=True, stop=True)
                    last.then_inc(down_done, 1)

                def step(b, slot):
                    pe.wait_ge(split, b + 1)
                    for x in range(experts):
                        widen(b, slot, x)
                        if x:
                            narrow(b, x - 1)
                        elif at_least(b, 1):
                            narrow(b - 1, experts - 1)
                            biases(b - 1)
                        if x == 1 and before(b, B - 1):
                            turn_rows(b + 1, 1 - slot)
                turn_rows(0, 0)
                steps(pe, B, 2, step)
                narrow(B - 1, experts - 1)
                biases(B - 1)

            @block.scalar
            def _(act):
                def round_y(b, slot):
                    act.wait_ge(turned, b + 1)
                    if at_least(b, 2):
                        act.wait_ge(up_done, b * UP - UP)
                    round_cols(act, y_hi[:, slot, :], turn).then_inc(rounded, 1)

                def step(b, slot):
                    for k in range(UP):
                        x, j = divmod(k, blocks)
                        act.wait_ge(up_done, b * UP + (k + 1))
                        if j == 0 and (at_least(b, 1) or x >= 2):
                            act.wait_ge(down_done, b * DOWN + (x - 1 if x >= 2 else x - 2))
                        act.activation(hid[:, x % 2, j, :].rearrange("p (h n) -> p h n", h=2), up[k % 2][:, :, 0:HALF],
                                       ACT.Gelu, bias=b1[:, 0, k:k + 1]).then_inc(act_done, 1)
                        if k == 2 * blocks + 1 and before(b, B - 1):
                            round_y(b + 1, 1 - slot)
                round_y(0, 0)
                steps(act, B, 2, step)

            @block.vector
            def _(dve):
                def split_y(b, slot):
                    dve.wait_ge(rounded, b + 1)
                    split_cols(dve, y_lo[:, slot, :], y_hi[:, slot, :], turn).then_inc(split, 1)

                def add(b, x):
                    n_done = b * DOWN + x
                    dve.wait_ge(down_done, n_done + 1)
                    dve.wait_ge(added, n_done * TILES) if at_least(b, 1) or x else None
                    for c, n in enumerate(ROWS):
                        out = down[0:n, c // 4, (c % 4) * P:(c % 4 + 1) * P]
                        h = g.h[0:n, bass.ds(b * TILES + c, 1), :].rearrange("p o d -> p (o d)")
                        if x < shared or x == experts:
                            ins = dve.tensor_tensor(h, out, h, ALU.add)
                        else:
                            ins = dve.scalar_tensor_tensor(
                                out=h, in0=out, scalar=gate[0:n, c, bass.ds(b * E_N + (x - shared), 1)], in1=h,
                                op0=ALU.mult, op1=ALU.add)
                        ins.then_inc(added, 1)
                    dve.wait_ge(added, n_done * TILES + TILES)
                    dve.sem_inc(down_used, 1)

                def step(b, slot):
                    for x in range(experts):
                        if x:
                            add(b, x - 1)
                        elif at_least(b, 1):
                            add(b - 1, experts - 1)
                            add(b - 1, experts)
                            if plain_bias is not None:
                                plain(b - 1)
                        if x == 2 and before(b, B - 1):
                            split_y(b + 1, 1 - slot)

                def plain(b):
                    h = g.h[:, bass.ds(b * TILES, TILES), :]
                    dve.tensor_tensor(h, h, plain_bias[:, :].unsqueeze(1).broadcast_to([P, TILES, P]), ALU.add)
                split_y(0, 0)
                steps(dve, B, 2, step)
                add(B - 1, experts - 1)
                add(B - 1, experts)
                if plain_bias is not None:
                    plain(B - 1)


def load_small(nc, loads, tag):
    clears = [c for _, _, c in loads if c is not None]
    with ExitStack() as ctx:
        sem = semaphores(nc, ctx, "_" + tag)
        done, cleared = sem("small_loaded"), sem("small_cleared")
        with nc.Block() as block:
            @block.vector
            def _(dve):
                for c in clears:
                    dve.memset(c, 0.0).then_inc(cleared, 1)

            @block.sync
            def _(sp):
                if clears:
                    sp.wait_ge(cleared, len(clears))
                for dst, src, _ in loads:
                    sp.dma_start(dst, src).then_inc(done, 16)
                sp.wait_ge(done, 16 * len(loads))


def expert_choice(nc, g, w):
    HID = 256
    BLOCKS = HID // P
    K_TOKENS = min(max(T * 2 // E_N, 1), T)
    row_statistics(nc, g, "n1")
    with ExitStack() as ctx:
        def sb(name, shape, dt=F32):
            return ctx.enter_context(nc.sbuf_tensor(name, shape, dt))

        gate = sb("c_gate", [P, TILES, P])
        gate_cols = sb("c_gate_cols", [P, T])
        w1_hi = sb("c_w1_hi", [P, E_N * BLOCKS, P], F32R)
        w1_lo = sb("c_w1_lo", [P, E_N * BLOCKS, P], F32R)
        w2 = sb("c_w2", [P, E_N * BLOCKS, P])
        b1 = sb("c_b1", [P, 1, E_N * BLOCKS])
        b2_rows = sb("c_b2", [P, B, P])
        with ExitStack() as inner:
            wg_hi = inner.enter_context(nc.sbuf_tensor("c_wg_hi", [P, 1, E_N], F32R))
            wg_lo = inner.enter_context(nc.sbuf_tensor("c_wg_lo", [P, 1, E_N], F32R))
            logits = inner.enter_context(nc.sbuf_tensor("c_logits", [P, TILES, B, E_N], F32))
            split_weights(nc, g, [
                (wg_hi[:, :, :], wg_lo[:, :, :], w["L0_ffn_Wg"].rearrange("h (o e) -> h o e", o=1), False),
                *[(w1_hi[:, e * BLOCKS:(e + 1) * BLOCKS, :], w1_lo[:, e * BLOCKS:(e + 1) * BLOCKS, :],
                   w["L0_ffn_W1"][e].rearrange("h (j f) -> h j f", f=P), False) for e in range(E_N)],
                (b1[:, :, :], None, w["L0_ffn_b1"].rearrange("e (j o f) -> (e j) o f", o=1, f=P), True),
            ], "c")
            load_small(nc, [(w2[:, :, :], w["L0_ffn_W2"].rearrange("e (j f) h -> f (e j) h", f=P), None)] +
                       [(b2_rows[b * E_N:(b + 1) * E_N, b, :], w["L0_ffn_b2"], b2_rows[:, :, :] if b == 0 else None)
                        for b in range(B)], "c")
            router_logits(nc, g, wg_hi, wg_lo, None, logits, "c")
            route(nc, g, logits, gate, gate_cols, K_TOKENS, None, "c")
        gated_ffn(nc, g, w1_hi, w1_lo, b1, w2, BLOCKS, 0, gate, gate_cols, b2_rows, None, "c")


S_HEADS = 8
S_DIM = 64
SLICES = 32
HS = S_HEADS * SLICES


def slice_weights(nc, g, w, wqk_hi, wqk_lo, fold, bias_q, bias_k, bias_out):
    with ExitStack() as ctx:
        def sb(name, shape, dt=F32):
            return ctx.enter_context(nc.sbuf_tensor(name, shape, dt))

        def psum(name, shape):
            return ctx.enter_context(nc.psum_tensor(name, shape, F32))

        sem = semaphores(nc, ctx)

        win_t = sb("win_t", [S_DIM, S_HEADS, P])
        wv_t = sb("wv_t", [S_DIM, 1, S_DIM])
        b_col = sb("b_col", [S_DIM, 1, S_HEADS])
        wqk = sb("wqk_raw", [S_DIM, 2, SLICES])
        w_out = sb("w_out_raw", [S_DIM, S_HEADS, P])
        b_out = sb("b_out_rows", [P, P])
        b_wide = sb("b_wide", [S_DIM, S_HEADS, P])
        wvo = sb("wvo", [S_DIM, S_HEADS, P])
        split_weights(nc, g, [
            (win_t[:, :, :], None, w["L1_attn_W_in"].rearrange("d (h k) -> d h k", k=S_DIM), True),
            (wv_t[:, :, :], None, w["L1_attn_Wv"].rearrange("k (o c) -> k o c", o=1), True),
            (b_col[:, :, :], None, w["L1_attn_b_in"].rearrange("(h o k) -> h o k", o=1, k=S_DIM), True)], "d")
        load_small(nc, [
            (wqk[:, 0, :], w["L1_attn_Wq"], None), (wqk[:, 1, :], w["L1_attn_Wk"], None),
            (w_out[:, :, :], w["L1_attn_W_out"].rearrange("(h k) o -> k h o", k=S_DIM), None),
            (b_out[:, :], w["L1_attn_b_out"].unsqueeze(0).broadcast_to([P, P]), None)], "d")
        p_vo = psum("p_vo", [S_DIM, 2, 4, P])
        p_qk = psum("p_qk", [P, S_HEADS, 2, SLICES])
        p_fold = psum("p_fold", [P, 2, 4, P])
        p_bq = psum("p_bq", [P, S_HEADS, SLICES])
        p_bo = psum("p_bo", [P, 2, P])
        p_bk = psum("p_bk", [P, 2])
        widened, vo_done, vo_kept, rest_done, rounded = (
            sem(s) for s in ("b_widened", "vo_done", "vo_kept", "rest_done", "wqk_rounded"))
        with nc.Block() as block:
            @block.tensor
            def _(pe):
                for h in range(S_HEADS):
                    last = pe.matmul(p_vo[:, h // 4, h % 4, :], wv_t[:, 0, :], w_out[:, h, :], start=True, stop=True)
                last.then_inc(vo_done, 1)
                pe.wait_ge(widened, 1)
                pe.wait_ge(vo_kept, 1)
                for h in range(S_HEADS):
                    at = slice((h % 4) * SLICES, (h % 4 + 1) * SLICES)
                    pe.matmul(p_qk[:, h, :, :], win_t[:, h, :], wqk[:, :, :], start=True, stop=True)
                    pe.matmul(p_fold[:, h // 4, h % 4, :], win_t[:, h, :], wvo[:, h, :], start=True, stop=True)
                    pe.matmul(p_bq[:, h, :], b_wide[:, h, :], wqk[:, 0, :], start=True, stop=True)
                    pe.matmul(p_bo[at, h // 4, :], b_wide[:, h, 0:SLICES], wvo[:, h, :], start=True, stop=True)
                    last = pe.matmul(p_bk[at, h // 4:h // 4 + 1], wqk[:, 1, :], b_col[:, 0, h:h + 1],
                                     start=True, stop=True)
                last.then_inc(rest_done, 1)

            @block.vector
            def _(dve):
                dve.tensor_copy(b_wide[:, :, :], b_col[:, 0, :].unsqueeze(2).broadcast_to([S_DIM, S_HEADS, P])
                                ).then_inc(widened, 1)
                dve.wait_ge(vo_done, 1)
                dve.tensor_copy(wvo[:, :, :], p_vo[:, :, :, :].rearrange("p a b o -> p (a b) o")).then_inc(vo_kept, 1)
                dve.wait_ge(rest_done, 1)
                for j in range(2):
                    dve.scalar_tensor_tensor(out=bias_out[:, j, :], in0=b_out[:, :], scalar=1.0 / S_HEADS,
                                             in1=p_bo[:, j, :], op0=ALU.mult, op1=ALU.add)
                dve.tensor_copy(bias_k[:, :], p_bk[:, :])
                dve.tensor_copy(fold[:, :, :], p_fold[:, :, :, :].rearrange("p a b o -> p (a b) o"))
                dve.wait_ge(rounded, 3)
                for j in range(2):
                    dve.tensor_tensor(wqk_lo[:, j, :].rearrange("p (h s) -> p h s", s=SLICES), p_qk[:, :, j, :],
                                      wqk_hi[:, j, :].bitcast(F32).rearrange("p (h s) -> p h s", s=SLICES), ALU.subtract)
                dve.tensor_tensor(bias_q[:, 1, :].rearrange("p (h s) -> p h s", s=SLICES), p_bq[:, :, :],
                                  bias_q[:, 0, :].bitcast(F32).rearrange("p (h s) -> p h s", s=SLICES), ALU.subtract)

            @block.scalar
            def _(act):
                act.wait_ge(rest_done, 1)
                for j in range(2):
                    act.copy(wqk_hi[:, j, :].rearrange("p (h s) -> p h s", s=SLICES), p_qk[:, :, j, :]
                             ).then_inc(rounded, 1)
                act.copy(bias_q[:, 0, :].rearrange("p (h s) -> p h s", s=SLICES), p_bq[:, :, :]).then_inc(rounded, 1)


def slice_attention(nc, g, w):
    row_statistics(nc, g, "n2")
    with ExitStack() as ctx:
        def sb(name, shape, dt=F32):
            return ctx.enter_context(nc.sbuf_tensor(name, shape, dt))

        sem = semaphores(nc, ctx)

        wqk_hi, wqk_lo = sb("wqk_hi", [P, 2, HS], F32R), sb("wqk_lo", [P, 2, HS], F32R)
        fold = sb("fold", [P, S_HEADS, P])
        bias_q = sb("bias_q", [P, 2, HS], F32R)
        bias_k = sb("bias_k", [P, 2])
        bias_out = sb("bias_out", [P, 2, P])
        slice_weights(nc, g, w, wqk_hi, wqk_lo, fold, bias_q, bias_k, bias_out)

        first_row = sb("first_row", [P, P], F32R)
        rows = sb("d_rows", [P, 2, TILES, P])
        y_hi, y_lo = sb("d_hi", [P, 2, T], F32R), sb("d_lo", [P, 2, T], F32R)
        k_neg, k_shift = sb("k_neg", [P, 2]), sb("k_shift", [P, 2])
        k_sum, k_inv = sb("k_sum", [P, 2, 2]), sb("k_inv", [P, 2])
        k_exp = sb("k_exp", [P, 2, T])
        k_tok = sb("k_tok", [P, TILES, HS])
        ky = sb("ky", [P, HS])
        mix = sb("mix", [P, 2, P])
        q_sb = sb("q_sb", [P, 2, TILES * S_HEADS, SLICES])
        q_peak, q_sum = sb("q_peak", [P, TILES * S_HEADS]), sb("q_sum", [P, 2, TILES * S_HEADS])
        q_cols = sb("q_cols", [P, 2, T])
        PA, PB, PC = [ctx.enter_context(nc.psum_tensor(f"d_pair{k}", [P, 2, 512], F32)) for k in range(3)]
        p_ky = ctx.enter_context(nc.psum_tensor("p_ky", [P, HS], F32))
        p_mix = ctx.enter_context(nc.psum_tensor("p_mix", [P, 2, P], F32))
        used = [sem(f"d_used{k}") for k in range(3)]
        (row_set, centred, ready, turned, rounded, k_done, k_negated, k_shifted, k_turned, ky_done, ky_kept, mix_done,
         k_inverted, mix_ready, q_done, q_peaked, q_exped, q_summed, q_inverted, q_ready, q_turned, out_done) = (
            sem("d_" + s) for s in (
                "row_set", "centred", "ready", "turned", "rounded", "k_done", "k_negated", "k_shifted", "k_turned",
                "ky_done", "ky_kept", "mix_done", "k_inverted", "mix_ready", "q_done", "q_peaked", "q_exped",
                "q_summed", "q_inverted", "q_ready", "q_turned", "out_done"))
        A, B_, C = range(3)
        PLACE = {"y": (A, 0), "k0": (A, 1), "q1": (A, 2), "out": (A, 3),
                 "kt0": (B_, 0), "k1": (B_, 1), "qt0": (B_, 2),
                 "kt1": (C, 0), "q0": (C, 1), "qt1": (C, 2)}
        AHEAD = {"y": 0, "k0": 1, "q1": 2, "k1": 0, "q0": 0}
        LEFT = {"kt0": 0, "qt0": 1, "kt1": 0, "qt1": 1, "out": 0}
        ROUND = {A: 4, B_: 3, C: 3}
        START = {A: 3, B_: 1, C: 1}

        def place(job, b):
            pair, at = PLACE[job]
            if job in AHEAD:
                if isinstance(b, int) and b == 0:
                    return pair, AHEAD[job]
                return pair, b * ROUND[pair] + (START[pair] - ROUND[pair] + at)
            if isinstance(b, int) and b == B - 1:
                at = LEFT[job]
            return pair, b * ROUND[pair] + (START[pair] + at)

        def free(eng, job, b):
            pair, before_it = place(job, b)
            if not (isinstance(before_it, int) and before_it == 0):
                eng.wait_ge(used[pair], before_it)

        def over(eng, job, b):
            pair, before_it = place(job, b)
            eng.wait_ge(used[pair], before_it + 1)

        Q_PARTS = [(0, 4), (4, 2)]


        with nc.Block() as block:
            @block.gpsimd
            def _(pool):
                pool.memset(first_row[:, :].bitcast(F32), 0.0).then_inc(row_set, 1)
                pool.wait_ge(row_set, 1)
                pool.memset(first_row[0:1, :].bitcast(F32), 1.0).then_inc(row_set, 1)

                def norm(b, slot):
                    if at_least(b, 2):
                        pool.wait_ge(ky_done, b - 1)
                    normalize(pool, g, rows[:, slot, :, :], b, centred, b + 1).then_inc(ready, 1)

                def scale_q(b, slot):
                    for part, (c, n) in enumerate(Q_PARTS):
                        pool.wait_ge(q_inverted, b * 2 + (part + 1))
                        at = slice(c * S_HEADS, (c + n) * S_HEADS)
                        q = q_sb[:, slot, at, :]
                        pool.tensor_tensor(q, q, q_sum[:, slot, at].unsqueeze(2).broadcast_to(
                            [P, n * S_HEADS, SLICES]), ALU.mult).then_inc(q_ready, 1)

                def rounds(b, slot):
                    if before(b, B - 1):
                        scale_q(b + 1, 1 - slot)
                    if before(b, B - 2):
                        norm(b + 2, slot)
                norm(0, 0)
                norm(1, 1)
                scale_q(0, 0)
                steps(pool, B, 2, rounds)

            @block.tensor
            def _(pe):
                def turn_y(b, slot):
                    pe.wait_ge(ready, b + 1)
                    free(pe, "y", b)
                    turn_tiles(pe, g, PA, rows[:, slot, :, :]).then_inc(turned, 1)

                def k_proj(b, slot, j):
                    if j == 0:
                        over(pe, "y", b)
                    free(pe, f"k{j}", b)
                    for h, cols in enumerate(HALVES):
                        for i, (a, m) in enumerate([(wqk_hi, y_hi), (wqk_hi, y_lo), (wqk_lo, y_hi)]):
                            last = pe.matmul((PA, PB)[j][:, h, 0:HALF], a[:, 1, j * P:(j + 1) * P], m[:, slot, cols],
                                             start=(i == 0), stop=(i == 2))
                    last.then_inc(k_done, 1)

                def q_proj(b, slot, part):
                    free(pe, f"q{part}", b)
                    c0, n_tiles = Q_PARTS[part]
                    for c in range(c0, c0 + n_tiles):
                        n, at = ROWS[c], c - c0
                        out = (PC, PA)[part][0:n, at // 2, (at % 2) * HS:(at % 2 + 1) * HS]
                        for i, (a, m) in enumerate([(y_hi, wqk_hi), (y_hi, wqk_lo), (y_lo, wqk_hi)]):
                            pe.matmul(out, a[:, slot, c * P:c * P + n], m[:, 0, :], start=(i == 0), stop=False)
                        pe.matmul(out, first_row[:, 0:n], bias_q[:, 0, :], start=False, stop=False)
                        last = pe.matmul(out, first_row[:, 0:n], bias_q[:, 1, :], start=False, stop=True)
                    last.then_inc(q_done, 1)

                def k_turn(b, part):
                    if part == 0:
                        over(pe, "k0", b)
                        over(pe, "k1", b)
                    free(pe, f"kt{part}", b)
                    c0, n_tiles = Q_PARTS[part]
                    for c in range(c0, c0 + n_tiles):
                        at = c - c0
                        for j in range(2):
                            last = pe.transpose((PB, PC)[part][0:ROWS[c], at // 2, (at % 2) * HS + j * P:
                                                               (at % 2) * HS + (j + 1) * P],
                                                k_exp[:, j, c * P:c * P + ROWS[c]], g.ident[:, :])
                    last.then_inc(k_turned, 1)

                def ky_sum(b, slot):
                    over(pe, "kt0", b)
                    over(pe, "kt1", b)
                    if at_least(b, 1):
                        pe.wait_ge(ky_kept, b)
                    for c, n in enumerate(ROWS):
                        last = pe.matmul(p_ky[:, :], rows[0:n, slot, c, :], k_tok[0:n, c, :],
                                         start=(c == 0), stop=(c == TILES - 1))
                    last.then_inc(ky_done, 1)

                def mixing(b):
                    pe.wait_ge(ky_kept, b + 1)
                    if at_least(b, 1):
                        pe.wait_ge(mix_ready, b)
                    for h in range(S_HEADS):
                        last = pe.matmul(p_mix[(h % 4) * SLICES:(h % 4 + 1) * SLICES, h // 4, :],
                                         ky[:, h * SLICES:(h + 1) * SLICES], fold[:, h, :], start=True, stop=True)
                    last.then_inc(mix_done, 1)

                def q_turn(b, slot, j):
                    if j == 0:
                        pe.wait_ge(q_ready, b * 2 + 2)
                    free(pe, f"qt{j}", b)
                    for c, n in enumerate(ROWS):
                        src = q_sb[0:n, slot, c * S_HEADS + j * 4:c * S_HEADS + (j + 1) * 4, :]
                        last = pe.transpose((PB, PC)[j][:, c // 4, (c % 4) * P:(c % 4) * P + n],
                                            src.rearrange("p h s -> p (h s)"), g.ident[0:n, 0:n])
                    last.then_inc(q_turned, 1)

                def output(b):
                    over(pe, "qt0", b)
                    over(pe, "qt1", b)
                    pe.wait_ge(mix_ready, b + 1)
                    free(pe, "out", b)
                    for c, n in enumerate(ROWS):
                        for j in range(2):
                            last = pe.matmul(PA[0:n, c // 4, (c % 4) * P:(c % 4 + 1) * P],
                                             q_cols[:, j, c * P:c * P + n], mix[:, j, :], start=(j == 0), stop=(j == 1))
                    last.then_inc(out_done, 1)

                def rounds(b, slot):
                    nxt, more = 1 - slot, before(b, B - 1)
                    if more:
                        turn_y(b + 1, nxt)
                    k_turn(b, 0)
                    k_turn(b, 1)
                    if more:
                        k_proj(b + 1, nxt, 0)
                        k_proj(b + 1, nxt, 1)
                    ky_sum(b, slot)
                    if more:
                        q_proj(b + 1, nxt, 0)
                    mixing(b)
                    if more:
                        q_proj(b + 1, nxt, 1)
                    q_turn(b, slot, 0)
                    q_turn(b, slot, 1)
                    output(b)
                pe.wait_ge(row_set, 2)
                turn_y(0, 0)
                k_proj(0, 0, 0)
                k_proj(0, 0, 1)
                q_proj(0, 0, 0)
                q_proj(0, 0, 1)
                steps(pe, B, 2, rounds)

            @block.vector
            def _(dve):
                def split_y(b, slot):
                    dve.wait_ge(rounded, b + 1)
                    split_cols(dve, y_lo[:, slot, :], y_hi[:, slot, :], PA).then_inc(used[A], 1)

                def k_peak(b, j):
                    dve.wait_ge(k_done, b * 2 + (j + 1))
                    dve.tensor_reduce(k_neg[:, j:j + 1], (PA, PB)[j][:, :, 0:HALF], AX.XY, ALU.max, negate=True
                                      ).then_inc(k_negated, 1)
                    dve.wait_ge(k_negated, b * 2 + (j + 1))
                    if at_least(b, 1):
                        dve.wait_ge(used[(A, B_)[j]], place(f"k{j}", b)[1])
                    dve.scalar_tensor_tensor(out=k_shift[:, j:j + 1], in0=k_neg[:, j:j + 1], scalar=bias_k[:, j:j + 1],
                                             in1=bias_k[:, j:j + 1], op0=ALU.subtract, op1=ALU.add
                                             ).then_inc(k_shifted, 1)

                def q_centre(b, slot, part):
                    dve.wait_ge(q_done, b * 2 + (part + 1))
                    c, n = Q_PARTS[part]
                    at = slice(c * S_HEADS, (c + n) * S_HEADS)
                    src = (PC[:, :, :] if part == 0 else PA[:, 0:1, :]).rearrange("p a (h s) -> p (a h) s", s=SLICES)
                    dve.tensor_reduce(q_peak[:, at], src, AX.X, ALU.max).then_inc(q_peaked, 1)
                    dve.wait_ge(q_peaked, b * 2 + (part + 1))
                    if at_least(b, 2):
                        dve.wait_ge(q_turned, b * 2 - 2)
                    dve.tensor_tensor(q_sb[:, slot, at, :], src, q_peak[:, at].unsqueeze(2).broadcast_to(
                        [P, n * S_HEADS, SLICES]), ALU.subtract).then_inc(used[(C, A)[part]], 1)

                def q_total(b, slot, part):
                    c, n = Q_PARTS[part]
                    at = slice(c * S_HEADS, (c + n) * S_HEADS)
                    dve.wait_ge(q_exped, b * 2 + (part + 1))
                    dve.tensor_reduce(q_sum[:, slot, at], q_sb[:, slot, at, :], AX.X, ALU.add).then_inc(q_summed, 1)
                    dve.wait_ge(q_summed, b * 2 + (part + 1))
                    dve.reciprocal(q_sum[:, slot, at], q_sum[:, slot, at]).then_inc(q_inverted, 1)

                def mix_out(b, slot):
                    over(dve, "k0", b)
                    over(dve, "k1", b)
                    dve.reciprocal(k_inv[:, :], k_sum[:, slot, :]).then_inc(k_inverted, 1)
                    dve.wait_ge(k_inverted, b + 1)
                    dve.wait_ge(mix_done, b + 1)
                    if at_least(b, 1):
                        dve.wait_ge(out_done, b)
                    for j in range(2):
                        last = dve.scalar_tensor_tensor(out=mix[:, j, :], in0=p_mix[:, j, :], scalar=k_inv[:, j:j + 1],
                                                        in1=bias_out[:, j, :], op0=ALU.mult, op1=ALU.add)
                    last.then_inc(mix_ready, 1)

                def add(b):
                    dve.wait_ge(out_done, b + 1)
                    for c0, c1, n in [(0, 4, P), (4, 5, P), (5, 6, LAST)]:
                        h = g.h[0:n, bass.ds(b * TILES + c0, c1 - c0), :]
                        src = PA[0:n, c0 // 4, (c0 % 4) * P:((c1 - 1) % 4 + 1) * P].rearrange("p (c d) -> p c d", d=P)
                        last = dve.tensor_tensor(h, src, h, ALU.add)
                    last.then_inc(used[A], 1)

                def rounds(b, slot):
                    nxt, more = 1 - slot, before(b, B - 1)
                    if more:
                        split_y(b + 1, nxt)
                        k_peak(b + 1, 0)
                        k_peak(b + 1, 1)
                        q_centre(b + 1, nxt, 0)
                    mix_out(b, slot)
                    if more:
                        q_centre(b + 1, nxt, 1)
                        q_total(b + 1, nxt, 0)
                        q_total(b + 1, nxt, 1)
                    add(b)
                split_y(0, 0)
                for j in range(2):
                    k_peak(0, j)
                for part in range(2):
                    q_centre(0, 0, part)
                for part in range(2):
                    q_total(0, 0, part)
                steps(dve, B, 2, rounds)

            @block.scalar
            def _(act):
                def round_y(b, slot):
                    act.wait_ge(turned, b + 1)
                    if at_least(b, 2):
                        act.wait_ge(q_done, b * 2 - 2)
                    round_cols(act, y_hi[:, slot, :], PA).then_inc(rounded, 1)

                def k_keep(b, part):
                    act.wait_ge(k_turned, b * 2 + (part + 1))
                    if at_least(b, 1):
                        act.wait_ge(ky_done, b)
                    c, n = Q_PARTS[part]
                    src = PB[:, :, :] if part == 0 else PC[:, 0:1, :]
                    act.copy(k_tok[:, c:c + n, :].rearrange("p (a c) s -> p a (c s)", c=2), src
                             ).then_inc(used[(B_, C)[part]], 1)

                def k_exps(b, slot, j):
                    act.wait_ge(k_shifted, b * 2 + (j + 1))
                    if at_least(b, 1):
                        act.wait_ge(k_turned, b * 2)
                    act.activation(k_exp[:, j, :].rearrange("p (h n) -> p h n", h=2), (PA, PB)[j][:, :, 0:HALF],
                                   ACT.Exp, bias=k_shift[:, j:j + 1], accum_out=k_sum[:, slot, j:j + 1]
                                   ).then_inc(used[(A, B_)[j]], 1)

                def ky_keep(b):
                    act.wait_ge(ky_done, b + 1)
                    if at_least(b, 1):
                        act.wait_ge(mix_done, b)
                    act.copy(ky[:, :], p_ky[:, :]).then_inc(ky_kept, 1)

                def q_exps(b, slot, part):
                    over(act, f"q{part}", b)
                    c, n = Q_PARTS[part]
                    q = q_sb[:, slot, c * S_HEADS:(c + n) * S_HEADS, :]
                    act.activation(q, q, ACT.Exp).then_inc(q_exped, 1)

                def q_keep(b, j):
                    act.wait_ge(q_turned, b * 2 + (j + 1))
                    if at_least(b, 1):
                        act.wait_ge(out_done, b)
                    act.copy(q_cols[:, j, 0:512], (PB, PC)[j][:, 0, :])
                    act.copy(q_cols[:, j, 512:T], (PB, PC)[j][:, 1, 0:T - 512]).then_inc(used[(B_, C)[j]], 1)

                def rounds(b, slot):
                    nxt, more = 1 - slot, before(b, B - 1)
                    if more:
                        round_y(b + 1, nxt)
                    k_keep(b, 0)
                    k_keep(b, 1)
                    if more:
                        k_exps(b + 1, nxt, 0)
                        k_exps(b + 1, nxt, 1)
                    ky_keep(b)
                    if more:
                        q_exps(b + 1, nxt, 0)
                        q_exps(b + 1, nxt, 1)
                    q_keep(b, 0)
                    q_keep(b, 1)
                round_y(0, 0)
                for j in range(2):
                    k_exps(0, 0, j)
                for part in range(2):
                    q_exps(0, 0, part)
                steps(act, B, 2, rounds)


def mixture(nc, g, w):
    HID = 512
    BLOCKS = HID // P
    SHARED = 2
    TOP = 2
    ALL = SHARED + E_N
    row_statistics(nc, g, "n3")
    with ExitStack() as ctx:
        def sb(name, shape, dt=F32):
            return ctx.enter_context(nc.sbuf_tensor(name, shape, dt))

        gate = sb("e_gate", [P, TILES, P])
        gate_cols = sb("e_gate_cols", [P, T])
        w1_hi = sb("e_w1_hi", [P, ALL * BLOCKS, P], F32R)
        w1_lo = sb("e_w1_lo", [P, ALL * BLOCKS, P], F32R)
        w2 = sb("e_w2", [P, ALL * BLOCKS, P])
        b1 = sb("e_b1", [P, 1, ALL * BLOCKS])
        b2_rows = sb("e_b2", [P, B, P])
        shared_bias = sb("e_sb2", [P, SHARED, P])
        gate_bias = sb("e_gate_b", [P, E_N])
        with ExitStack() as inner:
            wg_hi = inner.enter_context(nc.sbuf_tensor("e_wg_hi", [P, 1, E_N], F32R))
            wg_lo = inner.enter_context(nc.sbuf_tensor("e_wg_lo", [P, 1, E_N], F32R))
            logits = inner.enter_context(nc.sbuf_tensor("e_logits", [P, TILES, B, E_N], F32))

            def ups(name, first, n):
                return [(w1_hi[:, (first + e) * BLOCKS:(first + e + 1) * BLOCKS, :],
                         w1_lo[:, (first + e) * BLOCKS:(first + e + 1) * BLOCKS, :],
                         w[name][e].rearrange("(j f) d -> f j d", f=P), True) for e in range(n)]

            def downs(name, first, n):
                return [(w2[:, (first + e) * BLOCKS:(first + e + 1) * BLOCKS, :], None,
                         w[name][e].rearrange("d (j f) -> d j f", f=P), True) for e in range(n)]

            def bias_columns(name, first, n):
                return (b1[:, :, first * BLOCKS:(first + n) * BLOCKS], None,
                        w[name].rearrange("e (j o f) -> (e j) o f", o=1, f=P), True)

            split_weights(nc, g, [
                (wg_hi[:, :, :], wg_lo[:, :, :], w["L1_ffn_gate_w"].rearrange("e (o d) -> e o d", o=1), True),
                *ups("L1_ffn_sw1", 0, SHARED), *ups("L1_ffn_rw1", SHARED, E_N),
                *downs("L1_ffn_sw2", 0, SHARED), *downs("L1_ffn_rw2", SHARED, E_N),
                bias_columns("L1_ffn_sb1", 0, SHARED), bias_columns("L1_ffn_rb1", SHARED, E_N)], "e")
            load_small(nc, [(b2_rows[b * E_N:(b + 1) * E_N, b, :], w["L1_ffn_rb2"], b2_rows[:, :, :] if b == 0 else None)
                            for b in range(B)] + [
                (shared_bias[:, :, :], w["L1_ffn_sb2"].unsqueeze(0).broadcast_to([P, SHARED, P]), None),
                (gate_bias[:, :], w["L1_ffn_gate_b"].unsqueeze(0).broadcast_to([P, E_N]), None)], "e")
            with nc.Block() as block:
                @block.vector
                def _(dve):
                    dve.tensor_tensor(shared_bias[:, 0, :], shared_bias[:, 0, :], shared_bias[:, 1, :], ALU.add)
            router_logits(nc, g, wg_hi, wg_lo, gate_bias, logits, "e")
            route(nc, g, logits, gate, gate_cols, None, TOP, "e")
        gated_ffn(nc, g, w1_hi, w1_lo, b1, w2, BLOCKS, SHARED, gate, gate_cols, b2_rows, shared_bias[:, 0, :], "e")


def store(nc, g, out):
    with nc.semaphore("stored") as stored, nc.Block() as block:
        @block.sync
        def _(sp):
            with sp.Fori(0, B) as b:
                sp.dma_start(out[bass.ds(b, 1), 0:(TILES - 1) * P, :].rearrange("o (c p) d -> (o p) c d", p=P),
                             g.h[:, bass.ds(b * TILES, TILES - 1), :]).then_inc(stored, 16)
                sp.dma_start(out[bass.ds(b, 1), (TILES - 1) * P:T, :].rearrange("o p d -> (o p) d"),
                             g.h[0:LAST, bass.ds(b * TILES + (TILES - 1), 1), :].rearrange("p o d -> p (o d)")
                             ).then_inc(stored, 16)
            sp.wait_ge(stored, 32 * B)


def audio_tower(nc, w, out):
    with ExitStack() as ctx:
        g = Shared()
        g.h = ctx.enter_context(nc.sbuf_tensor("h", [P, B * TILES, P], F32))
        g.mean = ctx.enter_context(nc.sbuf_tensor("mean", [P, B * TILES], F32))
        g.rstd = ctx.enter_context(nc.sbuf_tensor("rstd", [P, B * TILES], F32))
        constants(nc, ctx, g)
        quasi_recurrent(nc, g, w["x"], w["L0_tok_kernel"])
        cross_attention(nc, g, w)
        expert_choice(nc, g, w)
        slice_attention(nc, g, w)
        mixture(nc, g, w)
        store(nc, g, out)


_INS = ['x', 'L0_tok_kernel', 'L0_attn_q_w', 'L0_attn_kv_w', 'L0_ffn_Wg', 'L0_ffn_W1', 'L0_ffn_b1', 'L0_ffn_W2',
        'L0_ffn_b2', 'L1_attn_W_in', 'L1_attn_b_in', 'L1_attn_Wq', 'L1_attn_Wk', 'L1_attn_Wv', 'L1_attn_W_out',
        'L1_attn_b_out', 'L1_ffn_gate_w', 'L1_ffn_gate_b', 'L1_ffn_sw1', 'L1_ffn_sb1', 'L1_ffn_sw2', 'L1_ffn_sb2',
        'L1_ffn_rw1', 'L1_ffn_rb1', 'L1_ffn_rw2', 'L1_ffn_rb2']


def kernel(**inputs):
    import numpy as _np
    import concourse.bacc as _bacc
    from concourse import mybir as _mybir
    from concourse.bass_utils import run_bass_kernel_spmd as _run

    nc = _bacc.Bacc("TRN2", target_bir_lowering=False, num_devices=1)
    arrays, aps = {}, {}
    for name in _INS:
        a = _np.ascontiguousarray(inputs[name])
        arrays[f"in_{name}_dram"] = a
        aps[name] = nc.dram_tensor(f"in_{name}_dram", a.shape, _mybir.dt.from_np(a.dtype), kind="ExternalInput").ap()
    out = nc.dram_tensor("out_0_dram", (B, T, P), _mybir.dt.float32, kind="ExternalOutput").ap()
    audio_tower(nc, aps, out)
    r = _run(nc, [arrays], core_ids=[0])
    return r.results[0]["out_0_dram"]
```

```python
from contextlib import ExitStack

import concourse.bass as bass
from concourse import mybir

F32 = mybir.dt.float32
F32R = mybir.dt.float32r
U32 = mybir.dt.uint32
ALU = mybir.AluOpType
ACT = mybir.ActivationFunctionType
AX = mybir.AxisListType

P = 128
B = 16
T_IN = 750
WINDOW = 3
T = T_IN - WINDOW + 1
HALF = T // 2
TILES = -(-T // P)
ROWS = [min(P, T - P * c) for c in range(TILES)]
LAST = ROWS[-1]
HALVES = [slice(0, HALF), slice(HALF, T)]
EPS = 1e-5


def steps(eng, n, peel, body):
    assert (n - 2 * peel) % 2 == 0
    for k in range(peel):
        body(k, k % 2)
    with eng.Fori(0, (n - 2 * peel) // 2) as i:
        for q in range(2):
            body(i * 2 + (peel + q), (peel + q) % 2)
    for k in range(n - peel, n):
        body(k, k % 2)


def at_least(k, low):
    return not isinstance(k, int) or k >= low


def before(k, high):
    return not isinstance(k, int) or k < high


def semaphores(nc, ctx, tag=""):
    made = []

    def clear():
        with nc.Block() as block:
            @block.sync
            def _(sp):
                for s in made:
                    sp.sem_clear(s)
        for s in made:
            nc.release_semaphore(s)

    def sem(name):
        made.append(nc.alloc_semaphore(f"{name}{tag}"))
        return made[-1]

    ctx.callback(clear)
    return sem


class Shared:
    pass

def steps3(eng, n, low, high, body):
    assert (n - low - high) % 3 == 0
    for k in range(low):
        body(k, k % 3)
    with eng.Fori(0, (n - low - high) // 3) as i:
        for q in range(3):
            body(i * 3 + (low + q), (low + q) % 3)
    for k in range(n - high, n):
        body(k, k % 3)


def row_statistics(nc, g, tag):
    N = B * TILES
    STEP = 8
    with ExitStack() as ctx:
        def sb(name, shape):
            return ctx.enter_context(nc.sbuf_tensor(f"{name}_{tag}", shape, F32))
        stats = sb("stats", [P, N, 6])
        diff, spread, std = sb("diff", [P, N]), sb("spread", [P, N]), sb("std", [P, N])
        sem = semaphores(nc, ctx, "_" + tag)
        stats_done, sums_done, std_done = sem("stats_done"), sem("sums_done"), sem("std_done")
        eps = sb("eps", [P, 1])
        half = P // 2
        with nc.Block() as block:
            @block.vector
            def _(dve):
                dve.memset(eps[:, :], EPS)
                with dve.Fori(0, N // STEP) as i:
                    for q in range(STEP):
                        dve.bn_stats(stats[:, bass.ds(i * STEP + q, 1), :].rearrange("p o s -> p (o s)"),
                                     g.h[:, bass.ds(i * STEP + q, 1), :].rearrange("p o d -> p (o d)")
                                     ).then_inc(stats_done, 1)
                dve.wait_ge(stats_done, N)
                dve.tensor_tensor(diff[:, :], stats[:, :, 1], stats[:, :, 4], ALU.subtract)
                dve.tensor_tensor(g.mean[:, :], stats[:, :, 1], stats[:, :, 4], ALU.add)
                dve.tensor_tensor(spread[:, :], stats[:, :, 2], stats[:, :, 5], ALU.add).then_inc(sums_done, 1)
                dve.wait_ge(sums_done, 1)
                dve.tensor_scalar(g.mean[:, :], g.mean[:, :], 0.5, None, ALU.mult)
                dve.tensor_tensor(diff[:, :], diff[:, :], diff[:, :], ALU.mult).then_inc(sums_done, 1)
                dve.wait_ge(sums_done, 2)
                dve.scalar_tensor_tensor(out=spread[:, :], in0=diff[:, :], scalar=half / 2.0, in1=spread[:, :],
                                         op0=ALU.mult, op1=ALU.add).then_inc(sums_done, 1)
                dve.wait_ge(std_done, 1)
                dve.reciprocal(g.rstd[:, :], std[:, :])

            @block.scalar
            def _(act):
                act.wait_ge(sums_done, 3)
                act.activation(std[:, :], spread[:, :], ACT.Sqrt, bias=eps[:, :], scale=1.0 / P
                               ).then_inc(std_done, 1)


def normalize(pool, g, rows, b, centred, n):
    tiles = bass.ds(b * TILES, TILES)
    mean = g.mean[:, tiles].unsqueeze(2).broadcast_to([P, TILES, P])
    rstd = g.rstd[:, tiles].unsqueeze(2).broadcast_to([P, TILES, P])
    pool.tensor_tensor(rows, g.h[:, tiles, :], mean, ALU.subtract).then_inc(centred, 1)
    pool.wait_ge(centred, n)
    return pool.tensor_tensor(rows, rows, rstd, ALU.mult)


def split_weights(nc, g, jobs, tag):
    CHUNK = 4
    pieces = []
    for hi, lo, view, turned in jobs:
        for k in range(0, view.shape[1], CHUNK):
            n = min(CHUNK, view.shape[1] - k)
            pieces.append((hi[:, k:k + n, :], None if lo is None else lo[:, k:k + n, :], view[:, k:k + n, :], turned))
    turns = [sum(p[3] for p in pieces[:j + 1]) for j in range(len(pieces))]
    with ExitStack() as ctx:
        sem = semaphores(nc, ctx, "_" + tag)

        raw = ctx.enter_context(nc.sbuf_tensor(f"raw_{tag}", [P, 2, CHUNK, P], F32))
        turn = [ctx.enter_context(nc.psum_tensor(f"wturn{j}_{tag}", [P, CHUNK, P], F32)) for j in range(2)]
        loaded = [sem("w_in0"), sem("w_in1")]
        turned_n, hi_n, lo_n = sem("w_turned"), sem("w_hi"), sem("w_lo")

        def block_of(j):
            hi, lo, view, turned = pieces[j]
            rows, n, cols = view.shape
            return turn[j % 2][0:cols, 0:n, 0:rows] if turned else raw[0:rows, j % 2, 0:n, 0:cols]

        with nc.Block() as block:
            @block.sync
            def _(sp):
                for j, (hi, lo, view, turned) in enumerate(pieces):
                    rows, n, cols = view.shape
                    if j >= 2:
                        sp.wait_ge(lo_n, j - 1)
                    sp.dma_start(raw[0:rows, j % 2, 0:n, 0:cols], view).then_inc(loaded[j % 2], 16)

            @block.tensor
            def _(pe):
                for j, (hi, lo, view, turned) in enumerate(pieces):
                    rows, n, cols = view.shape
                    if not turned:
                        continue
                    pe.wait_ge(loaded[j % 2], 16 * (j // 2 + 1))
                    if j >= 2:
                        pe.wait_ge(lo_n, j - 1)
                    for c in range(n):
                        last = pe.transpose(turn[j % 2][0:cols, c, 0:rows], raw[0:rows, j % 2, c, 0:cols],
                                            g.ident[0:rows, 0:rows])
                    last.then_inc(turned_n, 1)

            def wait_for(eng, j):
                if pieces[j][3]:
                    eng.wait_ge(turned_n, turns[j])
                else:
                    eng.wait_ge(loaded[j % 2], 16 * (j // 2 + 1))

            @block.scalar
            def _(act):
                for j, (hi, lo, view, turned) in enumerate(pieces):
                    if lo is not None:
                        wait_for(act, j)
                        act.copy(hi, block_of(j)).then_inc(hi_n, 1)

            @block.vector
            def _(dve):
                rounded = 0
                for j, (hi, lo, view, turned) in enumerate(pieces):
                    if lo is None:
                        wait_for(dve, j)
                        dve.tensor_copy(hi, block_of(j)).then_inc(lo_n, 1)
                    else:
                        rounded += 1
                        dve.wait_ge(hi_n, rounded)
                        dve.tensor_tensor(lo, block_of(j), hi.bitcast(F32), ALU.subtract).then_inc(lo_n, 1)


def turn_tiles(pe, g, turn, rows):
    for c, n in enumerate(ROWS):
        last = pe.transpose(turn[:, c // 4, (c % 4) * P:(c % 4) * P + n], rows[0:n, c, :], g.ident[0:n, 0:n])
    return last


def round_cols(act, hi, turn):
    act.copy(hi[:, 0:512], turn[:, 0, :])
    return act.copy(hi[:, 512:T], turn[:, 1, 0:T - 512])


def split_cols(dve, lo, hi, turn):
    dve.tensor_tensor(lo[:, 0:512], turn[:, 0, :], hi[:, 0:512].bitcast(F32), ALU.subtract)
    return dve.tensor_tensor(lo[:, 512:T], turn[:, 1, 0:T - 512], hi[:, 512:T].bitcast(F32), ALU.subtract)


def constants(nc, ctx, g):
    g.ident = ctx.enter_context(nc.sbuf_tensor("ident", [P, P], F32))
    made = ctx.enter_context(nc.semaphore("ident_zeroed"))
    with nc.Block() as block:
        @block.gpsimd
        def _(pool):
            pool.memset(g.ident[:], 0.0).then_inc(made, 1)
            pool.wait_ge(made, 1)
            pool.affine_select(out=g.ident[:], in_=g.ident[:], compare_op=ALU.not_equal, fill=1.0, base=0,
                               pattern=[[-1, P]], channel_multiplier=1)

        @block.vector
        def _(dve):
            dve.memset(g.h[:, :, :], 0.0)


def quasi_recurrent(nc, g, x, w):
    GATES = 3
    with ExitStack() as ctx:
        def sb(name, shape, dt=F32):
            return ctx.enter_context(nc.sbuf_tensor(name, shape, dt))

        sem = semaphores(nc, ctx)

        x_rows = sb("x_rows", [P, 2, TILES, P])
        x_hi = sb("x_hi", [P, 2, T_IN], F32R)
        x_lo = sb("x_lo", [P, 2, T_IN], F32R)
        w_raw = sb("w_raw", [P, WINDOW, GATES * P])
        w_hi = sb("w_hi", [P, WINDOW, GATES * P], F32R)
        w_lo = sb("w_lo", [P, WINDOW, GATES * P], F32R)
        gates = sb("gates", [P, 2, GATES, T])
        fresh = sb("fresh", [P, 2, T])
        cell = sb("cell", [P, 2, T])
        hid = sb("hid", [P, 2, T])
        turn_in = ctx.enter_context(nc.psum_tensor("turn_in", [P, 2, 512], F32))
        conv = [ctx.enter_context(nc.psum_tensor(f"conv{k}", [P, 2, 512], F32)) for k in range(2)]
        turn_out = ctx.enter_context(nc.psum_tensor("turn_out", [P, 2, 512], F32))
        x_loaded = [sem("x_loaded0"), sem("x_loaded1")]
        w_loaded, w_rounded, w_split = sem("w_loaded"), sem("w_rounded"), sem("w_split")
        x_turned, x_rounded, x_split = sem("x_turned"), sem("x_rounded"), sem("x_split")
        conv_done, gate_done = sem("conv_done"), sem("gate_done")
        fresh_done, cell_done, hid_done = sem("fresh_done"), sem("cell_done"), sem("hid_done")
        h_turned, h_kept = sem("h_turned"), sem("h_kept")
        full_in = T_IN // P
        rows_in = [min(P, T_IN - P * c) for c in range(full_in + 1)]

        with nc.Block() as block:
            @block.sync
            def _(sp):
                sp.dma_start(w_raw[:, :, :], w.rearrange("k d n -> d k n")).then_inc(w_loaded, 16)

                def load(b, slot):
                    if at_least(b, 2):
                        sp.wait_ge(x_turned, b - 1)
                    sp.dma_start(x_rows[:, slot, 0:full_in, :],
                                 x[bass.ds(b, 1), 0:full_in * P, :].rearrange("o (c p) d -> (o p) c d", p=P)
                                 ).then_inc(x_loaded[slot], 16)
                    sp.dma_start(x_rows[0:rows_in[-1], slot, full_in, :],
                                 x[bass.ds(b, 1), full_in * P:T_IN, :].rearrange("o p d -> (o p) d")
                                 ).then_inc(x_loaded[slot], 16)
                steps(sp, B, 2, load)

            @block.tensor
            def _(pe):
                def turn(b, slot):
                    half = b // 2 if isinstance(b, int) else None
                    pe.wait_ge(x_loaded[slot], 32 * (half + 1) if half is not None else (b - slot) * 16 + 32)
                    if at_least(b, 1):
                        pe.wait_ge(x_split, b)
                    for c, n in enumerate(rows_in):
                        last = pe.transpose(turn_in[:, c // 4, (c % 4) * P:(c % 4) * P + n], x_rows[0:n, slot, c, :],
                                            g.ident[0:n, 0:n])
                    last.then_inc(x_turned, 1)

                def convolve(b, slot):
                    pe.wait_ge(x_split, b + 1)
                    for gate in range(GATES):
                        if at_least(b, 1) or gate == 2:
                            pe.wait_ge(gate_done, b * GATES + (0, -1, 1)[gate])
                        out = conv[gate % 2]
                        for h, cols in enumerate(HALVES):
                            for k in range(WINDOW):
                                for j, (a, m) in enumerate([(w_hi, x_hi), (w_hi, x_lo), (w_lo, x_hi)]):
                                    last = pe.matmul(out[:, h, 0:HALF], a[:, k, gate * P:(gate + 1) * P],
                                                     m[:, slot, cols.start + k:cols.stop + k],
                                                     start=(k == 0 and j == 0), stop=(k == WINDOW - 1 and j == 2))
                        last.then_inc(conv_done, 1)

                def turn_back(b, slot):
                    pe.wait_ge(hid_done, b + 1)
                    if at_least(b, 1):
                        pe.wait_ge(h_kept, b)
                    for c, n in enumerate(ROWS):
                        last = pe.transpose(turn_out[0:n, c // 4, (c % 4) * P:(c % 4) * P + P],
                                            hid[:, slot, c * P:c * P + n], g.ident[:, :])
                    last.then_inc(h_turned, 1)

                def step(b, slot):
                    if before(b, B - 1):
                        turn(b + 1, 1 - slot)
                    convolve(b, slot)
                    if at_least(b, 1):
                        turn_back(b - 1, 1 - slot)

                pe.wait_ge(w_split, 1)
                turn(0, 0)
                steps(pe, B, 2, step)
                turn_back(B - 1, (B - 1) % 2)

            @block.scalar
            def _(act):
                act.wait_ge(w_loaded, 16)
                act.copy(w_hi[:, :, :], w_raw[:, :, :]).then_inc(w_rounded, 1)

                def round_x(b, slot):
                    act.wait_ge(x_turned, b + 1)
                    if at_least(b, 2):
                        act.wait_ge(conv_done, b * GATES - GATES)
                    act.copy(x_hi[:, slot, 0:512], turn_in[:, 0, :]).then_inc(x_rounded, 1)
                    act.copy(x_hi[:, slot, 512:T_IN], turn_in[:, 1, 0:T_IN - 512]).then_inc(x_rounded, 1)

                def open_gates(b, slot):
                    for gate, func in enumerate([ACT.Tanh, ACT.Sigmoid, ACT.Sigmoid]):
                        act.wait_ge(conv_done, b * GATES + (gate + 1))
                        if at_least(b, 2) and gate == 0:
                            act.wait_ge(hid_done, b - 1)
                        act.activation(gates[:, slot, gate, :].rearrange("p (h n) -> p h n", h=2),
                                       conv[gate % 2][:, :, 0:HALF], func).then_inc(gate_done, 1)

                def keep(b, slot):
                    act.wait_ge(h_turned, b + 1)
                    act.copy(g.h[:, bass.ds(b * TILES, 4), :], turn_out[:, 0, :].rearrange("p (c d) -> p c d", c=4))
                    act.copy(g.h[:, bass.ds(b * TILES + 4, 1), :], turn_out[:, 1:2, 0:P])
                    act.copy(g.h[0:LAST, bass.ds(b * TILES + 5, 1), :], turn_out[0:LAST, 1:2, P:2 * P]
                             ).then_inc(h_kept, 1)

                def step(b, slot):
                    if before(b, B - 1):
                        round_x(b + 1, 1 - slot)
                    open_gates(b, slot)
                    if at_least(b, 1):
                        keep(b - 1, 1 - slot)
                round_x(0, 0)
                steps(act, B, 2, step)
                keep(B - 1, (B - 1) % 2)

            @block.vector
            def _(dve):
                dve.wait_ge(w_rounded, 1)
                dve.tensor_tensor(w_lo[:, :, :], w_raw[:, :, :], w_hi[:, :, :].bitcast(F32), ALU.subtract
                                  ).then_inc(w_split, 1)

                def split_x(b, slot):
                    dve.wait_ge(x_rounded, b * 2 + 2)
                    if at_least(b, 2):
                        dve.wait_ge(conv_done, b * GATES - GATES)
                    dve.tensor_tensor(x_lo[:, slot, 0:512], turn_in[:, 0, :], x_hi[:, slot, 0:512].bitcast(F32),
                                      ALU.subtract)
                    dve.tensor_tensor(x_lo[:, slot, 512:T_IN], turn_in[:, 1, 0:T_IN - 512],
                                      x_hi[:, slot, 512:T_IN].bitcast(F32), ALU.subtract).then_inc(x_split, 1)

                def recur(b, slot):
                    dve.wait_ge(gate_done, b * GATES + 2)
                    dve.scalar_tensor_tensor(out=fresh[:, slot, :], in0=gates[:, slot, 1, :], scalar=1.0,
                                             in1=gates[:, slot, 0, :], op0=ALU.subtract, op1=ALU.mult
                                             ).then_inc(fresh_done, 1)
                    dve.wait_ge(fresh_done, b + 1)
                    dve.tensor_tensor_scan(cell[:, slot, :], gates[:, slot, 1, :], fresh[:, slot, :], 0.0,
                                           ALU.mult, ALU.subtract).then_inc(cell_done, 1)
                    dve.wait_ge(cell_done, b + 1)
                    dve.wait_ge(gate_done, b * GATES + 3)
                    if at_least(b, 2):
                        dve.wait_ge(h_turned, b - 1)
                    dve.tensor_tensor(hid[:, slot, :], gates[:, slot, 2, :], cell[:, slot, :], ALU.mult
                                      ).then_inc(hid_done, 1)

                def step(b, slot):
                    if before(b, B - 1):
                        split_x(b + 1, 1 - slot)
                    recur(b, slot)
                split_x(0, 0)
                steps(dve, B, 2, step)


HEADS = 8
DH = P // HEADS
GROUPS = 2
GH = HEADS // GROUPS
UNITS = B * GROUPS
VCOLS = DH + 1
LANE = 32


def attention_inputs(nc, g, w, q_parts, k_parts, v_rows):
    SCALE = float(P) ** -0.5
    with ExitStack() as ctx:
        def sb(name, shape, dt=F32):
            return ctx.enter_context(nc.sbuf_tensor(name, shape, dt))

        sem = semaphores(nc, ctx)

        w_hi = sb("qkv_hi", [P, 3, P], F32R)
        w_lo = sb("qkv_lo", [P, 3, P], F32R)
        split_weights(nc, g, [(w_hi[:, 0:1, :], w_lo[:, 0:1, :], w["L0_attn_q_w"].rearrange("o (i k) -> o i k", i=1), True),
                              (w_hi[:, 1:3, :], w_lo[:, 1:3, :],
                               w["L0_attn_kv_w"].rearrange("(j o) k -> o j k", j=2), True)], "qkv")
        rows = sb("y_rows", [P, 2, TILES, P])
        y_hi = sb("y_hi", [P, 2, T], F32R)
        y_lo = sb("y_lo", [P, 2, T], F32R)
        out_hi = [sb(f"{s}_hi", [P, 2, T], F32R) for s in "qk"]
        out_lo = [sb(f"{s}_lo", [P, 2, T], F32R) for s in "qk"]
        v_out = sb("v_out", [P, 2, GROUPS, TILES, GH, VCOLS])
        turn = ctx.enter_context(nc.psum_tensor("y_turn", [P, 2, 512], F32))
        proj = [ctx.enter_context(nc.psum_tensor(f"{s}_proj", [P, 2, 512], F32)) for s in "qk"]
        v_proj = ctx.enter_context(nc.psum_tensor("v_proj", [P, 2, 512], F32))
        centred, ready, turned = sem("centred"), sem("y_ready"), sem("y_turned")
        rounded, split = sem("y_rounded"), sem("y_split")
        done, v_done = [sem("q_done"), sem("k_done")], sem("v_done")
        hi_done, lo_done, v_kept = [sem("q_hi_done"), sem("k_hi_done")], [sem("q_lo_done"), sem("k_lo_done")], sem("v_kept")
        stored, ones_set = [sem("qkv_stored0"), sem("qkv_stored1")], sem("ones_set")
        STORES = 10

        with nc.Block() as block:
            @block.gpsimd
            def _(pool):
                pool.memset(v_out[:, :, :, :, :, :], 1.0).then_inc(ones_set, 1)

                def norm(b, slot):
                    if at_least(b, 2):
                        pool.wait_ge(turned, b - 1)
                    normalize(pool, g, rows[:, slot, :, :], b, centred, b + 1).then_inc(ready, 1)
                steps(pool, B, 2, norm)

            @block.tensor
            def _(pe):
                def turn_rows(b, slot):
                    pe.wait_ge(ready, b + 1)
                    if at_least(b, 1):
                        pe.wait_ge(split, b)
                    for c, n in enumerate(ROWS):
                        last = pe.transpose(turn[:, c // 4, (c % 4) * P:(c % 4) * P + n], rows[0:n, slot, c, :],
                                            g.ident[0:n, 0:n])
                    last.then_inc(turned, 1)

                def project(b, slot):
                    pe.wait_ge(split, b + 1)
                    for j in range(2):
                        if at_least(b, 1):
                            pe.wait_ge(lo_done[j], b)
                        for h, cols in enumerate(HALVES):
                            for k, (a, m) in enumerate([(w_hi, y_hi), (w_hi, y_lo), (w_lo, y_hi)]):
                                last = pe.matmul(proj[j][:, h, 0:HALF], a[:, j, :], m[:, slot, cols],
                                                 start=(k == 0), stop=(k == 2))
                        last.then_inc(done[j], 1)
                    if at_least(b, 1):
                        pe.wait_ge(v_kept, b)
                    for c, n in enumerate(ROWS):
                        for k, (a, m) in enumerate([(y_hi, w_hi), (y_hi, w_lo), (y_lo, w_hi)]):
                            last = pe.matmul(v_proj[0:n, c // 4, (c % 4) * P:(c % 4 + 1) * P],
                                             a[:, slot, c * P:c * P + n], m[:, 2, :], start=(k == 0), stop=(k == 2))
                    last.then_inc(v_done, 1)

                def step(b, slot):
                    if before(b, B - 1):
                        turn_rows(b + 1, 1 - slot)
                    project(b, slot)
                turn_rows(0, 0)
                steps(pe, B, 2, step)

            @block.scalar
            def _(act):
                def round_y(b, slot):
                    act.wait_ge(turned, b + 1)
                    if at_least(b, 2):
                        act.wait_ge(v_done, b - 1)
                    act.copy(y_hi[:, slot, 0:512], turn[:, 0, :])
                    act.copy(y_hi[:, slot, 512:T], turn[:, 1, 0:T - 512]).then_inc(rounded, 1)

                def keep(b, slot):
                    if at_least(b, 2):
                        act.wait_ge(stored[slot], (b - slot) * (8 * STORES))
                    for j in range(2):
                        act.wait_ge(done[j], b + 1)
                        act.mul(out_hi[j][:, slot, :].rearrange("p (h n) -> p h n", h=2), proj[j][:, :, 0:HALF],
                                SCALE if j == 0 else 1.0).then_inc(hi_done[j], 1)
                    act.wait_ge(v_done, b + 1)
                    if not at_least(b, 1):
                        act.wait_ge(ones_set, 1)
                    for c, n in enumerate(ROWS):
                        last = act.copy(v_out[0:n, slot, :, c, :, 0:DH],
                                        v_proj[0:n, c // 4, (c % 4) * P:(c % 4 + 1) * P]
                                        .rearrange("p (a k d) -> p a k d", a=GROUPS, k=GH))
                    last.then_inc(v_kept, 1)

                def step(b, slot):
                    if before(b, B - 1):
                        round_y(b + 1, 1 - slot)
                    keep(b, slot)
                round_y(0, 0)
                steps(act, B, 2, step)

            @block.vector
            def _(dve):
                def split_y(b, slot):
                    dve.wait_ge(rounded, b + 1)
                    dve.tensor_tensor(y_lo[:, slot, 0:512], turn[:, 0, :], y_hi[:, slot, 0:512].bitcast(F32),
                                      ALU.subtract)
                    dve.tensor_tensor(y_lo[:, slot, 512:T], turn[:, 1, 0:T - 512],
                                      y_hi[:, slot, 512:T].bitcast(F32), ALU.subtract).then_inc(split, 1)

                def low(b, slot):
                    for j in range(2):
                        dve.wait_ge(hi_done[j], b + 1)
                        dve.scalar_tensor_tensor(
                            out=out_lo[j][:, slot, :].rearrange("p (h n) -> p h n", h=2), in0=proj[j][:, :, 0:HALF],
                            scalar=SCALE if j == 0 else 1.0,
                            in1=out_hi[j][:, slot, :].bitcast(F32).rearrange("p (h n) -> p h n", h=2),
                            op0=ALU.mult, op1=ALU.subtract).then_inc(lo_done[j], 1)

                def step(b, slot):
                    if before(b, B - 1):
                        split_y(b + 1, 1 - slot)
                    low(b, slot)
                split_y(0, 0)
                steps(dve, B, 2, step)

            @block.sync
            def _(sp):
                def save(b, slot):
                    asker = (b + B // 2) % B
                    for j, (dram, batch) in enumerate([(q_parts, b), (k_parts, asker)]):
                        sp.wait_ge(lo_done[j], b + 1)
                        for part, src in enumerate([out_hi[j], out_lo[j]]):
                            for grp in range(GROUPS):
                                sp.dma_start(dram[bass.ds(batch * GROUPS + grp, 1), part, :, :]
                                             .rearrange("o p n -> (o p) n"),
                                             src[grp * 64:grp * 64 + 64, slot, :].bitcast(F32)).then_inc(stored[slot], 16)
                    sp.wait_ge(v_kept, b + 1)
                    for grp in range(GROUPS):
                        sp.dma_start(v_rows[bass.ds(asker * GROUPS + grp, 1), :, :].rearrange("o p n -> (o p) n"),
                                     v_out[:, slot, grp, :, :, :].rearrange("p c k d -> p (c k d)")
                                     ).then_inc(stored[slot], 16)
                steps(sp, B, 2, save)
                for slot in range(2):
                    sp.wait_ge(stored[slot], 16 * STORES * (B // 2))


def cross_attention(nc, g, w):
    row_statistics(nc, g, "n0")
    with ExitStack() as ctx:
        q_parts = nc.dram_tensor("q_parts", (UNITS, 2, GH * DH, T), F32, kind="Internal").ap()
        k_parts = nc.dram_tensor("k_parts", (UNITS, 2, GH * DH, T), F32, kind="Internal").ap()
        v_rows = nc.dram_tensor("v_rows", (UNITS, P, TILES * GH * VCOLS), F32, kind="Internal").ap()
        attention_inputs(nc, g, w, q_parts, k_parts, v_rows)

        def sb(name, shape, dt=F32):
            return ctx.enter_context(nc.sbuf_tensor(name, shape, dt))

        sem = semaphores(nc, ctx)

        SLOTS = 3
        PAD = TILES * P
        PARTS_ROWS = 4 * DH
        MAX_ROW = P - 1
        STEPS = 2 * (TILES // 2)
        MAXES = GH * TILES * 2
        SHARE = MAXES // STEPS
        RING = 3
        q_stack = [sb(f"q_stack{k}", [P, GH, PAD], F32R) for k in range(SLOTS)]
        k_stack = [sb(f"k_stack{k}", [P, GH, PAD], F32R) for k in range(SLOTS)]
        v_sb = [sb(f"v_sb{k}", [P, TILES, GH, VCOLS]) for k in range(SLOTS)]
        probs = sb("probs", [P, 2, GH, 2, HALF])
        part_max = sb("part_max", [P, GH, TILES, 2])
        neg_max = sb("neg_max", [P, GH * TILES])
        max_rows = sb("max_rows", [GH * TILES, P], F32R)
        o_cols = sb("o_cols", [P, T])
        ones = sb("ones", [1, GH, T])
        inv = sb("inv", [P, TILES, GH])
        o_rows = sb("o_rows", [P, TILES, GH, DH])
        score = [ctx.enter_context(nc.psum_tensor(f"score{k}", [P, 2, 512], F32)) for k in range(2)]
        ring = [ctx.enter_context(nc.psum_tensor(f"to_dve{k}", [P, 512], F32)) for k in range(RING)]
        o_sum = ctx.enter_context(nc.psum_tensor("o_sum", [P, 512], F32))
        qk_loaded = [sem(f"qk_loaded{k}") for k in range(SLOTS)]
        v_loaded = [sem(f"v_loaded{k}") for k in range(SLOTS)]
        row_loaded, padded, ones_made, ones_placed, zeroed = (
            sem("row_loaded"), sem("padded"), sem("ones_made"), sem("ones_placed"), sem("zeroed"))
        filled, used = sem("ring_filled"), sem("ring_used")
        negated, rows_ready = sem("negated"), sem("rows_ready")
        score_done, prob_done, pv_done = sem("score_done"), sem("prob_done"), sem("pv_done")
        o_copied, inverted, scaled, added = sem("o_copied"), sem("inverted"), sem("scaled"), sem("added")
        QK_LOADS = 8
        PARTS = [(0, 4), (4, 2)]

        def plan(u):
            def probes(ahead, k):
                if not before(u, UNITS - ahead):
                    return []
                return [("probe", ahead, i) for i in range(k * SHARE, (k + 1) * SHARE)]
            out = []
            for s in range(STEPS):
                items = probes(1, s + 1) if s < STEPS - 1 else probes(2, 0)
                if s in (2, 3) and at_least(u, 1):
                    items.append(("out", -1, s - 2))
                if s == STEPS - 1 and before(u, UNITS - 1):
                    items.insert(min(len(items), SHARE // 2), ("max", 1, 0))
                out.append(items)
            return out
        opening = [("probe", 0, i) for i in range(MAXES)] + [("max", 0, 0)] + [("probe", 1, i) for i in range(SHARE)]
        closing = [("out", 0, part) for part in range(2)]
        PER_UNIT = MAXES + 3
        firsts = [len(opening)]
        for u in range(UNITS):
            firsts.append(firsts[-1] + sum(len(items) for items in plan(u)))
        assert PER_UNIT % RING == 0 and all(firsts[u] == firsts[1] + (u - 1) * PER_UNIT for u in range(1, UNITS - 1))

        def number(u, s, k):
            at = sum(len(items) for items in plan(u)[:s]) + k
            if isinstance(u, int):
                return firsts[u] + at, (firsts[u] + at) % RING
            at += firsts[1] - PER_UNIT
            return u * PER_UNIT + at, at % RING

        with nc.Block() as block:
            @block.gpsimd
            def _(pool):
                pool.memset(ones[:, :, :], 1.0).then_inc(ones_made, 1)
                pool.wait_ge(ones_made, 1)
                for k in range(SLOTS):
                    pool.memset(k_stack[k][0:PARTS_ROWS, :, T:PAD].bitcast(F32), 0.0).then_inc(padded, 1)
                    pool.wait_ge(padded, 3 * k + 1)
                    pool.memset(k_stack[k][PARTS_ROWS:P, :, :].bitcast(F32), 0.0).then_inc(padded, 1)
                    pool.wait_ge(padded, 3 * k + 2)
                    pool.memset(q_stack[k][PARTS_ROWS:P, :, :].bitcast(F32), 0.0).then_inc(padded, 1)
                    pool.wait_ge(padded, 3 * k + 3)

                def add(u, part):
                    pool.wait_ge(scaled, u * 3 + (1, 3)[part])
                    first, count = PARTS[part]
                    for c0, n, rows in [(0, 4, P)] if part == 0 else [(4, 1, P), (5, 1, LAST)]:
                        h = g.h[0:rows, bass.ds((u // GROUPS) * TILES + c0, n), :].rearrange(
                            "p c (d k) -> p c k d", k=HEADS)[:, :, bass.ds((u % GROUPS) * GH, GH), :]
                        last = pool.tensor_tensor(h, h, o_rows[0:rows, c0:c0 + n, :, :], ALU.add)
                    last.then_inc(added, 1)
                with pool.Fori(0, UNITS) as u:
                    add(u, 0)
                    add(u, 1)

            @block.sync
            def _(sp):
                def load_qk(u, slot):
                    if at_least(u, SLOTS):
                        sp.wait_ge(score_done, u * (STEPS * GH) - (SLOTS - 1) * STEPS * GH)
                    for stack, dram, parts in [(q_stack, q_parts, (0, 1, 0, 1)), (k_stack, k_parts, (0, 1, 1, 0))]:
                        for r, part in enumerate(parts):
                            sp.dma_start(stack[slot][r * DH:(r + 1) * DH, :, 0:T].bitcast(F32),
                                         dram[bass.ds(u, 1), part, :, :].rearrange("o (k d) n -> (o d) k n", k=GH)
                                         ).then_inc(qk_loaded[slot], 16)

                def load_v(u, slot):
                    if at_least(u, SLOTS):
                        sp.wait_ge(pv_done, u * STEPS - (SLOTS - 1) * STEPS)
                    sp.dma_start(v_sb[slot][:, :, :, :].rearrange("p c k d -> p (c k d)"),
                                 v_rows[bass.ds(u, 1), :, :].rearrange("o p n -> (o p) n")).then_inc(v_loaded[slot], 16)

                def place_row(u, slot):
                    sp.wait_ge(rows_ready, u + 1)
                    sp.dma_start(q_stack[slot][MAX_ROW:P, :, :].bitcast(F32).rearrange("o k (c p) -> o (k c) p", p=P),
                                 max_rows[:, :].bitcast(F32)).then_inc(row_loaded, 16)

                def step(u, slot):
                    if before(u, UNITS - 2):
                        load_qk(u + 2, (slot + 2) % SLOTS)
                        load_v(u + 2, (slot + 2) % SLOTS)
                    if before(u, UNITS - 1):
                        place_row(u + 1, (slot + 1) % SLOTS)
                for k in range(SLOTS):
                    sp.wait_ge(padded, 3 * k + 2)
                    sp.dma_start(k_stack[k][MAX_ROW:P, :, 0:T].bitcast(F32), ones[:, :, :]).then_inc(ones_placed, 16)
                sp.wait_ge(padded, 3 * SLOTS)
                for u in range(2):
                    load_qk(u, u)
                    load_v(u, u)
                place_row(0, 0)
                steps3(sp, UNITS, 2, 3, step)

            @block.tensor
            def _(pe):
                def await_qk(u, slot):
                    if isinstance(u, int):
                        pe.wait_ge(qk_loaded[slot], 16 * QK_LOADS * (u // SLOTS + 1))
                    else:
                        pe.wait_ge(qk_loaded[slot], (u // SLOTS) * (16 * QK_LOADS) + 16 * QK_LOADS)

                def hand_over(u, slot, item, at, bank):
                    kind, ahead, i = item
                    unit, its_slot = u + ahead, (slot + ahead) % SLOTS
                    if kind == "probe" and i == 0:
                        await_qk(unit, its_slot)
                    if kind == "max":
                        pe.wait_ge(negated, unit + 1)
                    if kind == "out" and i == 0:
                        pe.wait_ge(o_copied, unit * 2 + 2)
                    if at_least(at, RING):
                        pe.wait_ge(used, at - (RING - 1))
                    if kind == "probe":
                        head, c, half = i // (2 * TILES), (i // 2) % TILES, i % 2
                        last = pe.matmul(ring[bank][0:ROWS[c], 0:HALF],
                                         q_stack[its_slot][0:MAX_ROW, head, c * P:c * P + ROWS[c]],
                                         k_stack[its_slot][0:MAX_ROW, head, HALVES[half]], start=True, stop=True)
                    elif kind == "max":
                        last = pe.transpose(ring[bank][0:GH * TILES, 0:P], neg_max[:, :], g.ident[:, :])
                    else:
                        first, n = PARTS[i]
                        for c in range(first, first + n):
                            last = pe.transpose(ring[bank][0:ROWS[c], (c - first) * P:(c - first + 1) * P],
                                                o_cols[:, c * P:c * P + ROWS[c]], g.ident[:, :])
                    last.then_inc(filled, 1)

                def score_one(u, slot, s, head):
                    e = s * GH + head
                    half, pair = divmod(s, TILES // 2)
                    if at_least(u, 1) or e >= 2:
                        pe.wait_ge(prob_done, u * (STEPS * GH) + (e - 1))
                    for m in range(2):
                        c = 2 * pair + m
                        last = pe.matmul(score[e % 2][:, m, 0:HALF], k_stack[slot][:, head, c * P:(c + 1) * P],
                                         q_stack[slot][:, head, HALVES[half]], start=True, stop=True)
                    last.then_inc(score_done, 1)

                def sum_one(u, slot, s, m):
                    half, pair = divmod(s, TILES // 2)
                    c = 2 * pair + m
                    if s == 0 and m == 0:
                        pe.wait_ge(v_loaded[slot], 16 * (u // SLOTS + 1) if isinstance(u, int) else
                                   (u // SLOTS) * 16 + 16)
                    if m == 0:
                        pe.wait_ge(prob_done, u * (STEPS * GH) + (s + 1) * GH)
                        if pair == 0 and (at_least(u, 1) or half):
                            pe.wait_ge(o_copied, u * 2 + half)
                    for head in range(GH):
                        last = pe.matmul(o_sum[head * LANE:head * LANE + VCOLS, 0:HALF],
                                         v_sb[slot][0:ROWS[c], c, head, :], probs[0:ROWS[c], s % 2, head, m, :],
                                         start=(c == 0), stop=(c == TILES - 1))
                    if m == 1:
                        last.then_inc(pv_done, 1)

                def step(u, slot):
                    pe.wait_ge(row_loaded, u * 16 + 16)
                    items = plan(u)
                    for s in range(STEPS):
                        todo = [(item, *number(u, s, k)) for k, item in enumerate(items[s])]

                        def some(share):
                            for item, at, bank in todo[:share]:
                                hand_over(u, slot, item, at, bank)
                            del todo[:share]

                        def sums(m):
                            if s:
                                sum_one(u, slot, s - 1, m)
                            elif at_least(u, 1):
                                sum_one(u - 1, (slot + 2) % SLOTS, STEPS - 1, m)
                        score_one(u, slot, s, 0)
                        some(2)
                        score_one(u, slot, s, 1)
                        some(1)
                        sums(0)
                        some(2)
                        score_one(u, slot, s, 2)
                        some(1)
                        sums(1)
                        some(1)
                        score_one(u, slot, s, 3)
                        some(len(todo))

                pe.wait_ge(ones_placed, 16 * SLOTS)
                pe.wait_ge(zeroed, 2)
                for k, item in enumerate(opening):
                    hand_over(0, 0, item, k, k % RING)
                steps3(pe, UNITS, 2, 3, step)
                for m in range(2):
                    sum_one(UNITS - 1, (UNITS - 1) % SLOTS, STEPS - 1, m)
                for k, item in enumerate(closing):
                    hand_over(UNITS - 1, 0, item, firsts[UNITS] + k, (firsts[UNITS] + k) % RING)

            @block.vector
            def _(dve):
                def take(u, item, at, bank):
                    kind, ahead, i = item
                    unit = u + ahead
                    dve.wait_ge(filled, at + 1)
                    if kind == "probe":
                        head, c, half = i // (2 * TILES), (i // 2) % TILES, i % 2
                        if i == 0 and at_least(unit, 1):
                            dve.wait_ge(negated, unit)
                        dve.tensor_reduce(part_max[0:ROWS[c], head, c, half:half + 1], ring[bank][0:ROWS[c], 0:HALF],
                                          AX.X, ALU.max).then_inc(used, 1)
                        if i == MAXES - 1:
                            dve.wait_ge(used, at + 1)
                            dve.tensor_reduce(neg_max[:, :], part_max[:, :, :, :].rearrange("p k c h -> p (k c) h"),
                                              AX.X, ALU.max, negate=True).then_inc(negated, 1)
                    elif kind == "max":
                        if at_least(unit, 1):
                            dve.wait_ge(row_loaded, unit * 16)
                        dve.tensor_copy(max_rows[:, :], ring[bank][0:GH * TILES, 0:P]).then_inc(rows_ready, 1)
                        dve.wait_ge(rows_ready, unit + 1)
                        dve.sem_inc(used, 1)
                    else:
                        for j, (c0, n, rows) in enumerate([(0, 4, P)] if i == 0 else [(4, 1, P), (5, 1, LAST)]):
                            first = PARTS[i][0]
                            o = ring[bank][0:rows, (c0 - first) * P:(c0 - first + n) * P].rearrange(
                                "p (c k e) -> p c k e", k=GH, e=LANE)
                            dve.reciprocal(inv[0:rows, c0:c0 + n, :], o[:, :, :, DH]).then_inc(inverted, 1)
                            dve.wait_ge(inverted, unit * 3 + (i + j + 1))
                            if at_least(unit, 1) and j == 0:
                                dve.wait_ge(added, unit * 2 + (i - 1))
                            dve.tensor_tensor(o_rows[0:rows, c0:c0 + n, :, :], o[:, :, :, 0:DH],
                                              inv[0:rows, c0:c0 + n, :].unsqueeze(3).broadcast_to([rows, n, GH, DH]),
                                              ALU.mult).then_inc(scaled, 1)
                        dve.wait_ge(scaled, unit * 3 + (1, 3)[i])
                        dve.sem_inc(used, 1)

                def step(u, slot):
                    for s, items in enumerate(plan(u)):
                        for k, item in enumerate(items):
                            take(u, item, *number(u, s, k))

                dve.memset(part_max[:, :, :, :], 0.0).then_inc(zeroed, 1)
                dve.memset(o_sum[:, :], 0.0).then_inc(zeroed, 1)
                dve.wait_ge(zeroed, 2)
                for k, item in enumerate(opening):
                    take(0, item, k, k % RING)
                steps3(dve, UNITS, 2, 3, step)
                for k, item in enumerate(closing):
                    take(UNITS - 1, item, firsts[UNITS] + k, (firsts[UNITS] + k) % RING)

            @block.scalar
            def _(act):
                def copy_o(u, half):
                    act.wait_ge(pv_done, u * STEPS + (half + 1) * (STEPS // 2))
                    if half == 0 and at_least(u, 1):
                        act.wait_ge(filled, number(u, 3, len(plan(u)[3]) - 1)[0] + 1)
                    act.copy(o_cols[:, HALVES[half]], o_sum[:, 0:HALF]).then_inc(o_copied, 1)

                def step(u, slot):
                    for s in range(STEPS):
                        for head in range(GH):
                            e = s * GH + head
                            act.wait_ge(score_done, u * (STEPS * GH) + (e + 1))
                            if at_least(u, 1) or s >= 2:
                                act.wait_ge(pv_done, u * STEPS + (s - 1))
                            act.activation(probs[:, s % 2, head, :, :], score[e % 2][:, :, 0:HALF], ACT.Exp
                                           ).then_inc(prob_done, 1)
                            if head == 0 and s == 1 and at_least(u, 1):
                                copy_o(u - 1, 1)
                            if head == 0 and s == 4:
                                copy_o(u, 0)
                steps3(act, UNITS, 2, 3, step)
                copy_o(UNITS - 1, 1)


E_N = 8


def router_logits(nc, g, wg_hi, wg_lo, bias, logits, tag):
    with ExitStack() as ctx:
        def sb(name, shape, dt=F32):
            return ctx.enter_context(nc.sbuf_tensor(f"{name}_{tag}", shape, dt))

        sem = semaphores(nc, ctx, "_" + tag)

        rows = sb("r_rows", [P, 2, TILES, P])
        y_hi = sb("r_hi", [P, 2, T], F32R)
        y_lo = sb("r_lo", [P, 2, T], F32R)
        turn = [ctx.enter_context(nc.psum_tensor(f"r_turn{k}_{tag}", [P, 2, 512], F32)) for k in range(2)]
        out = [ctx.enter_context(nc.psum_tensor(f"r_out{k}_{tag}", [P, TILES, E_N], F32)) for k in range(2)]
        centred, ready, turned, rounded, split, done, kept, cleared = (
            sem(s) for s in ("r_centred", "r_ready", "r_turned", "r_rounded", "r_split", "r_done", "r_kept",
                             "r_cleared"))
        with nc.Block() as block:
            @block.gpsimd
            def _(pool):
                def norm(b, slot):
                    if at_least(b, 2):
                        pool.wait_ge(turned, b - 1)
                    normalize(pool, g, rows[:, slot, :, :], b, centred, b + 1).then_inc(ready, 1)
                steps(pool, B, 2, norm)

            @block.tensor
            def _(pe):
                def turn_rows(b, slot):
                    pe.wait_ge(ready, b + 1)
                    if at_least(b, 2):
                        pe.wait_ge(split, b - 1)
                    turn_tiles(pe, g, turn[slot], rows[:, slot, :, :]).then_inc(turned, 1)

                def project(b, slot):
                    pe.wait_ge(split, b + 1)
                    if at_least(b, 2):
                        pe.wait_ge(kept, b - 1)
                    for c, n in enumerate(ROWS):
                        for k, (a, m) in enumerate([(y_hi, wg_hi), (y_hi, wg_lo), (y_lo, wg_hi)]):
                            last = pe.matmul(out[slot][0:n, c, :], a[:, slot, c * P:c * P + n], m[:, 0, :],
                                             start=(k == 0), stop=(k == 2))
                    last.then_inc(done, 1)

                def step(b, slot):
                    if before(b, B - 1):
                        turn_rows(b + 1, 1 - slot)
                    project(b, slot)
                turn_rows(0, 0)
                steps(pe, B, 2, step)

            @block.scalar
            def _(act):
                def round_y(b, slot):
                    act.wait_ge(turned, b + 1)
                    if at_least(b, 2):
                        act.wait_ge(done, b - 1)
                    round_cols(act, y_hi[:, slot, :], turn[slot]).then_inc(rounded, 1)
                steps(act, B, 2, round_y)

            @block.vector
            def _(dve):
                dve.memset(logits[:, :, :, :], 0.0).then_inc(cleared, 1)
                dve.wait_ge(cleared, 1)

                def split_y(b, slot):
                    dve.wait_ge(rounded, b + 1)
                    split_cols(dve, y_lo[:, slot, :], y_hi[:, slot, :], turn[slot]).then_inc(split, 1)

                def keep(b, slot):
                    dve.wait_ge(done, b + 1)
                    for c0, c1, n in [(0, TILES - 1, P), (TILES - 1, TILES, LAST)]:
                        dst = logits[0:n, c0:c1, bass.ds(b, 1), :].rearrange("p c o e -> p c (o e)")
                        if bias is None:
                            last = dve.tensor_copy(dst, out[slot][0:n, c0:c1, :])
                        else:
                            last = dve.tensor_tensor(dst, out[slot][0:n, c0:c1, :],
                                                     bias[0:n, :].unsqueeze(1).broadcast_to([n, c1 - c0, E_N]), ALU.add)
                    last.then_inc(kept, 1)

                def step(b, slot):
                    if before(b, B - 1):
                        split_y(b + 1, 1 - slot)
                    keep(b, slot)
                split_y(0, 0)
                steps(dve, B, 2, step)


def route(nc, g, logits, gates, k_tokens, k_experts, tag):
    N = B * TILES
    with ExitStack() as ctx:
        def sb(name, shape, dt=F32):
            return ctx.enter_context(nc.sbuf_tensor(f"{name}_{tag}", shape, dt))

        peak = sb("peak", [P, N])
        probs = logits
        total = sb("total", [P, N])
        turn = ctx.enter_context(nc.psum_tensor(f"g_turn_{tag}", [P, 2, 512], F32))
        gate_cols = sb("gate_cols", [P, T])
        work = sb("work", [P, T])
        cols = sb("cols", [P, T])
        best = sb("best", [P, 8])
        gate = sb("gate", [P, TILES, P]) if k_experts else None
        wins = sb("wins", [P, N, E_N])
        beats = sb("beats", [P, N, E_N])
        sem = semaphores(nc, ctx, "_" + tag)
        chain, exped, turned, copied, whole, kept = (
            sem(s) for s in ("g_chain", "g_exped", "g_turned", "g_copied", "g_whole", "g_kept"))
        flat = logits[:, :, :, :].rearrange("p c b e -> p (c b) e")

        def spread(a):
            return a[:, :].unsqueeze(2).broadcast_to([P, N, E_N])

        with nc.Block() as block:
            @block.vector
            def _(dve):
                count = [0]

                def then(ins):
                    count[0] += 1
                    ins.then_inc(chain, 1)
                    dve.wait_ge(chain, count[0])

                then(dve.tensor_reduce(peak[:, :], flat, AX.X, ALU.max))
                then(dve.tensor_tensor(flat, flat, spread(peak), ALU.subtract))
                dve.wait_ge(exped, 1)
                then(dve.tensor_reduce(total[:, :], flat, AX.X, ALU.add))
                then(dve.reciprocal(total[:, :], total[:, :]))
                then(dve.tensor_tensor(flat, flat, spread(total), ALU.mult))
                if k_experts:
                    then(dve.memset(wins[:, :, :], 0.0))
                    then(dve.memset(beats[:, :, :], 0.0))
                    for e in range(E_N):
                        one = flat[:, :, e:e + 1]
                        if e:
                            then(dve.tensor_tensor(beats[:, :, 0:e], one.broadcast_to([P, N, e]), flat[:, :, 0:e],
                                                   ALU.is_gt))
                        if e < E_N - 1:
                            then(dve.tensor_tensor(beats[:, :, e + 1:E_N], one.broadcast_to([P, N, E_N - 1 - e]),
                                                   flat[:, :, e + 1:E_N], ALU.is_ge))
                        if e:
                            then(dve.tensor_tensor(wins[:, :, 0:e], wins[:, :, 0:e], beats[:, :, 0:e], ALU.add))
                        if e < E_N - 1:
                            then(dve.tensor_tensor(wins[:, :, e + 1:E_N], wins[:, :, e + 1:E_N],
                                                   beats[:, :, e + 1:E_N], ALU.add))
                    then(dve.scalar_tensor_tensor(out=gate[:, :, :].rearrange("p c (b e) -> p (c b) e", e=E_N),
                                                  in0=wins[:, :, :], scalar=k_experts - 0.5, in1=flat,
                                                  op0=ALU.is_lt, op1=ALU.mult))
                dve.sem_inc(copied, 1)
                dve.wait_ge(turned, 1)
                if k_experts:
                    dve.tensor_copy(gate_cols[:, 0:512], turn[:, 0, :])
                    dve.tensor_copy(gate_cols[:, 512:T], turn[:, 1, 0:T - 512]).then_inc(whole, 1)
                    return
                for dst in (work, cols):
                    then(dve.tensor_copy(dst[:, 0:512], turn[:, 0, :]))
                    then(dve.tensor_copy(dst[:, 512:T], turn[:, 1, 0:T - 512]))
                rounds = -(-k_tokens // 8)
                for r in range(rounds):
                    then(dve.max(best[:, :], work[:, :]))
                    left = k_tokens - 8 * r
                    if left < 8:
                        then(dve.memset(best[:, left:8], -1.0))
                    then(dve.match_replace(work[:, :], best[:, :], work[:, :], -1.0))
                dve.scalar_tensor_tensor(out=gate_cols[:, :], in0=work[:, :], scalar=0.0, in1=cols[:, :],
                                         op0=ALU.is_lt, op1=ALU.mult).then_inc(whole, 1)

            @block.sync
            def _(sp):
                sp.wait_ge(whole, 1)
                sp.dma_start(gates, gate_cols[:, :]).then_inc(kept, 16)
                sp.wait_ge(kept, 16)

            @block.scalar
            def _(act):
                act.wait_ge(chain, 2)
                act.activation(flat, flat, ACT.Exp).then_inc(exped, 1)

            @block.tensor
            def _(pe):
                pe.wait_ge(copied, 1)
                src = gate[:, :, :] if k_experts else probs[:, :, :, :].rearrange("p c b e -> p c (b e)")
                turn_tiles(pe, g, turn, src).then_inc(turned, 1)


def gated_ffn(nc, g, w1_hi, w1_lo, b1, w2_hi, w2_lo, b2, shared_b2, blocks, shared, gates, tag):
    LAG, RING = 3, 4
    EXPERTS = w2_hi.shape[1] // blocks
    UP = EXPERTS * blocks
    FREE = shared * blocks
    FIRST = 1 if shared else 0
    ITEMS = FIRST + E_N
    SUMS = 2 * (ITEMS - 1)
    G_RING = 2 if shared else 4
    PARTS = [slice(0, 3 * P), slice(3 * P, T)]
    BACK_AT, TURN_AT = [5, 7], [9, 12]
    assert UP % RING == 0 and E_N % G_RING == 0 and UP > TURN_AT[1] + 1

    def item_of(k):
        return 0 if k < FREE else FIRST + (k - FREE) // blocks

    def opens(k):
        return k == 0 or k >= FREE and (k - FREE) % blocks == 0

    def ends(k):
        return k == FREE - 1 if k < FREE else (k - FREE) % blocks == blocks - 1

    def last_of(item):
        return FREE + (item - FIRST + 1) * blocks - 1

    with ExitStack() as ctx:
        def sb(name, shape, dt=F32):
            return ctx.enter_context(nc.sbuf_tensor(f"{name}_{tag}", shape, dt))

        def ps(name, shape):
            return ctx.enter_context(nc.psum_tensor(f"{name}_{tag}", shape, F32))

        sem = semaphores(nc, ctx, "_" + tag)

        rows = sb("f_rows", [P, TILES, P])
        y_hi = sb("f_hi", [P, 2, T], F32R)
        y_lo = sb("f_lo", [P, 2, T], F32R)
        hid = sb("f_hid", [P, 2, T])
        hid_hi = sb("f_hid_hi", [P, RING, T], F32R)
        hid_lo = sb("f_hid_lo", [P, RING, T], F32R)
        gate = sb("f_gate", [P, G_RING, T])
        acc = sb("f_acc", [P, 2, T])
        turn, back = ps("f_turn", [P, 512]), ps("f_back", [P, 4, P])
        up = [ps(f"f_up{h}", [P, 512]) for h in range(2)]
        down = [[ps(f"f_down{q}{h}", [P, 512]) for h in range(2)] for q in range(2)]
        (centred, ready, turned, rounded, split, up_done, gelu_done, hi_done, lo_done, hid_used, gated, summed,
         turned_back, returned) = (
            sem(s) for s in ("f_centred", "f_ready", "f_turned", "f_rounded", "f_split", "f_up_done", "f_gelu_done",
                             "f_hi_done", "f_lo_done", "f_hid_used", "f_gated", "f_summed", "f_turned_back",
                             "f_returned"))
        gate_in = [sem(f"f_gate_in{k}") for k in range(G_RING)]

        def sum_of(slot, item, h):
            place = (slot + item) % 2 if ITEMS % 2 else item % 2
            return down[place][h][:, 0:HALF]

        with nc.Block() as block:
            @block.sync
            def _(sp):
                def fetch(b, slot):
                    for e in range(E_N):
                        if e >= G_RING:
                            item = FIRST + e - G_RING
                            if item:
                                sp.wait_ge(summed, b * SUMS + 2 * item)
                            else:
                                sp.wait_ge(gated, b * (2 * ITEMS) + 2)
                        elif at_least(b, 1):
                            sp.wait_ge(summed, b * SUMS - 2 * (G_RING - e - 1))
                        sp.dma_start(gate[:, e % G_RING, :],
                                     gates[bass.ds(b * E_N + e, 1), :].broadcast_to([P, T])
                                     ).then_inc(gate_in[e % G_RING], 16)
                steps(sp, B, 2, fetch)

            @block.gpsimd
            def _(pool):
                def norm(b, slot):
                    if at_least(b, 1):
                        pool.wait_ge(turned, b * 2)
                    normalize(pool, g, rows[:, :, :], b, centred, b + 1).then_inc(ready, 1)
                steps(pool, B, 2, norm)

            @block.tensor
            def _(pe):
                def turn_rows(b, slot, part):
                    if part == 0:
                        pe.wait_ge(ready, b + 1)
                    if at_least(b, 1) or part:
                        pe.wait_ge(split, b * 2 + part)
                    for c in range(3 * part, 3 * part + 3):
                        last = pe.transpose(turn[:, (c % 3) * P:(c % 3) * P + ROWS[c]], rows[0:ROWS[c], c, :],
                                            g.ident[0:ROWS[c], 0:ROWS[c]])
                    last.then_inc(turned, 1)

                def widen(b, slot, k):
                    for h, cols in enumerate(HALVES):
                        if at_least(b, 1) or k:
                            pe.wait_ge(gelu_done, b * (2 * UP) + (2 * k - 1 + h))
                        for i, (a, m) in enumerate([(w1_hi, y_hi), (w1_hi, y_lo), (w1_lo, y_hi)]):
                            last = pe.matmul(up[h][:, 0:HALF], a[:, k, :], m[:, slot, cols],
                                             start=(i == 0), stop=(i == 2))
                        last.then_inc(up_done, 1)

                def narrow(b, slot, k):
                    item = item_of(k)
                    pe.wait_ge(lo_done, b * UP + (k + 1))
                    for h, cols in enumerate(HALVES):
                        if opens(k) and (at_least(b, 1) or item >= 2):
                            pe.wait_ge(gated, b * (2 * ITEMS) + (2 * item - 3 + h))
                        for i, (a, m) in enumerate([(w2_hi, hid_hi), (w2_hi, hid_lo), (w2_lo, hid_hi)]):
                            last = pe.matmul(sum_of(slot, item, h), a[:, k, :], m[:, k % RING, cols],
                                             start=(opens(k) and i == 0), stop=(ends(k) and i == 2))
                    last.then_inc(hid_used, 1)

                def turn_back(b, slot, part):
                    if part == 0:
                        pe.wait_ge(summed, b * SUMS + SUMS)
                    if at_least(b, 1) or part:
                        pe.wait_ge(returned, b * 2 + part)
                    for c in range(3 * part, 3 * part + 3):
                        last = pe.transpose(back[0:ROWS[c], c % 3, :], acc[:, slot, c * P:c * P + ROWS[c]],
                                            g.ident[:, :])
                    last.then_inc(turned_back, 1)

                def step(b, slot):
                    pe.wait_ge(split, b * 2 + 2)
                    for k in range(UP):
                        widen(b, slot, k)
                        if k >= LAG:
                            narrow(b, slot, k - LAG)
                        elif at_least(b, 1):
                            narrow(b - 1, 1 - slot, UP + k - LAG)
                        if k in BACK_AT and at_least(b, 1):
                            turn_back(b - 1, 1 - slot, BACK_AT.index(k))
                        if k in TURN_AT and before(b, B - 1):
                            turn_rows(b + 1, 1 - slot, TURN_AT.index(k))
                turn_rows(0, 0, 0)
                turn_rows(0, 0, 1)
                steps(pe, B, 2, step)
                for k in range(UP - LAG, UP):
                    narrow(B - 1, (B - 1) % 2, k)
                turn_back(B - 1, (B - 1) % 2, 0)
                turn_back(B - 1, (B - 1) % 2, 1)

            @block.scalar
            def _(act):
                def round_y(b, slot, part):
                    act.wait_ge(turned, b * 2 + (part + 1))
                    if at_least(b, 2):
                        act.wait_ge(up_done, b * (2 * UP) - 2 * UP)
                    cols = PARTS[part]
                    act.copy(y_hi[:, slot, cols], turn[:, 0:cols.stop - cols.start]).then_inc(rounded, 1)

                def step(b, slot):
                    for k in range(UP):
                        if at_least(b, 1) or k >= 2:
                            act.wait_ge(lo_done, b * UP + (k - 1))
                        for h, cols in enumerate(HALVES):
                            act.wait_ge(up_done, b * (2 * UP) + (2 * k + 1 + h))
                            act.activation(hid[:, k % 2, cols], up[h][:, 0:HALF], ACT.Gelu,
                                           bias=b1[:, 0, k:k + 1]).then_inc(gelu_done, 1)
                        act.wait_ge(gelu_done, b * (2 * UP) + (2 * k + 2))
                        if at_least(b, 1) or k >= RING:
                            act.wait_ge(hid_used, b * UP + (k - RING + 1))
                        act.copy(hid_hi[:, k % RING, :], hid[:, k % 2, :]).then_inc(hi_done, 1)
                        if k - 1 in TURN_AT and before(b, B - 1):
                            round_y(b + 1, 1 - slot, TURN_AT.index(k - 1))
                round_y(0, 0, 0)
                round_y(0, 0, 1)
                steps(act, B, 2, step)

            @block.vector
            def _(dve):
                def split_y(b, slot, part):
                    dve.wait_ge(rounded, b * 2 + (part + 1))
                    cols = PARTS[part]
                    dve.tensor_tensor(y_lo[:, slot, cols], turn[:, 0:cols.stop - cols.start],
                                      y_hi[:, slot, cols].bitcast(F32), ALU.subtract).then_inc(split, 1)

                def split_hid(b, k):
                    dve.wait_ge(hi_done, b * UP + (k + 1))
                    dve.tensor_tensor(hid_lo[:, k % RING, :], hid[:, k % 2, :],
                                      hid_hi[:, k % RING, :].bitcast(F32), ALU.subtract).then_inc(lo_done, 1)

                def take(b, slot, item):
                    e = item - FIRST
                    dve.wait_ge(hid_used, b * UP + (last_of(item) + 1))
                    if e >= 0:
                        dve.wait_ge(gate_in[e % G_RING], b * (16 * E_N // G_RING) + 16 * (e // G_RING + 1))
                    if item == 0 and at_least(b, 2):
                        dve.wait_ge(turned_back, b * 2 - 2)
                    for h, cols in enumerate(HALVES):
                        if e < 0:
                            ins = dve.tensor_scalar(acc[:, slot, cols], sum_of(slot, item, h), shared_b2, None, ALU.add)
                        else:
                            to = gate[:, e % G_RING, cols] if item else acc[:, slot, cols]
                            ins = dve.scalar_tensor_tensor(out=to, in0=sum_of(slot, item, h), scalar=b2[:, 0, e:e + 1],
                                                           in1=gate[:, e % G_RING, cols], op0=ALU.add, op1=ALU.mult)
                        ins.then_inc(gated, 1)
                    for h, cols in enumerate(HALVES if item else []):
                        dve.wait_ge(gated, b * (2 * ITEMS) + (2 * item + 1 + h))
                        if item >= 2:
                            dve.wait_ge(summed, b * SUMS + (2 * item - 3 + h))
                        dve.tensor_tensor(acc[:, slot, cols], acc[:, slot, cols], gate[:, e % G_RING, cols], ALU.add
                                          ).then_inc(summed, 1)

                def takes(b, slot, k):
                    if ends(k):
                        take(b, slot, item_of(k))

                def give_back(b, part):
                    dve.wait_ge(turned_back, b * 2 + (part + 1))
                    for c0, c1, n in [(0, 3, P)] if part == 0 else [(3, 5, P), (5, 6, LAST)]:
                        h = g.h[0:n, bass.ds(b * TILES + c0, c1 - c0), :]
                        last = dve.tensor_tensor(h, h, back[0:n, c0 % 3:c0 % 3 + (c1 - c0), :], ALU.add)
                    last.then_inc(returned, 1)

                def step(b, slot):
                    for k in range(UP):
                        split_hid(b, k)
                        if k >= LAG:
                            takes(b, slot, k - LAG)
                        elif at_least(b, 1):
                            takes(b - 1, 1 - slot, UP + k - LAG)
                        if k - 1 in BACK_AT and at_least(b, 1):
                            give_back(b - 1, BACK_AT.index(k - 1))
                        if k - 1 in TURN_AT and before(b, B - 1):
                            split_y(b + 1, 1 - slot, TURN_AT.index(k - 1))
                split_y(0, 0, 0)
                split_y(0, 0, 1)
                steps(dve, B, 2, step)
                for k in range(UP - LAG, UP):
                    takes(B - 1, (B - 1) % 2, k)
                give_back(B - 1, 0)
                give_back(B - 1, 1)


def load_small(nc, loads, tag):
    clears = [c for _, _, c in loads if c is not None]
    with ExitStack() as ctx:
        sem = semaphores(nc, ctx, "_" + tag)
        done, cleared = sem("small_loaded"), sem("small_cleared")
        with nc.Block() as block:
            @block.vector
            def _(dve):
                for c in clears:
                    dve.memset(c, 0.0).then_inc(cleared, 1)

            @block.sync
            def _(sp):
                if clears:
                    sp.wait_ge(cleared, len(clears))
                for dst, src, _ in loads:
                    sp.dma_start(dst, src).then_inc(done, 16)
                sp.wait_ge(done, 16 * len(loads))


def expert_choice(nc, g, w):
    HID = 256
    BLOCKS = HID // P
    K_TOKENS = min(max(T * 2 // E_N, 1), T)
    row_statistics(nc, g, "n1")
    with ExitStack() as ctx:
        def sb(name, shape, dt=F32):
            return ctx.enter_context(nc.sbuf_tensor(name, shape, dt))

        gates = nc.dram_tensor("c_gates", (P, T), F32, kind="Internal").ap()
        w1_hi = sb("c_w1_hi", [P, E_N * BLOCKS, P], F32R)
        w1_lo = sb("c_w1_lo", [P, E_N * BLOCKS, P], F32R)
        w2_hi = sb("c_w2_hi", [P, E_N * BLOCKS, P], F32R)
        w2_lo = sb("c_w2_lo", [P, E_N * BLOCKS, P], F32R)
        b1 = sb("c_b1", [P, 1, E_N * BLOCKS])
        b2 = sb("c_b2", [P, 1, E_N])
        with ExitStack() as inner:
            wg_hi = inner.enter_context(nc.sbuf_tensor("c_wg_hi", [P, 1, E_N], F32R))
            wg_lo = inner.enter_context(nc.sbuf_tensor("c_wg_lo", [P, 1, E_N], F32R))
            logits = inner.enter_context(nc.sbuf_tensor("c_logits", [P, TILES, B, E_N], F32))
            split_weights(nc, g, [
                (wg_hi[:, :, :], wg_lo[:, :, :], w["L0_ffn_Wg"].rearrange("h (o e) -> h o e", o=1), False),
                *[(w1_hi[:, e * BLOCKS:(e + 1) * BLOCKS, :], w1_lo[:, e * BLOCKS:(e + 1) * BLOCKS, :],
                   w["L0_ffn_W1"][e].rearrange("h (j f) -> h j f", f=P), False) for e in range(E_N)],
                (w2_hi[:, :, :], w2_lo[:, :, :], w["L0_ffn_W2"].rearrange("e (j f) h -> f (e j) h", f=P), False),
                (b2[:, :, :], None, w["L0_ffn_b2"].rearrange("e (o h) -> e o h", o=1), True),
                (b1[:, :, :], None, w["L0_ffn_b1"].rearrange("e (j o f) -> (e j) o f", o=1, f=P), True),
            ], "c")
            router_logits(nc, g, wg_hi, wg_lo, None, logits, "c")
            route(nc, g, logits, gates, K_TOKENS, None, "c")
        gated_ffn(nc, g, w1_hi, w1_lo, b1, w2_hi, w2_lo, b2, None, BLOCKS, 0, gates, "c")


S_HEADS = 8
S_DIM = 64
SLICES = 32
HS = S_HEADS * SLICES


def slice_weights(nc, g, w, wqk_hi, wqk_lo, fold, bias_q, bias_k, bias_out):
    with ExitStack() as ctx:
        def sb(name, shape, dt=F32):
            return ctx.enter_context(nc.sbuf_tensor(name, shape, dt))

        def psum(name, shape):
            return ctx.enter_context(nc.psum_tensor(name, shape, F32))

        sem = semaphores(nc, ctx)

        win_t = sb("win_t", [S_DIM, S_HEADS, P])
        wv_t = sb("wv_t", [S_DIM, 1, S_DIM])
        b_col = sb("b_col", [S_DIM, 1, S_HEADS])
        wqk = sb("wqk_raw", [S_DIM, 2, SLICES])
        w_out = sb("w_out_raw", [S_DIM, S_HEADS, P])
        b_out = sb("b_out_rows", [P, P])
        b_wide = sb("b_wide", [S_DIM, S_HEADS, P])
        wvo = sb("wvo", [S_DIM, S_HEADS, P])
        split_weights(nc, g, [
            (win_t[:, :, :], None, w["L1_attn_W_in"].rearrange("d (h k) -> d h k", k=S_DIM), True),
            (wv_t[:, :, :], None, w["L1_attn_Wv"].rearrange("k (o c) -> k o c", o=1), True),
            (b_col[:, :, :], None, w["L1_attn_b_in"].rearrange("(h o k) -> h o k", o=1, k=S_DIM), True)], "d")
        load_small(nc, [
            (wqk[:, 0, :], w["L1_attn_Wq"], None), (wqk[:, 1, :], w["L1_attn_Wk"], None),
            (w_out[:, :, :], w["L1_attn_W_out"].rearrange("(h k) o -> k h o", k=S_DIM), None),
            (b_out[:, :], w["L1_attn_b_out"].unsqueeze(0).broadcast_to([P, P]), None)], "d")
        p_vo = psum("p_vo", [S_DIM, 2, 4, P])
        p_qk = psum("p_qk", [P, S_HEADS, 2, SLICES])
        p_fold = psum("p_fold", [P, 2, 4, P])
        p_bq = psum("p_bq", [P, S_HEADS, SLICES])
        p_bo = psum("p_bo", [P, 2, P])
        p_bk = psum("p_bk", [P, 2])
        widened, vo_done, vo_kept, rest_done, rounded = (
            sem(s) for s in ("b_widened", "vo_done", "vo_kept", "rest_done", "wqk_rounded"))
        with nc.Block() as block:
            @block.tensor
            def _(pe):
                for h in range(S_HEADS):
                    last = pe.matmul(p_vo[:, h // 4, h % 4, :], wv_t[:, 0, :], w_out[:, h, :], start=True, stop=True)
                last.then_inc(vo_done, 1)
                pe.wait_ge(widened, 1)
                pe.wait_ge(vo_kept, 1)
                for h in range(S_HEADS):
                    at = slice((h % 4) * SLICES, (h % 4 + 1) * SLICES)
                    pe.matmul(p_qk[:, h, :, :], win_t[:, h, :], wqk[:, :, :], start=True, stop=True)
                    pe.matmul(p_fold[:, h // 4, h % 4, :], win_t[:, h, :], wvo[:, h, :], start=True, stop=True)
                    pe.matmul(p_bq[:, h, :], b_wide[:, h, :], wqk[:, 0, :], start=True, stop=True)
                    pe.matmul(p_bo[at, h // 4, :], b_wide[:, h, 0:SLICES], wvo[:, h, :], start=True, stop=True)
                    last = pe.matmul(p_bk[at, h // 4:h // 4 + 1], wqk[:, 1, :], b_col[:, 0, h:h + 1],
                                     start=True, stop=True)
                last.then_inc(rest_done, 1)

            @block.vector
            def _(dve):
                dve.tensor_copy(b_wide[:, :, :], b_col[:, 0, :].unsqueeze(2).broadcast_to([S_DIM, S_HEADS, P])
                                ).then_inc(widened, 1)
                dve.wait_ge(vo_done, 1)
                dve.tensor_copy(wvo[:, :, :], p_vo[:, :, :, :].rearrange("p a b o -> p (a b) o")).then_inc(vo_kept, 1)
                dve.wait_ge(rest_done, 1)
                for j in range(2):
                    dve.scalar_tensor_tensor(out=bias_out[:, j, :], in0=b_out[:, :], scalar=1.0 / S_HEADS,
                                             in1=p_bo[:, j, :], op0=ALU.mult, op1=ALU.add)
                dve.tensor_copy(bias_k[:, :], p_bk[:, :])
                dve.tensor_copy(fold[:, :, :], p_fold[:, :, :, :].rearrange("p a b o -> p (a b) o"))
                dve.wait_ge(rounded, 3)
                for j in range(2):
                    dve.tensor_tensor(wqk_lo[:, j, :].rearrange("p (h s) -> p h s", s=SLICES), p_qk[:, :, j, :],
                                      wqk_hi[:, j, :].bitcast(F32).rearrange("p (h s) -> p h s", s=SLICES), ALU.subtract)
                dve.tensor_tensor(bias_q[:, 1, :].rearrange("p (h s) -> p h s", s=SLICES), p_bq[:, :, :],
                                  bias_q[:, 0, :].bitcast(F32).rearrange("p (h s) -> p h s", s=SLICES), ALU.subtract)

            @block.scalar
            def _(act):
                act.wait_ge(rest_done, 1)
                for j in range(2):
                    act.copy(wqk_hi[:, j, :].rearrange("p (h s) -> p h s", s=SLICES), p_qk[:, :, j, :]
                             ).then_inc(rounded, 1)
                act.copy(bias_q[:, 0, :].rearrange("p (h s) -> p h s", s=SLICES), p_bq[:, :, :]).then_inc(rounded, 1)


def slice_attention(nc, g, w):
    row_statistics(nc, g, "n2")
    with ExitStack() as ctx:
        def sb(name, shape, dt=F32):
            return ctx.enter_context(nc.sbuf_tensor(name, shape, dt))

        sem = semaphores(nc, ctx)

        wqk_hi, wqk_lo = sb("wqk_hi", [P, 2, HS], F32R), sb("wqk_lo", [P, 2, HS], F32R)
        fold = sb("fold", [P, S_HEADS, P])
        bias_q = sb("bias_q", [P, 2, HS], F32R)
        bias_k = sb("bias_k", [P, 2])
        bias_out = sb("bias_out", [P, 2, P])
        slice_weights(nc, g, w, wqk_hi, wqk_lo, fold, bias_q, bias_k, bias_out)

        first_row = sb("first_row", [P, P], F32R)
        rows = sb("d_rows", [P, 2, TILES, P])
        y_hi, y_lo = sb("d_hi", [P, 2, T], F32R), sb("d_lo", [P, 2, T], F32R)
        k_neg, k_shift = sb("k_neg", [P, 2]), sb("k_shift", [P, 2])
        k_sum, k_inv = sb("k_sum", [P, 2, 2]), sb("k_inv", [P, 2])
        k_exp = sb("k_exp", [P, 2, T])
        k_tok = sb("k_tok", [P, TILES, HS])
        ky = sb("ky", [P, HS])
        mix = sb("mix", [P, 2, P])
        q_sb = sb("q_sb", [P, 2, TILES * S_HEADS, SLICES])
        q_peak, q_sum = sb("q_peak", [P, TILES * S_HEADS]), sb("q_sum", [P, 2, TILES * S_HEADS])
        q_cols = sb("q_cols", [P, 2, T])
        PA, PB, PC = [ctx.enter_context(nc.psum_tensor(f"d_pair{k}", [P, 2, 512], F32)) for k in range(3)]
        p_ky = ctx.enter_context(nc.psum_tensor("p_ky", [P, HS], F32))
        p_mix = ctx.enter_context(nc.psum_tensor("p_mix", [P, 2, P], F32))
        used = [sem(f"d_used{k}") for k in range(3)]
        (row_set, centred, ready, turned, rounded, k_done, k_negated, k_shifted, k_turned, ky_done, ky_kept, mix_done,
         k_inverted, mix_ready, q_done, q_peaked, q_exped, q_summed, q_inverted, q_ready, q_turned, out_done) = (
            sem("d_" + s) for s in (
                "row_set", "centred", "ready", "turned", "rounded", "k_done", "k_negated", "k_shifted", "k_turned",
                "ky_done", "ky_kept", "mix_done", "k_inverted", "mix_ready", "q_done", "q_peaked", "q_exped",
                "q_summed", "q_inverted", "q_ready", "q_turned", "out_done"))
        A, B_, C = range(3)
        PLACE = {"y": (A, 0), "k0": (A, 1), "q1": (A, 2), "out": (A, 3),
                 "kt0": (B_, 0), "k1": (B_, 1), "qt0": (B_, 2),
                 "kt1": (C, 0), "q0": (C, 1), "qt1": (C, 2)}
        AHEAD = {"y": 0, "k0": 1, "q1": 2, "k1": 0, "q0": 0}
        LEFT = {"kt0": 0, "qt0": 1, "kt1": 0, "qt1": 1, "out": 0}
        ROUND = {A: 4, B_: 3, C: 3}
        START = {A: 3, B_: 1, C: 1}

        def place(job, b):
            pair, at = PLACE[job]
            if job in AHEAD:
                if isinstance(b, int) and b == 0:
                    return pair, AHEAD[job]
                return pair, b * ROUND[pair] + (START[pair] - ROUND[pair] + at)
            if isinstance(b, int) and b == B - 1:
                at = LEFT[job]
            return pair, b * ROUND[pair] + (START[pair] + at)

        def free(eng, job, b):
            pair, before_it = place(job, b)
            if not (isinstance(before_it, int) and before_it == 0):
                eng.wait_ge(used[pair], before_it)

        def over(eng, job, b):
            pair, before_it = place(job, b)
            eng.wait_ge(used[pair], before_it + 1)

        Q_PARTS = [(0, 4), (4, 2)]


        with nc.Block() as block:
            @block.gpsimd
            def _(pool):
                pool.memset(first_row[:, :].bitcast(F32), 0.0).then_inc(row_set, 1)
                pool.wait_ge(row_set, 1)
                pool.memset(first_row[0:1, :].bitcast(F32), 1.0).then_inc(row_set, 1)

                def norm(b, slot):
                    if at_least(b, 2):
                        pool.wait_ge(ky_done, b - 1)
                    normalize(pool, g, rows[:, slot, :, :], b, centred, b + 1).then_inc(ready, 1)

                def scale_q(b, slot):
                    for part, (c, n) in enumerate(Q_PARTS):
                        pool.wait_ge(q_inverted, b * 2 + (part + 1))
                        at = slice(c * S_HEADS, (c + n) * S_HEADS)
                        q = q_sb[:, slot, at, :]
                        pool.tensor_tensor(q, q, q_sum[:, slot, at].unsqueeze(2).broadcast_to(
                            [P, n * S_HEADS, SLICES]), ALU.mult).then_inc(q_ready, 1)

                def rounds(b, slot):
                    if before(b, B - 1):
                        scale_q(b + 1, 1 - slot)
                    if before(b, B - 2):
                        norm(b + 2, slot)
                norm(0, 0)
                norm(1, 1)
                scale_q(0, 0)
                steps(pool, B, 2, rounds)

            @block.tensor
            def _(pe):
                def turn_y(b, slot):
                    pe.wait_ge(ready, b + 1)
                    free(pe, "y", b)
                    turn_tiles(pe, g, PA, rows[:, slot, :, :]).then_inc(turned, 1)

                def k_proj(b, slot, j):
                    if j == 0:
                        over(pe, "y", b)
                    free(pe, f"k{j}", b)
                    for h, cols in enumerate(HALVES):
                        for i, (a, m) in enumerate([(wqk_hi, y_hi), (wqk_hi, y_lo), (wqk_lo, y_hi)]):
                            last = pe.matmul((PA, PB)[j][:, h, 0:HALF], a[:, 1, j * P:(j + 1) * P], m[:, slot, cols],
                                             start=(i == 0), stop=(i == 2))
                    last.then_inc(k_done, 1)

                def q_proj(b, slot, part):
                    free(pe, f"q{part}", b)
                    c0, n_tiles = Q_PARTS[part]
                    for c in range(c0, c0 + n_tiles):
                        n, at = ROWS[c], c - c0
                        out = (PC, PA)[part][0:n, at // 2, (at % 2) * HS:(at % 2 + 1) * HS]
                        for i, (a, m) in enumerate([(y_hi, wqk_hi), (y_hi, wqk_lo), (y_lo, wqk_hi)]):
                            pe.matmul(out, a[:, slot, c * P:c * P + n], m[:, 0, :], start=(i == 0), stop=False)
                        pe.matmul(out, first_row[:, 0:n], bias_q[:, 0, :], start=False, stop=False)
                        last = pe.matmul(out, first_row[:, 0:n], bias_q[:, 1, :], start=False, stop=True)
                    last.then_inc(q_done, 1)

                def k_turn(b, part):
                    if part == 0:
                        over(pe, "k0", b)
                        over(pe, "k1", b)
                    free(pe, f"kt{part}", b)
                    c0, n_tiles = Q_PARTS[part]
                    for c in range(c0, c0 + n_tiles):
                        at = c - c0
                        for j in range(2):
                            last = pe.transpose((PB, PC)[part][0:ROWS[c], at // 2, (at % 2) * HS + j * P:
                                                               (at % 2) * HS + (j + 1) * P],
                                                k_exp[:, j, c * P:c * P + ROWS[c]], g.ident[:, :])
                    last.then_inc(k_turned, 1)

                def ky_sum(b, slot):
                    over(pe, "kt0", b)
                    over(pe, "kt1", b)
                    if at_least(b, 1):
                        pe.wait_ge(ky_kept, b)
                    for c, n in enumerate(ROWS):
                        last = pe.matmul(p_ky[:, :], rows[0:n, slot, c, :], k_tok[0:n, c, :],
                                         start=(c == 0), stop=(c == TILES - 1))
                    last.then_inc(ky_done, 1)

                def mixing(b):
                    pe.wait_ge(ky_kept, b + 1)
                    if at_least(b, 1):
                        pe.wait_ge(mix_ready, b)
                    for h in range(S_HEADS):
                        last = pe.matmul(p_mix[(h % 4) * SLICES:(h % 4 + 1) * SLICES, h // 4, :],
                                         ky[:, h * SLICES:(h + 1) * SLICES], fold[:, h, :], start=True, stop=True)
                    last.then_inc(mix_done, 1)

                def q_turn(b, slot, j):
                    if j == 0:
                        pe.wait_ge(q_ready, b * 2 + 2)
                    free(pe, f"qt{j}", b)
                    for c, n in enumerate(ROWS):
                        src = q_sb[0:n, slot, c * S_HEADS + j * 4:c * S_HEADS + (j + 1) * 4, :]
                        last = pe.transpose((PB, PC)[j][:, c // 4, (c % 4) * P:(c % 4) * P + n],
                                            src.rearrange("p h s -> p (h s)"), g.ident[0:n, 0:n])
                    last.then_inc(q_turned, 1)

                def output(b):
                    over(pe, "qt0", b)
                    over(pe, "qt1", b)
                    pe.wait_ge(mix_ready, b + 1)
                    free(pe, "out", b)
                    for c, n in enumerate(ROWS):
                        for j in range(2):
                            last = pe.matmul(PA[0:n, c // 4, (c % 4) * P:(c % 4 + 1) * P],
                                             q_cols[:, j, c * P:c * P + n], mix[:, j, :], start=(j == 0), stop=(j == 1))
                    last.then_inc(out_done, 1)

                def rounds(b, slot):
                    nxt, more = 1 - slot, before(b, B - 1)
                    if more:
                        turn_y(b + 1, nxt)
                    k_turn(b, 0)
                    k_turn(b, 1)
                    if more:
                        k_proj(b + 1, nxt, 0)
                        k_proj(b + 1, nxt, 1)
                    ky_sum(b, slot)
                    if more:
                        q_proj(b + 1, nxt, 0)
                    mixing(b)
                    if more:
                        q_proj(b + 1, nxt, 1)
                    q_turn(b, slot, 0)
                    q_turn(b, slot, 1)
                    output(b)
                pe.wait_ge(row_set, 2)
                turn_y(0, 0)
                k_proj(0, 0, 0)
                k_proj(0, 0, 1)
                q_proj(0, 0, 0)
                q_proj(0, 0, 1)
                steps(pe, B, 2, rounds)

            @block.vector
            def _(dve):
                def split_y(b, slot):
                    dve.wait_ge(rounded, b + 1)
                    split_cols(dve, y_lo[:, slot, :], y_hi[:, slot, :], PA).then_inc(used[A], 1)

                def k_peak(b, j):
                    dve.wait_ge(k_done, b * 2 + (j + 1))
                    dve.tensor_reduce(k_neg[:, j:j + 1], (PA, PB)[j][:, :, 0:HALF], AX.XY, ALU.max, negate=True
                                      ).then_inc(k_negated, 1)
                    dve.wait_ge(k_negated, b * 2 + (j + 1))
                    if at_least(b, 1):
                        dve.wait_ge(used[(A, B_)[j]], place(f"k{j}", b)[1])
                    dve.scalar_tensor_tensor(out=k_shift[:, j:j + 1], in0=k_neg[:, j:j + 1], scalar=bias_k[:, j:j + 1],
                                             in1=bias_k[:, j:j + 1], op0=ALU.subtract, op1=ALU.add
                                             ).then_inc(k_shifted, 1)

                def q_centre(b, slot, part):
                    dve.wait_ge(q_done, b * 2 + (part + 1))
                    c, n = Q_PARTS[part]
                    at = slice(c * S_HEADS, (c + n) * S_HEADS)
                    src = (PC[:, :, :] if part == 0 else PA[:, 0:1, :]).rearrange("p a (h s) -> p (a h) s", s=SLICES)
                    dve.tensor_reduce(q_peak[:, at], src, AX.X, ALU.max).then_inc(q_peaked, 1)
                    dve.wait_ge(q_peaked, b * 2 + (part + 1))
                    if at_least(b, 2):
                        dve.wait_ge(q_turned, b * 2 - 2)
                    dve.tensor_tensor(q_sb[:, slot, at, :], src, q_peak[:, at].unsqueeze(2).broadcast_to(
                        [P, n * S_HEADS, SLICES]), ALU.subtract).then_inc(used[(C, A)[part]], 1)

                def q_total(b, slot, part):
                    c, n = Q_PARTS[part]
                    at = slice(c * S_HEADS, (c + n) * S_HEADS)
                    dve.wait_ge(q_exped, b * 2 + (part + 1))
                    dve.tensor_reduce(q_sum[:, slot, at], q_sb[:, slot, at, :], AX.X, ALU.add).then_inc(q_summed, 1)
                    dve.wait_ge(q_summed, b * 2 + (part + 1))
                    dve.reciprocal(q_sum[:, slot, at], q_sum[:, slot, at]).then_inc(q_inverted, 1)

                def mix_out(b, slot):
                    over(dve, "k0", b)
                    over(dve, "k1", b)
                    dve.reciprocal(k_inv[:, :], k_sum[:, slot, :]).then_inc(k_inverted, 1)
                    dve.wait_ge(k_inverted, b + 1)
                    dve.wait_ge(mix_done, b + 1)
                    if at_least(b, 1):
                        dve.wait_ge(out_done, b)
                    for j in range(2):
                        last = dve.scalar_tensor_tensor(out=mix[:, j, :], in0=p_mix[:, j, :], scalar=k_inv[:, j:j + 1],
                                                        in1=bias_out[:, j, :], op0=ALU.mult, op1=ALU.add)
                    last.then_inc(mix_ready, 1)

                def add(b):
                    dve.wait_ge(out_done, b + 1)
                    for c0, c1, n in [(0, 4, P), (4, 5, P), (5, 6, LAST)]:
                        h = g.h[0:n, bass.ds(b * TILES + c0, c1 - c0), :]
                        src = PA[0:n, c0 // 4, (c0 % 4) * P:((c1 - 1) % 4 + 1) * P].rearrange("p (c d) -> p c d", d=P)
                        last = dve.tensor_tensor(h, src, h, ALU.add)
                    last.then_inc(used[A], 1)

                def rounds(b, slot):
                    nxt, more = 1 - slot, before(b, B - 1)
                    if more:
                        split_y(b + 1, nxt)
                        k_peak(b + 1, 0)
                        k_peak(b + 1, 1)
                        q_centre(b + 1, nxt, 0)
                    mix_out(b, slot)
                    if more:
                        q_centre(b + 1, nxt, 1)
                        q_total(b + 1, nxt, 0)
                        q_total(b + 1, nxt, 1)
                    add(b)
                split_y(0, 0)
                for j in range(2):
                    k_peak(0, j)
                for part in range(2):
                    q_centre(0, 0, part)
                for part in range(2):
                    q_total(0, 0, part)
                steps(dve, B, 2, rounds)

            @block.scalar
            def _(act):
                def round_y(b, slot):
                    act.wait_ge(turned, b + 1)
                    if at_least(b, 2):
                        act.wait_ge(q_done, b * 2 - 2)
                    round_cols(act, y_hi[:, slot, :], PA).then_inc(rounded, 1)

                def k_keep(b, part):
                    act.wait_ge(k_turned, b * 2 + (part + 1))
                    if at_least(b, 1):
                        act.wait_ge(ky_done, b)
                    c, n = Q_PARTS[part]
                    src = PB[:, :, :] if part == 0 else PC[:, 0:1, :]
                    act.copy(k_tok[:, c:c + n, :].rearrange("p (a c) s -> p a (c s)", c=2), src
                             ).then_inc(used[(B_, C)[part]], 1)

                def k_exps(b, slot, j):
                    act.wait_ge(k_shifted, b * 2 + (j + 1))
                    if at_least(b, 1):
                        act.wait_ge(k_turned, b * 2)
                    act.activation(k_exp[:, j, :].rearrange("p (h n) -> p h n", h=2), (PA, PB)[j][:, :, 0:HALF],
                                   ACT.Exp, bias=k_shift[:, j:j + 1], accum_out=k_sum[:, slot, j:j + 1]
                                   ).then_inc(used[(A, B_)[j]], 1)

                def ky_keep(b):
                    act.wait_ge(ky_done, b + 1)
                    if at_least(b, 1):
                        act.wait_ge(mix_done, b)
                    act.copy(ky[:, :], p_ky[:, :]).then_inc(ky_kept, 1)

                def q_exps(b, slot, part):
                    over(act, f"q{part}", b)
                    c, n = Q_PARTS[part]
                    q = q_sb[:, slot, c * S_HEADS:(c + n) * S_HEADS, :]
                    act.activation(q, q, ACT.Exp).then_inc(q_exped, 1)

                def q_keep(b, j):
                    act.wait_ge(q_turned, b * 2 + (j + 1))
                    if at_least(b, 1):
                        act.wait_ge(out_done, b)
                    act.copy(q_cols[:, j, 0:512], (PB, PC)[j][:, 0, :])
                    act.copy(q_cols[:, j, 512:T], (PB, PC)[j][:, 1, 0:T - 512]).then_inc(used[(B_, C)[j]], 1)

                def rounds(b, slot):
                    nxt, more = 1 - slot, before(b, B - 1)
                    if more:
                        round_y(b + 1, nxt)
                    k_keep(b, 0)
                    k_keep(b, 1)
                    if more:
                        k_exps(b + 1, nxt, 0)
                        k_exps(b + 1, nxt, 1)
                    ky_keep(b)
                    if more:
                        q_exps(b + 1, nxt, 0)
                        q_exps(b + 1, nxt, 1)
                    q_keep(b, 0)
                    q_keep(b, 1)
                round_y(0, 0)
                for j in range(2):
                    k_exps(0, 0, j)
                for part in range(2):
                    q_exps(0, 0, part)
                steps(act, B, 2, rounds)


def mixture(nc, g, w):
    HID = 512
    BLOCKS = HID // P
    SHARED = 2
    TOP = 2
    ALL = SHARED + E_N
    row_statistics(nc, g, "n3")
    with ExitStack() as ctx:
        def sb(name, shape, dt=F32):
            return ctx.enter_context(nc.sbuf_tensor(name, shape, dt))

        gates = nc.dram_tensor("e_gates", (P, T), F32, kind="Internal").ap()
        w1_hi = sb("e_w1_hi", [P, ALL * BLOCKS, P], F32R)
        w1_lo = sb("e_w1_lo", [P, ALL * BLOCKS, P], F32R)
        w2_hi = sb("e_w2_hi", [P, ALL * BLOCKS, P], F32R)
        w2_lo = sb("e_w2_lo", [P, ALL * BLOCKS, P], F32R)
        b1 = sb("e_b1", [P, 1, ALL * BLOCKS])
        b2 = sb("e_b2", [P, 1, E_N])
        shared_b2 = sb("e_sb2", [P, 1, SHARED])
        gate_bias = sb("e_gate_b", [P, E_N])
        with ExitStack() as inner:
            wg_hi = inner.enter_context(nc.sbuf_tensor("e_wg_hi", [P, 1, E_N], F32R))
            wg_lo = inner.enter_context(nc.sbuf_tensor("e_wg_lo", [P, 1, E_N], F32R))
            logits = inner.enter_context(nc.sbuf_tensor("e_logits", [P, TILES, B, E_N], F32))

            def ups(name, first, n):
                return [(w1_hi[:, (first + e) * BLOCKS:(first + e + 1) * BLOCKS, :],
                         w1_lo[:, (first + e) * BLOCKS:(first + e + 1) * BLOCKS, :],
                         w[name][e].rearrange("(j f) d -> f j d", f=P), True) for e in range(n)]

            def downs(name, first, n):
                return [(w2_hi[:, (first + e) * BLOCKS:(first + e + 1) * BLOCKS, :],
                         w2_lo[:, (first + e) * BLOCKS:(first + e + 1) * BLOCKS, :],
                         w[name][e].rearrange("d (j f) -> d j f", f=P), True) for e in range(n)]

            def bias_columns(name, first, n):
                return (b1[:, :, first * BLOCKS:(first + n) * BLOCKS], None,
                        w[name].rearrange("e (j o f) -> (e j) o f", o=1, f=P), True)

            split_weights(nc, g, [
                (wg_hi[:, :, :], wg_lo[:, :, :], w["L1_ffn_gate_w"].rearrange("e (o d) -> e o d", o=1), True),
                *ups("L1_ffn_sw1", 0, SHARED), *ups("L1_ffn_rw1", SHARED, E_N),
                *downs("L1_ffn_sw2", 0, SHARED), *downs("L1_ffn_rw2", SHARED, E_N),
                (b2[:, :, :], None, w["L1_ffn_rb2"].rearrange("e (o d) -> e o d", o=1), True),
                (shared_b2[:, :, :], None, w["L1_ffn_sb2"].rearrange("e (o d) -> e o d", o=1), True),
                bias_columns("L1_ffn_sb1", 0, SHARED), bias_columns("L1_ffn_rb1", SHARED, E_N)], "e")
            load_small(nc, [
                (gate_bias[:, :], w["L1_ffn_gate_b"].unsqueeze(0).broadcast_to([P, E_N]), None)], "e")
            with nc.Block() as block:
                @block.vector
                def _(dve):
                    dve.tensor_tensor(shared_b2[:, :, 0], shared_b2[:, :, 0], shared_b2[:, :, 1], ALU.add)
            router_logits(nc, g, wg_hi, wg_lo, gate_bias, logits, "e")
            route(nc, g, logits, gates, None, TOP, "e")
        gated_ffn(nc, g, w1_hi, w1_lo, b1, w2_hi, w2_lo, b2, shared_b2[:, 0, 0:1], BLOCKS, SHARED, gates, "e")


def store(nc, g, out):
    with nc.semaphore("stored") as stored, nc.Block() as block:
        @block.sync
        def _(sp):
            with sp.Fori(0, B) as b:
                sp.dma_start(out[bass.ds(b, 1), 0:(TILES - 1) * P, :].rearrange("o (c p) d -> (o p) c d", p=P),
                             g.h[:, bass.ds(b * TILES, TILES - 1), :]).then_inc(stored, 16)
                sp.dma_start(out[bass.ds(b, 1), (TILES - 1) * P:T, :].rearrange("o p d -> (o p) d"),
                             g.h[0:LAST, bass.ds(b * TILES + (TILES - 1), 1), :].rearrange("p o d -> p (o d)")
                             ).then_inc(stored, 16)
            sp.wait_ge(stored, 32 * B)


def audio_tower(nc, w, out):
    with ExitStack() as ctx:
        g = Shared()
        g.h = ctx.enter_context(nc.sbuf_tensor("h", [P, B * TILES, P], F32))
        g.mean = ctx.enter_context(nc.sbuf_tensor("mean", [P, B * TILES], F32))
        g.rstd = ctx.enter_context(nc.sbuf_tensor("rstd", [P, B * TILES], F32))
        constants(nc, ctx, g)
        quasi_recurrent(nc, g, w["x"], w["L0_tok_kernel"])
        cross_attention(nc, g, w)
        expert_choice(nc, g, w)
        slice_attention(nc, g, w)
        mixture(nc, g, w)
        store(nc, g, out)


_INS = ['x', 'L0_tok_kernel', 'L0_attn_q_w', 'L0_attn_kv_w', 'L0_ffn_Wg', 'L0_ffn_W1', 'L0_ffn_b1', 'L0_ffn_W2',
        'L0_ffn_b2', 'L1_attn_W_in', 'L1_attn_b_in', 'L1_attn_Wq', 'L1_attn_Wk', 'L1_attn_Wv', 'L1_attn_W_out',
        'L1_attn_b_out', 'L1_ffn_gate_w', 'L1_ffn_gate_b', 'L1_ffn_sw1', 'L1_ffn_sb1', 'L1_ffn_sw2', 'L1_ffn_sb2',
        'L1_ffn_rw1', 'L1_ffn_rb1', 'L1_ffn_rw2', 'L1_ffn_rb2']


def kernel(**inputs):
    import numpy as _np
    import concourse.bacc as _bacc
    from concourse import mybir as _mybir
    from concourse.bass_utils import run_bass_kernel_spmd as _run

    nc = _bacc.Bacc("TRN2", target_bir_lowering=False, num_devices=1)
    arrays, aps = {}, {}
    for name in _INS:
        a = _np.ascontiguousarray(inputs[name])
        arrays[f"in_{name}_dram"] = a
        aps[name] = nc.dram_tensor(f"in_{name}_dram", a.shape, _mybir.dt.from_np(a.dtype), kind="ExternalInput").ap()
    out = nc.dram_tensor("out_0_dram", (B, T, P), _mybir.dt.float32, kind="ExternalOutput").ap()
    audio_tower(nc, aps, out)
    r = _run(nc, [arrays], core_ids=[0])
    return r.results[0]["out_0_dram"]
```

```python
from contextlib import ExitStack

import concourse.bass as bass
from concourse import mybir

F32 = mybir.dt.float32
F32R = mybir.dt.float32r
ALU = mybir.AluOpType
ACT = mybir.ActivationFunctionType
AX = mybir.AxisListType

P = 128
B = 16
T_IN = 750
WINDOW = 3
T = T_IN - WINDOW + 1
HALF = T // 2
TILES = -(-T // P)
ROWS = [min(P, T - P * c) for c in range(TILES)]
LAST = ROWS[-1]
HALVES = [slice(0, HALF), slice(HALF, T)]
EPS = 1e-5


def steps(eng, n, peel, body):
    assert (n - 2 * peel) % 2 == 0
    for k in range(peel):
        body(k, k % 2)
    with eng.Fori(0, (n - 2 * peel) // 2) as i:
        for q in range(2):
            body(i * 2 + (peel + q), (peel + q) % 2)
    for k in range(n - peel, n):
        body(k, k % 2)


def at_least(k, low):
    return not isinstance(k, int) or k >= low


def before(k, high):
    return not isinstance(k, int) or k < high


def semaphores(nc, ctx, tag=""):
    made = []

    def clear():
        with nc.Block() as block:
            @block.sync
            def _(sp):
                for s in made:
                    sp.sem_clear(s)
        for s in made:
            nc.release_semaphore(s)

    def sem(name):
        made.append(nc.alloc_semaphore(f"{name}{tag}"))
        return made[-1]

    ctx.callback(clear)
    return sem


class Shared:
    pass

def steps3(eng, n, low, high, body):
    assert (n - low - high) % 3 == 0
    for k in range(low):
        body(k, k % 3)
    with eng.Fori(0, (n - low - high) // 3) as i:
        for q in range(3):
            body(i * 3 + (low + q), (low + q) % 3)
    for k in range(n - high, n):
        body(k, k % 3)


def normalize(pool, g, rows, b, centred, n):
    tiles = bass.ds(b * TILES, TILES)
    mean = g.mean[:, tiles].unsqueeze(2).broadcast_to([P, TILES, P])
    rstd = g.rstd[:, tiles].unsqueeze(2).broadcast_to([P, TILES, P])
    pool.tensor_tensor(rows, g.h[:, tiles, :], mean, ALU.subtract).then_inc(centred, 1)
    pool.wait_ge(centred, n)
    return pool.tensor_tensor(rows, rows, rstd, ALU.mult)


def take_statistics(dve, g, b, tiles):
    for c in tiles:
        at = bass.ds(b * TILES + c, 1)
        dve.bn_stats(g.stats[:, at, :].rearrange("p o s -> p (o s)"), g.h[:, at, :].rearrange("p o d -> p (o d)"))


def weights_and_statistics(nc, g, jobs, tag, taken):
    CHUNK, RING = 4, 4
    N = B * TILES
    pieces = []
    for hi, lo, view, turned in jobs:
        for k in range(0, view.shape[1], CHUNK):
            n = min(CHUNK, view.shape[1] - k)
            pieces.append((hi[:, k:k + n, :], None if lo is None else lo[:, k:k + n, :], view[:, k:k + n, :], turned))
    turns = [sum(p[3] for p in pieces[:j + 1]) for j in range(len(pieces))]
    with ExitStack() as ctx:
        sem = semaphores(nc, ctx, "_" + tag)

        def sb(name, shape):
            return ctx.enter_context(nc.sbuf_tensor(f"{name}_{tag}", shape, F32))
        raw = sb("raw", [P, RING, CHUNK, P])
        stats = g.stats
        diff, spread, std = sb("diff", [P, N]), sb("spread", [P, N]), sb("std", [P, N])
        eps = sb("eps", [P, 1])
        stats_done, sums_done, std_done = sem("stats_done"), sem("sums_done"), sem("std_done")
        turn = [ctx.enter_context(nc.psum_tensor(f"wturn{j}_{tag}", [P, CHUNK, P], F32)) for j in range(RING)]
        loaded = [sem(f"w_in{j}") for j in range(RING)]
        turned_n, hi_n, lo_n = sem("w_turned"), sem("w_hi"), sem("w_lo")

        def block_of(j):
            hi, lo, view, turned = pieces[j]
            rows, n, cols = view.shape
            return turn[j % RING][0:cols, 0:n, 0:rows] if turned else raw[0:rows, j % RING, 0:n, 0:cols]

        with nc.Block() as block:
            @block.sync
            def _(sp):
                for j, (hi, lo, view, turned) in enumerate(pieces):
                    rows, n, cols = view.shape
                    if j >= RING:
                        sp.wait_ge(lo_n, j - RING + 1)
                    sp.dma_start(raw[0:rows, j % RING, 0:n, 0:cols], view).then_inc(loaded[j % RING], 16)

            @block.tensor
            def _(pe):
                for j, (hi, lo, view, turned) in enumerate(pieces):
                    rows, n, cols = view.shape
                    if not turned:
                        continue
                    pe.wait_ge(loaded[j % RING], 16 * (j // RING + 1))
                    if j >= RING:
                        pe.wait_ge(lo_n, j - RING + 1)
                    for c in range(n):
                        last = pe.transpose(turn[j % RING][0:cols, c, 0:rows], raw[0:rows, j % RING, c, 0:cols],
                                            g.ident[0:rows, 0:rows])
                    last.then_inc(turned_n, 1)

            def wait_for(eng, j):
                if pieces[j][3]:
                    eng.wait_ge(turned_n, turns[j])
                else:
                    eng.wait_ge(loaded[j % RING], 16 * (j // RING + 1))

            @block.scalar
            def _(act):
                for j, (hi, lo, view, turned) in enumerate(pieces):
                    if lo is not None:
                        wait_for(act, j)
                        act.copy(hi, block_of(j)).then_inc(hi_n, 1)
                act.wait_ge(sums_done, 3)
                act.activation(std[:, :], spread[:, :], ACT.Sqrt, bias=eps[:, :], scale=1.0 / P
                               ).then_inc(std_done, 1)

            @block.vector
            def _(dve):
                dve.memset(eps[:, :], EPS)
                rounded = 0
                for j, (hi, lo, view, turned) in enumerate(pieces):
                    if lo is None:
                        wait_for(dve, j)
                        dve.tensor_copy(hi, block_of(j)).then_inc(lo_n, 1)
                    else:
                        rounded += 1
                        dve.wait_ge(hi_n, rounded)
                        dve.tensor_tensor(lo, block_of(j), hi.bitcast(F32), ALU.subtract).then_inc(lo_n, 1)
                    for t in [] if taken else range(N * j // len(pieces), N * (j + 1) // len(pieces)):
                        dve.bn_stats(stats[:, t, :], g.h[:, t, :]).then_inc(stats_done, 1)
                if not taken:
                    dve.wait_ge(stats_done, N)
                dve.tensor_tensor(diff[:, :], stats[:, :, 1], stats[:, :, 4], ALU.subtract)
                dve.tensor_tensor(g.mean[:, :], stats[:, :, 1], stats[:, :, 4], ALU.add)
                dve.tensor_tensor(spread[:, :], stats[:, :, 2], stats[:, :, 5], ALU.add).then_inc(sums_done, 1)
                dve.wait_ge(sums_done, 1)
                dve.tensor_scalar(g.mean[:, :], g.mean[:, :], 0.5, None, ALU.mult)
                dve.tensor_tensor(diff[:, :], diff[:, :], diff[:, :], ALU.mult).then_inc(sums_done, 1)
                dve.wait_ge(sums_done, 2)
                dve.scalar_tensor_tensor(out=spread[:, :], in0=diff[:, :], scalar=P / 4.0, in1=spread[:, :],
                                         op0=ALU.mult, op1=ALU.add).then_inc(sums_done, 1)
                dve.wait_ge(std_done, 1)
                dve.reciprocal(g.rstd[:, :], std[:, :])


def turn_tiles(pe, g, turn, rows):
    for c, n in enumerate(ROWS):
        last = pe.transpose(turn[:, c // 4, (c % 4) * P:(c % 4) * P + n], rows[0:n, c, :], g.ident[0:n, 0:n])
    return last


def round_cols(act, hi, turn):
    act.copy(hi[:, 0:512], turn[:, 0, :])
    return act.copy(hi[:, 512:T], turn[:, 1, 0:T - 512])


def split_cols(dve, lo, hi, turn):
    dve.tensor_tensor(lo[:, 0:512], turn[:, 0, :], hi[:, 0:512].bitcast(F32), ALU.subtract)
    return dve.tensor_tensor(lo[:, 512:T], turn[:, 1, 0:T - 512], hi[:, 512:T].bitcast(F32), ALU.subtract)


def constants(nc, ctx, g):
    g.ident = ctx.enter_context(nc.sbuf_tensor("ident", [P, P], F32))
    made = ctx.enter_context(nc.semaphore("ident_zeroed"))
    with nc.Block() as block:
        @block.gpsimd
        def _(pool):
            pool.memset(g.ident[:], 0.0).then_inc(made, 1)
            pool.wait_ge(made, 1)
            pool.affine_select(out=g.ident[:], in_=g.ident[:], compare_op=ALU.not_equal, fill=1.0, base=0,
                               pattern=[[-1, P]], channel_multiplier=1)

        @block.vector
        def _(dve):
            dve.memset(g.h[96:P, :, :].rearrange("p (b c) d -> p b c d", c=TILES)[:, :, TILES - 1, :], 0.0)


def quasi_recurrent(nc, g, x, w):
    GATES = 3
    with ExitStack() as ctx:
        def sb(name, shape, dt=F32):
            return ctx.enter_context(nc.sbuf_tensor(name, shape, dt))

        sem = semaphores(nc, ctx)

        x_rows = sb("x_rows", [P, 2, TILES, P])
        x_hi = sb("x_hi", [P, 2, T_IN], F32R)
        x_lo = sb("x_lo", [P, 2, T_IN], F32R)
        w_raw = sb("w_raw", [P, WINDOW, GATES * P])
        w_hi = sb("w_hi", [P, WINDOW, GATES * P], F32R)
        w_lo = sb("w_lo", [P, WINDOW, GATES * P], F32R)
        gates = sb("gates", [P, 2, GATES, T])
        fresh = sb("fresh", [P, 2, T])
        cell = sb("cell", [P, 2, T])
        hid = sb("hid", [P, 2, T])
        turn_in = ctx.enter_context(nc.psum_tensor("turn_in", [P, 2, 512], F32))
        conv = [ctx.enter_context(nc.psum_tensor(f"conv{k}", [P, 2, 512], F32)) for k in range(2)]
        turn_out = ctx.enter_context(nc.psum_tensor("turn_out", [P, 2, 512], F32))
        x_loaded = [sem("x_loaded0"), sem("x_loaded1")]
        w_loaded, w_rounded, w_split = sem("w_loaded"), sem("w_rounded"), sem("w_split")
        x_turned, x_rounded, x_split = sem("x_turned"), sem("x_rounded"), sem("x_split")
        conv_done, gate_done = sem("conv_done"), sem("gate_done")
        fresh_done, cell_done, hid_done = sem("fresh_done"), sem("cell_done"), sem("hid_done")
        h_turned, h_kept = sem("h_turned"), sem("h_kept")
        full_in = T_IN // P
        rows_in = [min(P, T_IN - P * c) for c in range(full_in + 1)]

        with nc.Block() as block:
            @block.sync
            def _(sp):
                sp.dma_start(w_raw[:, :, :], w.rearrange("k d n -> d k n")).then_inc(w_loaded, 16)

                def load(b, slot):
                    if at_least(b, 2):
                        sp.wait_ge(x_turned, b - 1)
                    sp.dma_start(x_rows[:, slot, 0:full_in, :],
                                 x[bass.ds(b, 1), 0:full_in * P, :].rearrange("o (c p) d -> (o p) c d", p=P)
                                 ).then_inc(x_loaded[slot], 16)
                    sp.dma_start(x_rows[0:rows_in[-1], slot, full_in, :],
                                 x[bass.ds(b, 1), full_in * P:T_IN, :].rearrange("o p d -> (o p) d")
                                 ).then_inc(x_loaded[slot], 16)
                steps(sp, B, 2, load)

            @block.tensor
            def _(pe):
                def turn(b, slot):
                    half = b // 2 if isinstance(b, int) else None
                    pe.wait_ge(x_loaded[slot], 32 * (half + 1) if half is not None else (b - slot) * 16 + 32)
                    if at_least(b, 1):
                        pe.wait_ge(x_split, b)
                    for c, n in enumerate(rows_in):
                        last = pe.transpose(turn_in[:, c // 4, (c % 4) * P:(c % 4) * P + n], x_rows[0:n, slot, c, :],
                                            g.ident[0:n, 0:n])
                    last.then_inc(x_turned, 1)

                def convolve(b, slot):
                    pe.wait_ge(x_split, b + 1)
                    for gate in range(GATES):
                        if at_least(b, 1) or gate == 2:
                            pe.wait_ge(gate_done, b * GATES + (0, -1, 1)[gate])
                        out = conv[gate % 2]
                        for h, cols in enumerate(HALVES):
                            for k in range(WINDOW):
                                for j, (a, m) in enumerate([(w_hi, x_hi), (w_hi, x_lo), (w_lo, x_hi)]):
                                    last = pe.matmul(out[:, h, 0:HALF], a[:, k, gate * P:(gate + 1) * P],
                                                     m[:, slot, cols.start + k:cols.stop + k],
                                                     start=(k == 0 and j == 0), stop=(k == WINDOW - 1 and j == 2))
                        last.then_inc(conv_done, 1)

                def turn_back(b, slot):
                    pe.wait_ge(hid_done, b + 1)
                    if at_least(b, 1):
                        pe.wait_ge(h_kept, b)
                    for c, n in enumerate(ROWS):
                        last = pe.transpose(turn_out[0:n, c // 4, (c % 4) * P:(c % 4) * P + P],
                                            hid[:, slot, c * P:c * P + n], g.ident[:, :])
                    last.then_inc(h_turned, 1)

                def step(b, slot):
                    if before(b, B - 1):
                        turn(b + 1, 1 - slot)
                    convolve(b, slot)
                    if at_least(b, 1):
                        turn_back(b - 1, 1 - slot)

                pe.wait_ge(w_split, 1)
                turn(0, 0)
                steps(pe, B, 2, step)
                turn_back(B - 1, (B - 1) % 2)

            @block.scalar
            def _(act):
                act.wait_ge(w_loaded, 16)
                act.copy(w_hi[:, :, :], w_raw[:, :, :]).then_inc(w_rounded, 1)

                def round_x(b, slot):
                    act.wait_ge(x_turned, b + 1)
                    if at_least(b, 2):
                        act.wait_ge(conv_done, b * GATES - GATES)
                    act.copy(x_hi[:, slot, 0:512], turn_in[:, 0, :]).then_inc(x_rounded, 1)
                    act.copy(x_hi[:, slot, 512:T_IN], turn_in[:, 1, 0:T_IN - 512]).then_inc(x_rounded, 1)

                def open_gates(b, slot):
                    for gate, func in enumerate([ACT.Tanh, ACT.Sigmoid, ACT.Sigmoid]):
                        act.wait_ge(conv_done, b * GATES + (gate + 1))
                        if at_least(b, 2) and gate == 0:
                            act.wait_ge(hid_done, b - 1)
                        act.activation(gates[:, slot, gate, :].rearrange("p (h n) -> p h n", h=2),
                                       conv[gate % 2][:, :, 0:HALF], func).then_inc(gate_done, 1)

                def keep(b, slot):
                    act.wait_ge(h_turned, b + 1)
                    act.copy(g.h[:, bass.ds(b * TILES, 4), :], turn_out[:, 0, :].rearrange("p (c d) -> p c d", c=4))
                    act.copy(g.h[:, bass.ds(b * TILES + 4, 1), :], turn_out[:, 1:2, 0:P])
                    act.copy(g.h[0:LAST, bass.ds(b * TILES + 5, 1), :], turn_out[0:LAST, 1:2, P:2 * P]
                             ).then_inc(h_kept, 1)

                def step(b, slot):
                    if before(b, B - 1):
                        round_x(b + 1, 1 - slot)
                    open_gates(b, slot)
                    if at_least(b, 1):
                        keep(b - 1, 1 - slot)
                round_x(0, 0)
                steps(act, B, 2, step)
                keep(B - 1, (B - 1) % 2)

            @block.vector
            def _(dve):
                dve.wait_ge(w_rounded, 1)
                dve.tensor_tensor(w_lo[:, :, :], w_raw[:, :, :], w_hi[:, :, :].bitcast(F32), ALU.subtract
                                  ).then_inc(w_split, 1)

                def split_x(b, slot):
                    dve.wait_ge(x_rounded, b * 2 + 2)
                    if at_least(b, 2):
                        dve.wait_ge(conv_done, b * GATES - GATES)
                    dve.tensor_tensor(x_lo[:, slot, 0:512], turn_in[:, 0, :], x_hi[:, slot, 0:512].bitcast(F32),
                                      ALU.subtract)
                    dve.tensor_tensor(x_lo[:, slot, 512:T_IN], turn_in[:, 1, 0:T_IN - 512],
                                      x_hi[:, slot, 512:T_IN].bitcast(F32), ALU.subtract).then_inc(x_split, 1)

                def recur(b, slot):
                    dve.wait_ge(gate_done, b * GATES + 2)
                    dve.scalar_tensor_tensor(out=fresh[:, slot, :], in0=gates[:, slot, 1, :], scalar=1.0,
                                             in1=gates[:, slot, 0, :], op0=ALU.subtract, op1=ALU.mult
                                             ).then_inc(fresh_done, 1)
                    dve.wait_ge(fresh_done, b + 1)
                    dve.tensor_tensor_scan(cell[:, slot, :], gates[:, slot, 1, :], fresh[:, slot, :], 0.0,
                                           ALU.mult, ALU.subtract).then_inc(cell_done, 1)
                    dve.wait_ge(cell_done, b + 1)
                    dve.wait_ge(gate_done, b * GATES + 3)
                    if at_least(b, 2):
                        dve.wait_ge(h_turned, b - 1)
                    dve.tensor_tensor(hid[:, slot, :], gates[:, slot, 2, :], cell[:, slot, :], ALU.mult
                                      ).then_inc(hid_done, 1)

                def step(b, slot):
                    if before(b, B - 1):
                        split_x(b + 1, 1 - slot)
                    recur(b, slot)
                    if at_least(b, 1):
                        dve.wait_ge(h_kept, b)
                        take_statistics(dve, g, b - 1, range(TILES))
                split_x(0, 0)
                steps(dve, B, 2, step)
                dve.wait_ge(h_kept, B)
                take_statistics(dve, g, B - 1, range(TILES))


HEADS = 8
DH = P // HEADS
GROUPS = 2
GH = HEADS // GROUPS
UNITS = B * GROUPS
VCOLS = DH + 1
LANE = 32


def attention_inputs(nc, g, w, q_parts, k_parts, v_rows):
    SCALE = float(P) ** -0.5
    with ExitStack() as ctx:
        def sb(name, shape, dt=F32):
            return ctx.enter_context(nc.sbuf_tensor(name, shape, dt))

        sem = semaphores(nc, ctx)

        w_hi = sb("qkv_hi", [P, 3, P], F32R)
        w_lo = sb("qkv_lo", [P, 3, P], F32R)
        weights_and_statistics(nc, g, [
            (w_hi[:, 0:1, :], w_lo[:, 0:1, :], w["L0_attn_q_w"].rearrange("o (i k) -> o i k", i=1), True),
            (w_hi[:, 1:3, :], w_lo[:, 1:3, :], w["L0_attn_kv_w"].rearrange("(j o) k -> o j k", j=2), True)],
            "qkv", True)
        rows = sb("y_rows", [P, 2, TILES, P])
        y_hi = sb("y_hi", [P, 2, T], F32R)
        y_lo = sb("y_lo", [P, 2, T], F32R)
        out_hi = [sb(f"{s}_hi", [P, 2, T], F32R) for s in "qk"]
        out_lo = [sb(f"{s}_lo", [P, 2, T], F32R) for s in "qk"]
        v_out = sb("v_out", [P, 2, GROUPS, TILES, GH, VCOLS])
        turn = ctx.enter_context(nc.psum_tensor("y_turn", [P, 2, 512], F32))
        proj = [ctx.enter_context(nc.psum_tensor(f"{s}_proj", [P, 2, 512], F32)) for s in "qk"]
        v_proj = ctx.enter_context(nc.psum_tensor("v_proj", [P, 2, 512], F32))
        centred, ready, turned = sem("centred"), sem("y_ready"), sem("y_turned")
        rounded, split = sem("y_rounded"), sem("y_split")
        done, v_done = [sem("q_done"), sem("k_done")], sem("v_done")
        hi_done, lo_done, v_kept = [sem("q_hi_done"), sem("k_hi_done")], [sem("q_lo_done"), sem("k_lo_done")], sem("v_kept")
        stored, ones_set = [sem("qkv_stored0"), sem("qkv_stored1")], sem("ones_set")
        STORES = 5

        with nc.Block() as block:
            @block.gpsimd
            def _(pool):
                pool.memset(v_out[:, :, :, :, :, :], 1.0).then_inc(ones_set, 1)

                def norm(b, slot):
                    if at_least(b, 2):
                        pool.wait_ge(turned, b - 1)
                    normalize(pool, g, rows[:, slot, :, :], b, centred, b + 1).then_inc(ready, 1)
                steps(pool, B, 2, norm)

            @block.tensor
            def _(pe):
                def turn_rows(b, slot):
                    pe.wait_ge(ready, b + 1)
                    if at_least(b, 1):
                        pe.wait_ge(split, b)
                    for c, n in enumerate(ROWS):
                        last = pe.transpose(turn[:, c // 4, (c % 4) * P:(c % 4) * P + n], rows[0:n, slot, c, :],
                                            g.ident[0:n, 0:n])
                    last.then_inc(turned, 1)

                def project(b, slot):
                    pe.wait_ge(split, b + 1)
                    for j in range(2):
                        if at_least(b, 1):
                            pe.wait_ge(lo_done[j], b)
                        for h, cols in enumerate(HALVES):
                            for k, (a, m) in enumerate([(w_hi, y_hi), (w_hi, y_lo), (w_lo, y_hi)]):
                                last = pe.matmul(proj[j][:, h, 0:HALF], a[:, j, :], m[:, slot, cols],
                                                 start=(k == 0), stop=(k == 2))
                        last.then_inc(done[j], 1)
                    if at_least(b, 1):
                        pe.wait_ge(v_kept, b)
                    for c, n in enumerate(ROWS):
                        for k, (a, m) in enumerate([(y_hi, w_hi), (y_hi, w_lo), (y_lo, w_hi)]):
                            last = pe.matmul(v_proj[0:n, c // 4, (c % 4) * P:(c % 4 + 1) * P],
                                             a[:, slot, c * P:c * P + n], m[:, 2, :], start=(k == 0), stop=(k == 2))
                    last.then_inc(v_done, 1)

                def step(b, slot):
                    if before(b, B - 1):
                        turn_rows(b + 1, 1 - slot)
                    project(b, slot)
                turn_rows(0, 0)
                steps(pe, B, 2, step)

            @block.scalar
            def _(act):
                def round_y(b, slot):
                    act.wait_ge(turned, b + 1)
                    if at_least(b, 2):
                        act.wait_ge(v_done, b - 1)
                    act.copy(y_hi[:, slot, 0:512], turn[:, 0, :])
                    act.copy(y_hi[:, slot, 512:T], turn[:, 1, 0:T - 512]).then_inc(rounded, 1)

                def keep(b, slot):
                    if at_least(b, 2):
                        act.wait_ge(stored[slot], (b - slot) * (8 * STORES))
                    for j in range(2):
                        act.wait_ge(done[j], b + 1)
                        act.mul(out_hi[j][:, slot, :].rearrange("p (h n) -> p h n", h=2), proj[j][:, :, 0:HALF],
                                SCALE if j == 0 else 1.0).then_inc(hi_done[j], 1)
                    act.wait_ge(v_done, b + 1)
                    if not at_least(b, 1):
                        act.wait_ge(ones_set, 1)
                    for c, n in enumerate(ROWS):
                        last = act.copy(v_out[0:n, slot, :, c, :, 0:DH],
                                        v_proj[0:n, c // 4, (c % 4) * P:(c % 4 + 1) * P]
                                        .rearrange("p (a k d) -> p a k d", a=GROUPS, k=GH))
                    last.then_inc(v_kept, 1)

                def step(b, slot):
                    if before(b, B - 1):
                        round_y(b + 1, 1 - slot)
                    keep(b, slot)
                round_y(0, 0)
                steps(act, B, 2, step)

            @block.vector
            def _(dve):
                def split_y(b, slot):
                    dve.wait_ge(rounded, b + 1)
                    dve.tensor_tensor(y_lo[:, slot, 0:512], turn[:, 0, :], y_hi[:, slot, 0:512].bitcast(F32),
                                      ALU.subtract)
                    dve.tensor_tensor(y_lo[:, slot, 512:T], turn[:, 1, 0:T - 512],
                                      y_hi[:, slot, 512:T].bitcast(F32), ALU.subtract).then_inc(split, 1)

                def low(b, slot):
                    for j in range(2):
                        dve.wait_ge(hi_done[j], b + 1)
                        dve.scalar_tensor_tensor(
                            out=out_lo[j][:, slot, :].rearrange("p (h n) -> p h n", h=2), in0=proj[j][:, :, 0:HALF],
                            scalar=SCALE if j == 0 else 1.0,
                            in1=out_hi[j][:, slot, :].bitcast(F32).rearrange("p (h n) -> p h n", h=2),
                            op0=ALU.mult, op1=ALU.subtract).then_inc(lo_done[j], 1)

                def step(b, slot):
                    if before(b, B - 1):
                        split_y(b + 1, 1 - slot)
                    low(b, slot)
                split_y(0, 0)
                steps(dve, B, 2, step)

            @block.sync
            def _(sp):
                def save(b, slot):
                    asker = (b + B // 2) % B
                    for j, (dram, batch) in enumerate([(q_parts, b), (k_parts, asker)]):
                        sp.wait_ge(lo_done[j], b + 1)
                        for part, src in enumerate([out_hi[j], out_lo[j]]):
                            sp.dma_start(dram[part, bass.ds(batch * P, P), :], src[:, slot, :].bitcast(F32)
                                         ).then_inc(stored[slot], 16)
                    sp.wait_ge(v_kept, b + 1)
                    sp.dma_start(v_rows[bass.ds(asker * GROUPS, GROUPS), :, :].rearrange("g p n -> p g n"),
                                 v_out[:, slot, :, :, :, :].rearrange("p g c k d -> p g (c k d)")
                                 ).then_inc(stored[slot], 16)
                steps(sp, B, 2, save)
                for slot in range(2):
                    sp.wait_ge(stored[slot], 16 * STORES * (B // 2))


def cross_attention(nc, g, w):
    with ExitStack() as ctx:
        q_parts = nc.dram_tensor("q_parts", (2, UNITS * GH * DH, T), F32, kind="Internal").ap()
        k_parts = nc.dram_tensor("k_parts", (2, UNITS * GH * DH, T), F32, kind="Internal").ap()
        v_rows = nc.dram_tensor("v_rows", (UNITS, P, TILES * GH * VCOLS), F32, kind="Internal").ap()
        attention_inputs(nc, g, w, q_parts, k_parts, v_rows)

        def sb(name, shape, dt=F32):
            return ctx.enter_context(nc.sbuf_tensor(name, shape, dt))

        sem = semaphores(nc, ctx)

        SLOTS = 3
        PAD = TILES * P
        PARTS_ROWS = 4 * DH
        MAX_ROW = P - 1
        STEPS = 2 * (TILES // 2)
        MAXES = GH * TILES * 2
        SHARE = MAXES // STEPS
        RING = 3
        q_stack = [sb(f"q_stack{k}", [P, GH, PAD], F32R) for k in range(SLOTS)]
        k_stack = [sb(f"k_stack{k}", [P, GH, PAD], F32R) for k in range(SLOTS)]
        v_sb = [sb(f"v_sb{k}", [P, TILES, GH, VCOLS]) for k in range(SLOTS)]
        probs = sb("probs", [P, 2, GH, 2, HALF])
        part_max = sb("part_max", [P, GH, TILES, 2])
        neg_max = sb("neg_max", [P, GH * TILES])
        max_rows = sb("max_rows", [GH * TILES, P], F32R)
        o_cols = sb("o_cols", [P, T])
        ones = sb("ones", [1, GH, T])
        inv = sb("inv", [P, TILES, GH])
        o_rows = sb("o_rows", [P, TILES, GH, DH])
        score = [ctx.enter_context(nc.psum_tensor(f"score{k}", [P, 2, 512], F32)) for k in range(2)]
        ring = [ctx.enter_context(nc.psum_tensor(f"to_dve{k}", [P, 512], F32)) for k in range(RING)]
        o_sum = ctx.enter_context(nc.psum_tensor("o_sum", [P, 512], F32))
        qk_loaded = [sem(f"qk_loaded{k}") for k in range(SLOTS)]
        v_loaded = [sem(f"v_loaded{k}") for k in range(SLOTS)]
        ones_placed = [sem(f"ones_placed{k}") for k in range(SLOTS)]
        row_loaded, padded, q_padded, ones_made, zeroed = (
            sem("row_loaded"), sem("padded"), sem("q_padded"), sem("ones_made"), sem("zeroed"))
        filled, used = sem("ring_filled"), sem("ring_used")
        negated, rows_ready = sem("negated"), sem("rows_ready")
        score_done, prob_done, pv_done = sem("score_done"), sem("prob_done"), sem("pv_done")
        o_copied, inverted, scaled, added = sem("o_copied"), sem("inverted"), sem("scaled"), sem("added")
        QK_LOADS = 8
        PARTS = [(0, 4), (4, 2)]

        def plan(u):
            def probes(ahead, k):
                if not before(u, UNITS - ahead):
                    return []
                return [("probe", ahead, i) for i in range(k * SHARE, (k + 1) * SHARE)]
            out = []
            for s in range(STEPS):
                items = probes(1, s + 1) if s < STEPS - 1 else probes(2, 0)
                if s in (2, 3) and at_least(u, 1):
                    items.append(("out", -1, s - 2))
                if s == STEPS - 1 and before(u, UNITS - 1):
                    items.insert(min(len(items), 2), ("max", 1, 0))
                out.append(items)
            return out
        opening = [("probe", 0, i) for i in range(MAXES)] + [("max", 0, 0)] + [("probe", 1, i) for i in range(SHARE)]
        closing = [("out", 0, part) for part in range(2)]
        PER_UNIT = MAXES + 3
        firsts = [len(opening)]
        for u in range(UNITS):
            firsts.append(firsts[-1] + sum(len(items) for items in plan(u)))
        assert PER_UNIT % RING == 0 and all(firsts[u] == firsts[1] + (u - 1) * PER_UNIT for u in range(1, UNITS - 1))

        def number(u, s, k):
            at = sum(len(items) for items in plan(u)[:s]) + k
            if isinstance(u, int):
                return firsts[u] + at, (firsts[u] + at) % RING
            at += firsts[1] - PER_UNIT
            return u * PER_UNIT + at, at % RING

        with nc.Block() as block:
            @block.gpsimd
            def _(pool):
                pool.memset(ones[:, :, :], 1.0).then_inc(ones_made, 1)
                pool.wait_ge(ones_made, 1)
                for k in range(SLOTS):
                    pool.memset(k_stack[k][0:PARTS_ROWS, :, T:PAD].bitcast(F32), 0.0).then_inc(padded, 1)
                    pool.wait_ge(padded, 2 * k + 1)
                    pool.memset(k_stack[k][PARTS_ROWS:P, :, :].bitcast(F32), 0.0).then_inc(padded, 1)
                    pool.wait_ge(padded, 2 * k + 2)

                def add(u, part):
                    pool.wait_ge(scaled, u * 3 + (1, 3)[part])
                    first, count = PARTS[part]
                    for c0, n, rows in [(0, 4, P)] if part == 0 else [(4, 1, P), (5, 1, LAST)]:
                        h = g.h[0:rows, bass.ds((u // GROUPS) * TILES + c0, n), :].rearrange(
                            "p c (d k) -> p c k d", k=HEADS)[:, :, bass.ds((u % GROUPS) * GH, GH), :]
                        last = pool.tensor_tensor(h, h, o_rows[0:rows, c0:c0 + n, :, :], ALU.add)
                    last.then_inc(added, 1)
                with pool.Fori(0, UNITS) as u:
                    add(u, 0)
                    add(u, 1)

            @block.sync
            def _(sp):
                def load_qk(u, slot):
                    if at_least(u, SLOTS):
                        sp.wait_ge(score_done, u * (STEPS * GH) - (SLOTS - 1) * STEPS * GH)
                    for stack, dram, parts in [(q_stack, q_parts, (0, 1, 0, 1)), (k_stack, k_parts, (0, 1, 1, 0))]:
                        for r, part in enumerate(parts):
                            sp.dma_start(stack[slot][r * DH:(r + 1) * DH, :, 0:T].bitcast(F32),
                                         dram[part, bass.ds(u * (GH * DH), GH * DH), :].rearrange("(k d) n -> d k n", k=GH)
                                         ).then_inc(qk_loaded[slot], 16)

                def load_v(u, slot):
                    if at_least(u, SLOTS):
                        sp.wait_ge(pv_done, u * STEPS - (SLOTS - 1) * STEPS)
                    sp.dma_start(v_sb[slot][:, :, :, :].rearrange("p c k d -> p (c k d)"),
                                 v_rows[bass.ds(u, 1), :, :].rearrange("o p n -> (o p) n")).then_inc(v_loaded[slot], 16)

                def place_row(u, slot):
                    sp.wait_ge(rows_ready, u + 1)
                    sp.dma_start(q_stack[slot][MAX_ROW:P, :, :].bitcast(F32).rearrange("o k (c p) -> o (k c) p", p=P),
                                 max_rows[:, :].bitcast(F32)).then_inc(row_loaded, 16)

                def step(u, slot):
                    if before(u, UNITS - 2):
                        load_qk(u + 2, (slot + 2) % SLOTS)
                        load_v(u + 2, (slot + 2) % SLOTS)
                    if before(u, UNITS - 1):
                        place_row(u + 1, (slot + 1) % SLOTS)
                for k in range(SLOTS):
                    sp.wait_ge(padded, 2 * k + 2)
                    sp.dma_start(k_stack[k][MAX_ROW:P, :, 0:T].bitcast(F32), ones[:, :, :]).then_inc(ones_placed[k], 16)
                    sp.wait_ge(q_padded, k + 1)
                    if k < 2:
                        load_qk(k, k)
                        load_v(k, k)
                place_row(0, 0)
                steps3(sp, UNITS, 2, 3, step)

            @block.tensor
            def _(pe):
                def await_qk(u, slot):
                    if isinstance(u, int):
                        pe.wait_ge(qk_loaded[slot], 16 * QK_LOADS * (u // SLOTS + 1))
                    else:
                        pe.wait_ge(qk_loaded[slot], (u // SLOTS) * (16 * QK_LOADS) + 16 * QK_LOADS)

                def hand_over(u, slot, item, at, bank):
                    kind, ahead, i = item
                    unit, its_slot = u + ahead, (slot + ahead) % SLOTS
                    if kind == "probe" and i == 0:
                        await_qk(unit, its_slot)
                        if isinstance(unit, int) and unit < SLOTS:
                            pe.wait_ge(ones_placed[its_slot], 16)
                    if kind == "max":
                        pe.wait_ge(negated, unit + 1)
                    if kind == "out" and i == 0:
                        pe.wait_ge(o_copied, unit * 2 + 2)
                    if at_least(at, RING):
                        pe.wait_ge(used, at - (RING - 1))
                    if kind == "probe":
                        head, c, half = i // (2 * TILES), (i // 2) % TILES, i % 2
                        last = pe.matmul(ring[bank][0:ROWS[c], 0:HALF],
                                         q_stack[its_slot][0:MAX_ROW, head, c * P:c * P + ROWS[c]],
                                         k_stack[its_slot][0:MAX_ROW, head, HALVES[half]], start=True, stop=True)
                    elif kind == "max":
                        last = pe.transpose(ring[bank][0:GH * TILES, 0:P], neg_max[:, :], g.ident[:, :])
                    else:
                        first, n = PARTS[i]
                        for c in range(first, first + n):
                            last = pe.transpose(ring[bank][0:ROWS[c], (c - first) * P:(c - first + 1) * P],
                                                o_cols[:, c * P:c * P + ROWS[c]], g.ident[:, :])
                    last.then_inc(filled, 1)

                def score_one(u, slot, s, head):
                    e = s * GH + head
                    half, pair = divmod(s, TILES // 2)
                    if at_least(u, 1) or e >= 2:
                        pe.wait_ge(prob_done, u * (STEPS * GH) + (e - 1))
                    for m in range(2):
                        c = 2 * pair + m
                        last = pe.matmul(score[e % 2][:, m, 0:HALF], k_stack[slot][:, head, c * P:(c + 1) * P],
                                         q_stack[slot][:, head, HALVES[half]], start=True, stop=True)
                    last.then_inc(score_done, 1)

                def sum_one(u, slot, s, m):
                    half, pair = divmod(s, TILES // 2)
                    c = 2 * pair + m
                    if s == 0 and m == 0:
                        pe.wait_ge(v_loaded[slot], 16 * (u // SLOTS + 1) if isinstance(u, int) else
                                   (u // SLOTS) * 16 + 16)
                    if m == 0:
                        pe.wait_ge(prob_done, u * (STEPS * GH) + (s + 1) * GH)
                        if pair == 0 and (at_least(u, 1) or half):
                            pe.wait_ge(o_copied, u * 2 + half)
                    for head in range(GH):
                        last = pe.matmul(o_sum[head * LANE:head * LANE + VCOLS, 0:HALF],
                                         v_sb[slot][0:ROWS[c], c, head, :], probs[0:ROWS[c], s % 2, head, m, :],
                                         start=(c == 0), stop=(c == TILES - 1))
                    if m == 1:
                        last.then_inc(pv_done, 1)

                def step(u, slot):
                    pe.wait_ge(row_loaded, u * 16 + 16)
                    items = plan(u)
                    for s in range(STEPS):
                        todo = [(item, *number(u, s, k)) for k, item in enumerate(items[s])]

                        def some(share):
                            for item, at, bank in todo[:share]:
                                hand_over(u, slot, item, at, bank)
                            del todo[:share]

                        def sums(m):
                            if s:
                                sum_one(u, slot, s - 1, m)
                            elif at_least(u, 1):
                                sum_one(u - 1, (slot + 2) % SLOTS, STEPS - 1, m)
                        score_one(u, slot, s, 0)
                        some(2)
                        score_one(u, slot, s, 1)
                        some(1)
                        sums(0)
                        some(2)
                        score_one(u, slot, s, 2)
                        some(1)
                        score_one(u, slot, s, 3)
                        some(1)
                        sums(1)
                        some(len(todo))

                pe.wait_ge(zeroed, 2)
                for k, item in enumerate(opening):
                    hand_over(0, 0, item, k, k % RING)
                steps3(pe, UNITS, 2, 3, step)
                for m in range(2):
                    sum_one(UNITS - 1, (UNITS - 1) % SLOTS, STEPS - 1, m)
                for k, item in enumerate(closing):
                    hand_over(UNITS - 1, 0, item, firsts[UNITS] + k, (firsts[UNITS] + k) % RING)

            @block.vector
            def _(dve):
                def take(u, item, at, bank):
                    kind, ahead, i = item
                    unit = u + ahead
                    dve.wait_ge(filled, at + 1)
                    if kind == "probe":
                        head, c, half = i // (2 * TILES), (i // 2) % TILES, i % 2
                        if i == 0 and at_least(unit, 1):
                            dve.wait_ge(negated, unit)
                        dve.tensor_reduce(part_max[0:ROWS[c], head, c, half:half + 1], ring[bank][0:ROWS[c], 0:HALF],
                                          AX.X, ALU.max).then_inc(used, 1)
                        if i == MAXES - 1:
                            dve.wait_ge(used, at + 1)
                            dve.tensor_reduce(neg_max[:, :], part_max[:, :, :, :].rearrange("p k c h -> p (k c) h"),
                                              AX.X, ALU.max, negate=True).then_inc(negated, 1)
                    elif kind == "max":
                        if at_least(unit, 1):
                            dve.wait_ge(row_loaded, unit * 16)
                        dve.tensor_copy(max_rows[:, :], ring[bank][0:GH * TILES, 0:P]).then_inc(rows_ready, 1)
                        dve.wait_ge(rows_ready, unit + 1)
                        dve.sem_inc(used, 1)
                    else:
                        for j, (c0, n, rows) in enumerate([(0, 4, P)] if i == 0 else [(4, 1, P), (5, 1, LAST)]):
                            first = PARTS[i][0]
                            o = ring[bank][0:rows, (c0 - first) * P:(c0 - first + n) * P].rearrange(
                                "p (c k e) -> p c k e", k=GH, e=LANE)
                            dve.reciprocal(inv[0:rows, c0:c0 + n, :], o[:, :, :, DH]).then_inc(inverted, 1)
                            dve.wait_ge(inverted, unit * 3 + (i + j + 1))
                            if at_least(unit, 1) and j == 0:
                                dve.wait_ge(added, unit * 2 + (i - 1))
                            dve.tensor_tensor(o_rows[0:rows, c0:c0 + n, :, :], o[:, :, :, 0:DH],
                                              inv[0:rows, c0:c0 + n, :].unsqueeze(3).broadcast_to([rows, n, GH, DH]),
                                              ALU.mult).then_inc(scaled, 1)
                        dve.wait_ge(scaled, unit * 3 + (1, 3)[i])
                        dve.sem_inc(used, 1)

                def step(u, slot):
                    for s, items in enumerate(plan(u)):
                        for k, item in enumerate(items):
                            take(u, item, *number(u, s, k))

                for k in range(SLOTS):
                    dve.memset(q_stack[k][PARTS_ROWS:P, :, :].bitcast(F32), 0.0).then_inc(q_padded, 1)
                dve.memset(part_max[:, :, :, :], 0.0).then_inc(zeroed, 1)
                dve.memset(o_sum[:, :], 0.0).then_inc(zeroed, 1)
                dve.wait_ge(zeroed, 2)
                for k, item in enumerate(opening):
                    take(0, item, k, k % RING)
                steps3(dve, UNITS, 2, 3, step)
                for k, item in enumerate(closing):
                    take(UNITS - 1, item, firsts[UNITS] + k, (firsts[UNITS] + k) % RING)

            @block.scalar
            def _(act):
                def copy_o(u, half):
                    act.wait_ge(pv_done, u * STEPS + (half + 1) * (STEPS // 2))
                    if half == 0 and at_least(u, 1):
                        act.wait_ge(filled, number(u, 3, len(plan(u)[3]) - 1)[0] + 1)
                    act.copy(o_cols[:, HALVES[half]], o_sum[:, 0:HALF]).then_inc(o_copied, 1)

                def step(u, slot):
                    for s in range(STEPS):
                        for head in range(GH):
                            e = s * GH + head
                            act.wait_ge(score_done, u * (STEPS * GH) + (e + 1))
                            if at_least(u, 1) or s >= 2:
                                act.wait_ge(pv_done, u * STEPS + (s - 1))
                            act.activation(probs[:, s % 2, head, :, :], score[e % 2][:, :, 0:HALF], ACT.Exp
                                           ).then_inc(prob_done, 1)
                            if head == 0 and s == 1 and at_least(u, 1):
                                copy_o(u - 1, 1)
                            if head == 0 and s == 4:
                                copy_o(u, 0)
                steps3(act, UNITS, 2, 3, step)
                copy_o(UNITS - 1, 1)


E_N = 8
AT = P - E_N
WIDE = AT + P


def router_logits(nc, g, wg_hi, wg_lo, bias, logits, tag):
    with ExitStack() as ctx:
        def sb(name, shape, dt=F32):
            return ctx.enter_context(nc.sbuf_tensor(f"{name}_{tag}", shape, dt))

        def ps(name, shape):
            return ctx.enter_context(nc.psum_tensor(f"{name}_{tag}", shape, F32))

        sem = semaphores(nc, ctx, "_" + tag)

        rows = sb("r_rows", [P, 2, TILES, P])
        y_hi = sb("r_hi", [P, 2, T], F32R)
        y_lo = sb("r_lo", [P, 2, T], F32R)
        kept = sb("r_kept", [P, T])
        turn = [ps(f"r_turn{k}", [P, 2, 512]) for k in range(2)]
        sums = ps("r_sums", [P, 2, 512])
        back = ps("r_back", [P, 2, 4, P])
        OWN = 4
        centred, pool_ready = sem("r_centred"), sem("r_pool_ready")
        cleared, ready, turned, rounded, split, done, sums_kept, sums_turned = (
            sem("r_" + s) for s in ("cleared", "ready", "turned", "rounded", "split", "done", "sums_kept",
                                    "sums_turned"))
        with nc.Block() as block:
            @block.gpsimd
            def _(pool):
                for part in (wg_hi, wg_lo):
                    for around in (part[:, 0, 0:AT], part[:, 0, AT + E_N:WIDE]):
                        pool.memset(around.bitcast(F32), 0.0).then_inc(cleared, 1)
                pool.memset(logits[:, :, :, :], 0.0).then_inc(cleared, 1)
                for b in range(B):
                    if b >= 2:
                        pool.wait_ge(turned, b - 1)
                    tiles = slice(b * TILES + OWN, (b + 1) * TILES)
                    out = rows[:, b % 2, OWN:TILES, :]
                    pool.tensor_tensor(out, g.h[:, tiles, :], g.mean[:, tiles].unsqueeze(2).broadcast_to(
                        [P, TILES - OWN, P]), ALU.subtract).then_inc(centred, 1)
                    pool.wait_ge(centred, b + 1)
                    pool.tensor_tensor(out, out, g.rstd[:, tiles].unsqueeze(2).broadcast_to([P, TILES - OWN, P]),
                                       ALU.mult).then_inc(pool_ready, 1)

            @block.tensor
            def _(pe):
                def turn_rows(b):
                    pe.wait_ge(ready, b + 1)
                    pe.wait_ge(pool_ready, b + 1)
                    if b >= 2:
                        pe.wait_ge(split, b - 1)
                    turn_tiles(pe, g, turn[b % 2], rows[:, b % 2, :, :]).then_inc(turned, 1)

                turn_rows(0)
                pe.wait_ge(cleared, 5)
                for b in range(B):
                    if b < B - 1:
                        turn_rows(b + 1)
                    pe.wait_ge(split, b + 1)
                    cut = slice(AT - E_N * b, AT - E_N * b + P)
                    for h, cols in enumerate(HALVES):
                        for i, (a, m) in enumerate([(wg_hi, y_hi), (wg_hi, y_lo), (wg_lo, y_hi)]):
                            last = pe.matmul(sums[:, h, 0:HALF], a[:, 0, cut], m[:, b % 2, cols],
                                             start=(b == 0 and i == 0), stop=(b == B - 1 and i == 2))
                    last.then_inc(done, 1)
                pe.wait_ge(sums_kept, 1)
                for c, n in enumerate(ROWS):
                    last = pe.transpose(back[0:n, c // 4, c % 4, :], kept[:, c * P:c * P + n], g.ident[:, :])
                last.then_inc(sums_turned, 1)

            @block.scalar
            def _(act):
                for b in range(B):
                    act.wait_ge(turned, b + 1)
                    if b >= 2:
                        act.wait_ge(done, b - 1)
                    round_cols(act, y_hi[:, b % 2, :], turn[b % 2]).then_inc(rounded, 1)

            @block.vector
            def _(dve):
                def norm(b):
                    if b >= 2:
                        dve.wait_ge(turned, b - 1)
                    for c in range(OWN):
                        at = b * TILES + c
                        last = dve.tensor_scalar(rows[:, b % 2, c, :], g.h[:, at, :], g.mean[:, at:at + 1],
                                                 g.rstd[:, at:at + 1], ALU.subtract, ALU.mult)
                    last.then_inc(ready, 1)

                norm(0)
                norm(1)
                for b in range(B):
                    dve.wait_ge(rounded, b + 1)
                    split_cols(dve, y_lo[:, b % 2, :], y_hi[:, b % 2, :], turn[b % 2]).then_inc(split, 1)
                    if b < B - 2:
                        norm(b + 2)
                dve.wait_ge(done, B)
                dve.tensor_copy(kept[:, :].rearrange("p (h n) -> p h n", h=2), sums[:, :, 0:HALF]).then_inc(sums_kept, 1)
                dve.wait_ge(cleared, 5)
                dve.wait_ge(sums_turned, 1)
                for c0, c1, n in [(0, 4, P), (4, 5, P), (5, 6, LAST)]:
                    dst = logits[0:n, c0:c1, :, :].rearrange("p c b e -> p (c b) e")
                    src = back[0:n, c0 // 4, c0 % 4:c0 % 4 + (c1 - c0), :].rearrange("p c (b e) -> p (c b) e", e=E_N)
                    if bias is None:
                        dve.tensor_copy(dst, src)
                    else:
                        dve.tensor_tensor(dst, src, bias[0:n, :].unsqueeze(1).broadcast_to([n, (c1 - c0) * B, E_N]),
                                          ALU.add)


def route(nc, g, logits, gates, k_tokens, k_experts, tag):
    N = B * TILES
    with ExitStack() as ctx:
        def sb(name, shape, dt=F32):
            return ctx.enter_context(nc.sbuf_tensor(f"{name}_{tag}", shape, dt))

        peak = sb("peak", [P, N])
        probs = logits
        total = sb("total", [P, N])
        turn = ctx.enter_context(nc.psum_tensor(f"g_turn_{tag}", [P, 2, 512], F32))
        gate_cols = sb("gate_cols", [P, T])
        work = sb("work", [P, T])
        cols = sb("cols", [P, T])
        best = sb("best", [P, 8])
        gate = sb("gate", [P, TILES, P]) if k_experts else None
        wins, beats = [sb(s, [P, N, E_N]) for s in ("wins", "beats")] if k_experts else (None, None)
        sem = semaphores(nc, ctx, "_" + tag)
        chain, exped, turned, copied, whole, kept = (
            sem(s) for s in ("g_chain", "g_exped", "g_turned", "g_copied", "g_whole", "g_kept"))
        flat = logits[:, :, :, :].rearrange("p c b e -> p (c b) e")

        def spread(a):
            return a[:, :].unsqueeze(2).broadcast_to([P, N, E_N])

        with nc.Block() as block:
            @block.vector
            def _(dve):
                count = [0]

                def then(ins):
                    count[0] += 1
                    ins.then_inc(chain, 1)
                    dve.wait_ge(chain, count[0])

                then(dve.tensor_reduce(peak[:, :], flat, AX.X, ALU.max))
                then(dve.tensor_tensor(flat, flat, spread(peak), ALU.subtract))
                dve.wait_ge(exped, 1)
                then(dve.tensor_reduce(total[:, :], flat, AX.X, ALU.add))
                then(dve.reciprocal(total[:, :], total[:, :]))
                then(dve.tensor_tensor(flat, flat, spread(total), ALU.mult))
                if k_experts:
                    then(dve.memset(wins[:, :, :], 0.0))
                    then(dve.memset(beats[:, :, :], 0.0))
                    for e in range(E_N):
                        one = flat[:, :, e:e + 1]
                        if e:
                            then(dve.tensor_tensor(beats[:, :, 0:e], one.broadcast_to([P, N, e]), flat[:, :, 0:e],
                                                   ALU.is_gt))
                        if e < E_N - 1:
                            then(dve.tensor_tensor(beats[:, :, e + 1:E_N], one.broadcast_to([P, N, E_N - 1 - e]),
                                                   flat[:, :, e + 1:E_N], ALU.is_ge))
                        if e:
                            then(dve.tensor_tensor(wins[:, :, 0:e], wins[:, :, 0:e], beats[:, :, 0:e], ALU.add))
                        if e < E_N - 1:
                            then(dve.tensor_tensor(wins[:, :, e + 1:E_N], wins[:, :, e + 1:E_N],
                                                   beats[:, :, e + 1:E_N], ALU.add))
                    then(dve.scalar_tensor_tensor(out=gate[:, :, :].rearrange("p c (b e) -> p (c b) e", e=E_N),
                                                  in0=wins[:, :, :], scalar=k_experts - 0.5, in1=flat,
                                                  op0=ALU.is_lt, op1=ALU.mult))
                dve.sem_inc(copied, 1)
                dve.wait_ge(turned, 1)
                if k_experts:
                    dve.tensor_copy(gate_cols[:, 0:512], turn[:, 0, :])
                    dve.tensor_copy(gate_cols[:, 512:T], turn[:, 1, 0:T - 512]).then_inc(whole, 1)
                    return
                for dst in (work, cols):
                    then(dve.tensor_copy(dst[:, 0:512], turn[:, 0, :]))
                    then(dve.tensor_copy(dst[:, 512:T], turn[:, 1, 0:T - 512]))
                rounds = -(-k_tokens // 8)
                for r in range(rounds):
                    then(dve.max(best[:, :], work[:, :]))
                    left = k_tokens - 8 * r
                    if left < 8:
                        then(dve.memset(best[:, left:8], -1.0))
                    then(dve.match_replace(work[:, :], best[:, :], work[:, :], -1.0))
                dve.scalar_tensor_tensor(out=gate_cols[:, :], in0=work[:, :], scalar=0.0, in1=cols[:, :],
                                         op0=ALU.is_lt, op1=ALU.mult).then_inc(whole, 1)

            @block.sync
            def _(sp):
                sp.wait_ge(whole, 1)
                sp.dma_start(gates, gate_cols[:, :]).then_inc(kept, 16)
                sp.wait_ge(kept, 16)

            @block.scalar
            def _(act):
                act.wait_ge(chain, 2)
                act.activation(flat, flat, ACT.Exp).then_inc(exped, 1)

            @block.tensor
            def _(pe):
                pe.wait_ge(copied, 1)
                src = gate[:, :, :] if k_experts else probs[:, :, :, :].rearrange("p c b e -> p c (b e)")
                turn_tiles(pe, g, turn, src).then_inc(turned, 1)


def gated_ffn(nc, g, w1_hi, w1_lo, b1, w2_hi, w2_lo, b2, shared_b2, blocks, shared, gates, out, tag):
    LAG, RING = 3, 4
    EXPERTS = w2_hi.shape[1] // blocks
    UP = EXPERTS * blocks
    FREE = shared * blocks
    FIRST = 1 if shared else 0
    ITEMS = FIRST + E_N
    SUMS = ITEMS - 1
    G_RING = 2 if shared else 4
    PARTS = [slice(0, 3 * P), slice(3 * P, T)]
    BACK_AT, TURN_AT = [5, 8], [9, 12]
    assert UP % RING == 0 and E_N % G_RING == 0 and UP > TURN_AT[1] + 1

    def item_of(k):
        return 0 if k < FREE else FIRST + (k - FREE) // blocks

    def opens(k):
        return k == 0 or k >= FREE and (k - FREE) % blocks == 0

    def ends(k):
        return k == FREE - 1 if k < FREE else (k - FREE) % blocks == blocks - 1

    def last_of(item):
        return FREE + (item - FIRST + 1) * blocks - 1

    with ExitStack() as ctx:
        def sb(name, shape, dt=F32):
            return ctx.enter_context(nc.sbuf_tensor(f"{name}_{tag}", shape, dt))

        def ps(name, shape):
            return ctx.enter_context(nc.psum_tensor(f"{name}_{tag}", shape, F32))

        sem = semaphores(nc, ctx, "_" + tag)

        rows = sb("f_rows", [P, TILES, P])
        y_hi = sb("f_hi", [P, 2, T], F32R)
        y_lo = sb("f_lo", [P, 2, T], F32R)
        hid = sb("f_hid", [P, 2, T])
        hid_hi = sb("f_hid_hi", [P, RING, T], F32R)
        hid_lo = sb("f_hid_lo", [P, RING, T], F32R)
        gate = sb("f_gate", [P, G_RING, T])
        acc = sb("f_acc", [P, 2, T])
        turn, back = ps("f_turn", [P, 512]), ps("f_back", [P, 4, P])
        up = [ps(f"f_up{h}", [P, 512]) for h in range(2)]
        down = [[ps(f"f_down{q}{h}", [P, 512]) for h in range(2)] for q in range(2)]
        (centred, ready, turned, rounded, split, up_done, gelu_done, hi_done, lo_done, hid_used, gated, summed,
         turned_back, returned) = (
            sem(s) for s in ("f_centred", "f_ready", "f_turned", "f_rounded", "f_split", "f_up_done", "f_gelu_done",
                             "f_hi_done", "f_lo_done", "f_hid_used", "f_gated", "f_summed", "f_turned_back",
                             "f_returned"))
        stored = sem("f_stored")
        gate_in = [sem(f"f_gate_in{k}") for k in range(G_RING)]

        def sum_of(slot, item, h):
            place = (slot + item) % 2 if ITEMS % 2 else item % 2
            return down[place][h][:, 0:HALF]

        with nc.Block() as block:
            @block.sync
            def _(sp):
                def fetch(b, slot):
                    for e in range(E_N):
                        if e >= G_RING:
                            item = FIRST + e - G_RING
                            if item:
                                sp.wait_ge(summed, b * SUMS + item)
                            else:
                                sp.wait_ge(gated, b * (2 * ITEMS) + 2)
                        elif at_least(b, 1):
                            sp.wait_ge(summed, b * SUMS - (G_RING - e - 1))
                        sp.dma_start(gate[:, e % G_RING, :],
                                     gates[bass.ds(b * E_N + e, 1), :].broadcast_to([P, T])
                                     ).then_inc(gate_in[e % G_RING], 16)

                def store(b):
                    sp.wait_ge(returned, b * 2 + 2)
                    sp.dma_start(out[bass.ds(b, 1), 0:(TILES - 1) * P, :].rearrange("o (c p) d -> (o p) c d", p=P),
                                 g.h[:, bass.ds(b * TILES, TILES - 1), :]).then_inc(stored, 16)
                    sp.dma_start(out[bass.ds(b, 1), (TILES - 1) * P:T, :].rearrange("o p d -> (o p) d"),
                                 g.h[0:LAST, bass.ds(b * TILES + (TILES - 1), 1), :].rearrange("p o d -> p (o d)")
                                 ).then_inc(stored, 16)

                def step(b, slot):
                    fetch(b, slot)
                    if out is not None and at_least(b, 1):
                        store(b - 1)
                steps(sp, B, 2, step)
                if out is not None:
                    store(B - 1)
                    sp.wait_ge(stored, 32 * B)

            @block.gpsimd
            def _(pool):
                def norm(b):
                    if at_least(b, 1):
                        pool.wait_ge(turned, b * 2)
                    normalize(pool, g, rows[:, :, :], b, centred, b + 1).then_inc(ready, 1)

                def step(b, slot):
                    if before(b, B - 1):
                        norm(b + 1)
                    for item in range(1, ITEMS):
                        place = gate[:, (item - FIRST) % G_RING, :]
                        pool.wait_ge(gated, b * (2 * ITEMS) + (2 * item + 2))
                        if item >= 2:
                            pool.wait_ge(summed, b * SUMS + (item - 1))
                        pool.tensor_tensor(acc[:, slot, :], acc[:, slot, :], place, ALU.add).then_inc(summed, 1)
                norm(0)
                steps(pool, B, 2, step)

            @block.tensor
            def _(pe):
                def turn_rows(b, slot, part):
                    if part == 0:
                        pe.wait_ge(ready, b + 1)
                    if at_least(b, 1) or part:
                        pe.wait_ge(split, b * 2 + part)
                    for c in range(3 * part, 3 * part + 3):
                        last = pe.transpose(turn[:, (c % 3) * P:(c % 3) * P + ROWS[c]], rows[0:ROWS[c], c, :],
                                            g.ident[0:ROWS[c], 0:ROWS[c]])
                    last.then_inc(turned, 1)

                def widen(b, slot, k):
                    for h, cols in enumerate(HALVES):
                        if at_least(b, 1) or k:
                            pe.wait_ge(gelu_done, b * (2 * UP) + (2 * k - 1 + h))
                        for i, (a, m) in enumerate([(w1_hi, y_hi), (w1_hi, y_lo), (w1_lo, y_hi)]):
                            last = pe.matmul(up[h][:, 0:HALF], a[:, k, :], m[:, slot, cols],
                                             start=(i == 0), stop=(i == 2))
                        last.then_inc(up_done, 1)

                def narrow(b, slot, k):
                    item = item_of(k)
                    pe.wait_ge(lo_done, b * UP + (k + 1))
                    for h, cols in enumerate(HALVES):
                        if opens(k) and (at_least(b, 1) or item >= 2):
                            pe.wait_ge(gated, b * (2 * ITEMS) + (2 * item - 3 + h))
                        for i, (a, m) in enumerate([(w2_hi, hid_hi), (w2_hi, hid_lo), (w2_lo, hid_hi)]):
                            last = pe.matmul(sum_of(slot, item, h), a[:, k, :], m[:, k % RING, cols],
                                             start=(opens(k) and i == 0), stop=(ends(k) and i == 2))
                    last.then_inc(hid_used, 1)

                def turn_back(b, slot, part):
                    if part == 0:
                        pe.wait_ge(summed, b * SUMS + SUMS)
                    if at_least(b, 1) or part:
                        pe.wait_ge(returned, b * 2 + part)
                    for c in range(3 * part, 3 * part + 3):
                        last = pe.transpose(back[0:ROWS[c], c % 3, :], acc[:, slot, c * P:c * P + ROWS[c]],
                                            g.ident[:, :])
                    last.then_inc(turned_back, 1)

                def step(b, slot):
                    pe.wait_ge(split, b * 2 + 2)
                    for k in range(UP):
                        widen(b, slot, k)
                        if k >= LAG:
                            narrow(b, slot, k - LAG)
                        elif at_least(b, 1):
                            narrow(b - 1, 1 - slot, UP + k - LAG)
                        if k in BACK_AT and at_least(b, 1):
                            turn_back(b - 1, 1 - slot, BACK_AT.index(k))
                        if k in TURN_AT and before(b, B - 1):
                            turn_rows(b + 1, 1 - slot, TURN_AT.index(k))
                turn_rows(0, 0, 0)
                turn_rows(0, 0, 1)
                steps(pe, B, 2, step)
                for k in range(UP - LAG, UP):
                    narrow(B - 1, (B - 1) % 2, k)
                turn_back(B - 1, (B - 1) % 2, 0)
                turn_back(B - 1, (B - 1) % 2, 1)

            @block.scalar
            def _(act):
                def round_y(b, slot, part):
                    act.wait_ge(turned, b * 2 + (part + 1))
                    if at_least(b, 2):
                        act.wait_ge(up_done, b * (2 * UP) - 2 * UP)
                    cols = PARTS[part]
                    act.copy(y_hi[:, slot, cols], turn[:, 0:cols.stop - cols.start]).then_inc(rounded, 1)

                def step(b, slot):
                    for k in range(UP):
                        if at_least(b, 1) or k >= 2:
                            act.wait_ge(lo_done, b * UP + (k - 1))
                        for h, cols in enumerate(HALVES):
                            act.wait_ge(up_done, b * (2 * UP) + (2 * k + 1 + h))
                            act.activation(hid[:, k % 2, cols], up[h][:, 0:HALF], ACT.Gelu,
                                           bias=b1[:, 0, k:k + 1]).then_inc(gelu_done, 1)
                        act.wait_ge(gelu_done, b * (2 * UP) + (2 * k + 2))
                        if at_least(b, 1) or k >= RING:
                            act.wait_ge(hid_used, b * UP + (k - RING + 1))
                        act.copy(hid_hi[:, k % RING, :], hid[:, k % 2, :]).then_inc(hi_done, 1)
                        if k - 1 in TURN_AT and before(b, B - 1):
                            round_y(b + 1, 1 - slot, TURN_AT.index(k - 1))
                round_y(0, 0, 0)
                round_y(0, 0, 1)
                steps(act, B, 2, step)

            @block.vector
            def _(dve):
                def split_y(b, slot, part):
                    dve.wait_ge(rounded, b * 2 + (part + 1))
                    cols = PARTS[part]
                    dve.tensor_tensor(y_lo[:, slot, cols], turn[:, 0:cols.stop - cols.start],
                                      y_hi[:, slot, cols].bitcast(F32), ALU.subtract).then_inc(split, 1)

                def split_hid(b, k):
                    dve.wait_ge(hi_done, b * UP + (k + 1))
                    dve.tensor_tensor(hid_lo[:, k % RING, :], hid[:, k % 2, :],
                                      hid_hi[:, k % RING, :].bitcast(F32), ALU.subtract).then_inc(lo_done, 1)

                def take(b, slot, item):
                    e = item - FIRST
                    dve.wait_ge(hid_used, b * UP + (last_of(item) + 1))
                    if e >= 0:
                        dve.wait_ge(gate_in[e % G_RING], b * (16 * E_N // G_RING) + 16 * (e // G_RING + 1))
                    if item == 0 and at_least(b, 2):
                        dve.wait_ge(turned_back, b * 2 - 2)
                    for h, cols in enumerate(HALVES):
                        if e < 0:
                            ins = dve.tensor_scalar(acc[:, slot, cols], sum_of(slot, item, h), shared_b2, None, ALU.add)
                        else:
                            to = gate[:, e % G_RING, cols] if item else acc[:, slot, cols]
                            ins = dve.scalar_tensor_tensor(out=to, in0=sum_of(slot, item, h), scalar=b2[:, 0, e:e + 1],
                                                           in1=gate[:, e % G_RING, cols], op0=ALU.add, op1=ALU.mult)
                        ins.then_inc(gated, 1)

                def takes(b, slot, k):
                    if ends(k):
                        take(b, slot, item_of(k))

                def give_back(b, part):
                    dve.wait_ge(turned_back, b * 2 + (part + 1))
                    for c0, c1, n in [(0, 3, P)] if part == 0 else [(3, 5, P), (5, 6, LAST)]:
                        h = g.h[0:n, bass.ds(b * TILES + c0, c1 - c0), :]
                        last = dve.tensor_tensor(h, h, back[0:n, c0 % 3:c0 % 3 + (c1 - c0), :], ALU.add)
                    last.then_inc(returned, 1)
                    if out is None:
                        dve.wait_ge(returned, b * 2 + (part + 1))
                        take_statistics(dve, g, b, range(3 * part, 3 * part + 3))

                def step(b, slot):
                    for k in range(UP):
                        split_hid(b, k)
                        if k >= LAG:
                            takes(b, slot, k - LAG)
                        elif at_least(b, 1):
                            takes(b - 1, 1 - slot, UP + k - LAG)
                        if k - 1 in BACK_AT and at_least(b, 1):
                            give_back(b - 1, BACK_AT.index(k - 1))
                        if k - 1 in TURN_AT and before(b, B - 1):
                            split_y(b + 1, 1 - slot, TURN_AT.index(k - 1))
                split_y(0, 0, 0)
                split_y(0, 0, 1)
                steps(dve, B, 2, step)
                for k in range(UP - LAG, UP):
                    takes(B - 1, (B - 1) % 2, k)
                give_back(B - 1, 0)
                give_back(B - 1, 1)


def load_small(nc, loads, tag):
    clears = [c for _, _, c in loads if c is not None]
    with ExitStack() as ctx:
        sem = semaphores(nc, ctx, "_" + tag)
        done, cleared = sem("small_loaded"), sem("small_cleared")
        with nc.Block() as block:
            @block.vector
            def _(dve):
                for c in clears:
                    dve.memset(c, 0.0).then_inc(cleared, 1)

            @block.sync
            def _(sp):
                if clears:
                    sp.wait_ge(cleared, len(clears))
                for dst, src, _ in loads:
                    sp.dma_start(dst, src).then_inc(done, 16)
                sp.wait_ge(done, 16 * len(loads))


def expert_choice(nc, g, w):
    HID = 256
    BLOCKS = HID // P
    K_TOKENS = min(max(T * 2 // E_N, 1), T)
    with ExitStack() as ctx:
        def sb(name, shape, dt=F32):
            return ctx.enter_context(nc.sbuf_tensor(name, shape, dt))

        gates = nc.dram_tensor("c_gates", (P, T), F32, kind="Internal").ap()
        w1_hi = sb("c_w1_hi", [P, E_N * BLOCKS, P], F32R)
        w1_lo = sb("c_w1_lo", [P, E_N * BLOCKS, P], F32R)
        w2_hi = sb("c_w2_hi", [P, E_N * BLOCKS, P], F32R)
        w2_lo = sb("c_w2_lo", [P, E_N * BLOCKS, P], F32R)
        b1 = sb("c_b1", [P, 1, E_N * BLOCKS])
        b2 = sb("c_b2", [P, 1, E_N])
        with ExitStack() as inner:
            wg_hi = inner.enter_context(nc.sbuf_tensor("c_wg_hi", [P, 1, WIDE], F32R))
            wg_lo = inner.enter_context(nc.sbuf_tensor("c_wg_lo", [P, 1, WIDE], F32R))
            logits = inner.enter_context(nc.sbuf_tensor("c_logits", [P, TILES, B, E_N], F32))
            weights_and_statistics(nc, g, [
                (wg_hi[:, :, AT:AT + E_N], wg_lo[:, :, AT:AT + E_N], w["L0_ffn_Wg"].rearrange("h (o e) -> h o e", o=1), False),
                *[(w1_hi[:, e * BLOCKS:(e + 1) * BLOCKS, :], w1_lo[:, e * BLOCKS:(e + 1) * BLOCKS, :],
                   w["L0_ffn_W1"][e].rearrange("h (j f) -> h j f", f=P), False) for e in range(E_N)],
                (w2_hi[:, :, :], w2_lo[:, :, :], w["L0_ffn_W2"].rearrange("e (j f) h -> f (e j) h", f=P), False),
                (b2[:, :, :], None, w["L0_ffn_b2"].rearrange("e (o h) -> e o h", o=1), True),
                (b1[:, :, :], None, w["L0_ffn_b1"].rearrange("e (j o f) -> (e j) o f", o=1, f=P), True),
            ], "c", False)
            router_logits(nc, g, wg_hi, wg_lo, None, logits, "c")
            route(nc, g, logits, gates, K_TOKENS, None, "c")
        gated_ffn(nc, g, w1_hi, w1_lo, b1, w2_hi, w2_lo, b2, None, BLOCKS, 0, gates, None, "c")


S_HEADS = 8
S_DIM = 64
SLICES = 32
HS = S_HEADS * SLICES


def slice_weights(nc, g, w, wqk_hi, wqk_lo, fold, bias_q, bias_k, bias_out):
    with ExitStack() as ctx:
        def sb(name, shape, dt=F32):
            return ctx.enter_context(nc.sbuf_tensor(name, shape, dt))

        def psum(name, shape):
            return ctx.enter_context(nc.psum_tensor(name, shape, F32))

        sem = semaphores(nc, ctx)

        win_t = sb("win_t", [S_DIM, S_HEADS, P])
        wv_t = sb("wv_t", [S_DIM, 1, S_DIM])
        b_col = sb("b_col", [S_DIM, 1, S_HEADS])
        wqk = sb("wqk_raw", [S_DIM, 2, SLICES])
        w_out = sb("w_out_raw", [S_DIM, S_HEADS, P])
        b_out = sb("b_out_rows", [P, P])
        b_wide = sb("b_wide", [S_DIM, S_HEADS, P])
        wvo = sb("wvo", [S_DIM, S_HEADS, P])
        weights_and_statistics(nc, g, [
            (win_t[:, :, :], None, w["L1_attn_W_in"].rearrange("d (h k) -> d h k", k=S_DIM), True),
            (wv_t[:, :, :], None, w["L1_attn_Wv"].rearrange("k (o c) -> k o c", o=1), True),
            (b_col[:, :, :], None, w["L1_attn_b_in"].rearrange("(h o k) -> h o k", o=1, k=S_DIM), True)], "d", True)
        load_small(nc, [
            (wqk[:, 0, :], w["L1_attn_Wq"], None), (wqk[:, 1, :], w["L1_attn_Wk"], None),
            (w_out[:, :, :], w["L1_attn_W_out"].rearrange("(h k) o -> k h o", k=S_DIM), None),
            (b_out[:, :], w["L1_attn_b_out"].unsqueeze(0).broadcast_to([P, P]), None)], "d")
        p_vo = psum("p_vo", [S_DIM, 2, 4, P])
        p_qk = psum("p_qk", [P, S_HEADS, 2, SLICES])
        p_fold = psum("p_fold", [P, 2, 4, P])
        p_bq = psum("p_bq", [P, S_HEADS, SLICES])
        p_bo = psum("p_bo", [P, 2, P])
        p_bk = psum("p_bk", [P, 2])
        widened, vo_done, vo_kept, rest_done, rounded = (
            sem(s) for s in ("b_widened", "vo_done", "vo_kept", "rest_done", "wqk_rounded"))
        with nc.Block() as block:
            @block.tensor
            def _(pe):
                for h in range(S_HEADS):
                    last = pe.matmul(p_vo[:, h // 4, h % 4, :], wv_t[:, 0, :], w_out[:, h, :], start=True, stop=True)
                last.then_inc(vo_done, 1)
                pe.wait_ge(widened, 1)
                pe.wait_ge(vo_kept, 1)
                for h in range(S_HEADS):
                    at = slice((h % 4) * SLICES, (h % 4 + 1) * SLICES)
                    pe.matmul(p_qk[:, h, :, :], win_t[:, h, :], wqk[:, :, :], start=True, stop=True)
                    pe.matmul(p_fold[:, h // 4, h % 4, :], win_t[:, h, :], wvo[:, h, :], start=True, stop=True)
                    pe.matmul(p_bq[:, h, :], b_wide[:, h, :], wqk[:, 0, :], start=True, stop=True)
                    pe.matmul(p_bo[at, h // 4, :], b_wide[:, h, 0:SLICES], wvo[:, h, :], start=True, stop=True)
                    last = pe.matmul(p_bk[at, h // 4:h // 4 + 1], wqk[:, 1, :], b_col[:, 0, h:h + 1],
                                     start=True, stop=True)
                last.then_inc(rest_done, 1)

            @block.vector
            def _(dve):
                dve.tensor_copy(b_wide[:, :, :], b_col[:, 0, :].unsqueeze(2).broadcast_to([S_DIM, S_HEADS, P])
                                ).then_inc(widened, 1)
                dve.wait_ge(vo_done, 1)
                dve.tensor_copy(wvo[:, :, :], p_vo[:, :, :, :].rearrange("p a b o -> p (a b) o")).then_inc(vo_kept, 1)
                dve.wait_ge(rest_done, 1)
                for j in range(2):
                    dve.scalar_tensor_tensor(out=bias_out[:, j, :], in0=b_out[:, :], scalar=1.0 / S_HEADS,
                                             in1=p_bo[:, j, :], op0=ALU.mult, op1=ALU.add)
                dve.tensor_copy(bias_k[:, :], p_bk[:, :])
                dve.tensor_copy(fold[:, :, :], p_fold[:, :, :, :].rearrange("p a b o -> p (a b) o"))
                dve.wait_ge(rounded, 3)
                for j in range(2):
                    dve.tensor_tensor(wqk_lo[:, j, :].rearrange("p (h s) -> p h s", s=SLICES), p_qk[:, :, j, :],
                                      wqk_hi[:, j, :].bitcast(F32).rearrange("p (h s) -> p h s", s=SLICES), ALU.subtract)
                dve.tensor_tensor(bias_q[:, 1, :].rearrange("p (h s) -> p h s", s=SLICES), p_bq[:, :, :],
                                  bias_q[:, 0, :].bitcast(F32).rearrange("p (h s) -> p h s", s=SLICES), ALU.subtract)

            @block.scalar
            def _(act):
                act.wait_ge(rest_done, 1)
                for j in range(2):
                    act.copy(wqk_hi[:, j, :].rearrange("p (h s) -> p h s", s=SLICES), p_qk[:, :, j, :]
                             ).then_inc(rounded, 1)
                act.copy(bias_q[:, 0, :].rearrange("p (h s) -> p h s", s=SLICES), p_bq[:, :, :]).then_inc(rounded, 1)


def slice_attention(nc, g, w):
    with ExitStack() as ctx:
        def sb(name, shape, dt=F32):
            return ctx.enter_context(nc.sbuf_tensor(name, shape, dt))

        sem = semaphores(nc, ctx)

        wqk_hi, wqk_lo = sb("wqk_hi", [P, 2, HS], F32R), sb("wqk_lo", [P, 2, HS], F32R)
        fold = sb("fold", [P, S_HEADS, P])
        bias_q = sb("bias_q", [P, 2, HS], F32R)
        bias_k = sb("bias_k", [P, 2])
        bias_out = sb("bias_out", [P, 2, P])
        slice_weights(nc, g, w, wqk_hi, wqk_lo, fold, bias_q, bias_k, bias_out)

        first_row = sb("first_row", [P, P], F32R)
        rows = sb("d_rows", [P, 2, TILES, P])
        y_hi, y_lo = sb("d_hi", [P, 2, T], F32R), sb("d_lo", [P, 2, T], F32R)
        k_neg, k_shift = sb("k_neg", [P, 2]), sb("k_shift", [P, 2])
        k_sum, k_inv = sb("k_sum", [P, 2, 2]), sb("k_inv", [P, 2])
        k_exp = sb("k_exp", [P, 2, T])
        k_tok = sb("k_tok", [P, TILES, HS])
        ky = sb("ky", [P, HS])
        mix = sb("mix", [P, 2, P])
        q_sb = sb("q_sb", [P, 2, TILES * S_HEADS, SLICES])
        q_peak, q_sum = sb("q_peak", [P, TILES * S_HEADS]), sb("q_sum", [P, 2, TILES * S_HEADS])
        q_cols = sb("q_cols", [P, 2, T])
        PA, PB, PC = [ctx.enter_context(nc.psum_tensor(f"d_pair{k}", [P, 2, 512], F32)) for k in range(3)]
        PD = ctx.enter_context(nc.psum_tensor("d_single", [P, 512], F32))
        p_sums = ctx.enter_context(nc.psum_tensor("p_sums", [P, 2, HS], F32))
        p_ky, p_mix = p_sums[:, 0, :], p_sums[:, 1, :].rearrange("p (j o) -> p j o", j=2)
        used = [sem(f"d_used{k}") for k in range(4)]
        (row_set, bank_cleared, centred, ready, turned, rounded, k_done, k_negated, k_shifted, k_turned, ky_done, ky_kept, mix_done,
         k_inverted, mix_ready, q_done, q_peaked, q_exped, q_summed, q_inverted, q_ready, q_turned, out_done) = (
            sem("d_" + s) for s in (
                "row_set", "bank_cleared", "centred", "ready", "turned", "rounded", "k_done", "k_negated", "k_shifted", "k_turned",
                "ky_done", "ky_kept", "mix_done", "k_inverted", "mix_ready", "q_done", "q_peaked", "q_exped",
                "q_summed", "q_inverted", "q_ready", "q_turned", "out_done"))
        A, B_, C, D = range(4)
        PLACE = {"y": (A, 0), "k0": (A, 1), "out": (A, 2),
                 "kt0": (B_, 0), "k1": (B_, 1), "qt0": (B_, 2),
                 "kt1": (C, 0), "qt1": (C, 1), "q1": (C, 2), "q0": (D, 0)}
        AHEAD = {"y": 0, "k0": 1, "k1": 0, "q0": 0, "q1": 0}
        LEFT = {"kt0": 0, "qt0": 1, "kt1": 0, "qt1": 1, "out": 0}
        ROUND = {A: 3, B_: 3, C: 3, D: 1}
        START = {A: 2, B_: 1, C: 1, D: 1}

        def place(job, b):
            pair, at = PLACE[job]
            if job in AHEAD:
                if isinstance(b, int) and b == 0:
                    return pair, AHEAD[job]
                return pair, b * ROUND[pair] + (START[pair] - ROUND[pair] + at)
            if isinstance(b, int) and b == B - 1:
                at = LEFT[job]
            return pair, b * ROUND[pair] + (START[pair] + at)

        def free(eng, job, b):
            pair, before_it = place(job, b)
            if not (isinstance(before_it, int) and before_it == 0):
                eng.wait_ge(used[pair], before_it)

        def over(eng, job, b):
            pair, before_it = place(job, b)
            eng.wait_ge(used[pair], before_it + 1)

        K_PARTS, Q_PARTS = [(0, 4), (4, 2)], [(4, 2), (0, 4)]
        Q_BANKS = [PD[:, :].unsqueeze(1), PC[:, :, :]]

        with nc.Block() as block:
            @block.gpsimd
            def _(pool):
                pool.memset(first_row[:, :].bitcast(F32), 0.0).then_inc(row_set, 1)
                pool.wait_ge(row_set, 1)
                pool.memset(first_row[0:1, :].bitcast(F32), 1.0).then_inc(row_set, 1)

                def norm(b, slot):
                    if at_least(b, 2):
                        pool.wait_ge(ky_done, b - 1)
                    normalize(pool, g, rows[:, slot, :, :], b, centred, b + 1).then_inc(ready, 1)

                def scale_q(b, slot):
                    for part, (c, n) in enumerate(Q_PARTS):
                        pool.wait_ge(q_inverted, b * 2 + (part + 1))
                        at = slice(c * S_HEADS, (c + n) * S_HEADS)
                        q = q_sb[:, slot, at, :]
                        pool.tensor_tensor(q, q, q_sum[:, slot, at].unsqueeze(2).broadcast_to(
                            [P, n * S_HEADS, SLICES]), ALU.mult).then_inc(q_ready, 1)

                def rounds(b, slot):
                    if before(b, B - 2):
                        norm(b + 2, slot)
                    if before(b, B - 1):
                        scale_q(b + 1, 1 - slot)
                norm(0, 0)
                norm(1, 1)
                scale_q(0, 0)
                steps(pool, B, 2, rounds)

            @block.tensor
            def _(pe):
                def turn_y(b, slot):
                    pe.wait_ge(ready, b + 1)
                    free(pe, "y", b)
                    turn_tiles(pe, g, PA, rows[:, slot, :, :]).then_inc(turned, 1)

                def k_proj(b, slot, j):
                    if j == 0:
                        over(pe, "y", b)
                    free(pe, f"k{j}", b)
                    for h, cols in enumerate(HALVES):
                        for i, (a, m) in enumerate([(wqk_hi, y_hi), (wqk_hi, y_lo), (wqk_lo, y_hi)]):
                            last = pe.matmul((PA, PB)[j][:, h, 0:HALF], a[:, 1, j * P:(j + 1) * P], m[:, slot, cols],
                                             start=(i == 0), stop=(i == 2))
                    last.then_inc(k_done, 1)

                def q_proj(b, slot, part):
                    free(pe, f"q{part}", b)
                    c0, n_tiles = Q_PARTS[part]
                    for c in range(c0, c0 + n_tiles):
                        n, at = ROWS[c], c - c0
                        out = Q_BANKS[part][0:n, at // 2, (at % 2) * HS:(at % 2 + 1) * HS]
                        for i, (a, m) in enumerate([(y_hi, wqk_hi), (y_hi, wqk_lo), (y_lo, wqk_hi)]):
                            pe.matmul(out, a[:, slot, c * P:c * P + n], m[:, 0, :], start=(i == 0), stop=False)
                        pe.matmul(out, first_row[:, 0:n], bias_q[:, 0, :], start=False, stop=False)
                        last = pe.matmul(out, first_row[:, 0:n], bias_q[:, 1, :], start=False, stop=True)
                    last.then_inc(q_done, 1)

                def k_turn(b, part):
                    if part == 0:
                        over(pe, "k0", b)
                    free(pe, f"kt{part}", b)
                    c0, n_tiles = K_PARTS[part]
                    for c in range(c0, c0 + n_tiles):
                        at = c - c0
                        for j in range(2):
                            last = pe.transpose((PB, PC)[part][0:ROWS[c], at // 2, (at % 2) * HS + j * P:
                                                               (at % 2) * HS + (j + 1) * P],
                                                k_exp[:, j, c * P:c * P + ROWS[c]], g.ident[:, :])
                    last.then_inc(k_turned, 1)

                def ky_sum(b, slot):
                    over(pe, "kt0", b)
                    over(pe, "kt1", b)
                    if at_least(b, 1):
                        pe.wait_ge(ky_kept, b)
                    for c, n in enumerate(ROWS):
                        last = pe.matmul(p_ky, rows[0:n, slot, c, :], k_tok[0:n, c, :],
                                         start=(c == 0), stop=(c == TILES - 1))
                    last.then_inc(ky_done, 1)

                def mixing(b):
                    pe.wait_ge(ky_kept, b + 1)
                    if at_least(b, 1):
                        pe.wait_ge(mix_ready, b)
                    for h in range(S_HEADS):
                        last = pe.matmul(p_mix[(h % 4) * SLICES:(h % 4 + 1) * SLICES, h // 4, :],
                                         ky[:, h * SLICES:(h + 1) * SLICES], fold[:, h, :], start=True, stop=True)
                    last.then_inc(mix_done, 1)

                def q_turn(b, slot, j):
                    if j == 1:
                        pe.wait_ge(q_ready, b * 2 + 2)
                    free(pe, f"qt{j}", b)
                    for c, n in enumerate(ROWS):
                        src = q_sb[0:n, slot, c * S_HEADS + j * 4:c * S_HEADS + (j + 1) * 4, :]
                        last = pe.transpose((PB, PC)[j][:, c // 4, (c % 4) * P:(c % 4) * P + n],
                                            src.rearrange("p h s -> p (h s)"), g.ident[0:n, 0:n])
                    last.then_inc(q_turned, 1)

                def output(b):
                    over(pe, "qt0", b)
                    over(pe, "qt1", b)
                    pe.wait_ge(mix_ready, b + 1)
                    free(pe, "out", b)
                    for c, n in enumerate(ROWS):
                        for j in range(2):
                            last = pe.matmul(PA[0:n, c // 4, (c % 4) * P:(c % 4 + 1) * P],
                                             q_cols[:, j, c * P:c * P + n], mix[:, j, :], start=(j == 0), stop=(j == 1))
                    last.then_inc(out_done, 1)

                def rounds(b, slot):
                    nxt, more = 1 - slot, before(b, B - 1)
                    if more:
                        turn_y(b + 1, nxt)
                    k_turn(b, 0)
                    k_turn(b, 1)
                    if more:
                        k_proj(b + 1, nxt, 0)
                        k_proj(b + 1, nxt, 1)
                    ky_sum(b, slot)
                    q_turn(b, slot, 1)
                    if more:
                        q_proj(b + 1, nxt, 0)
                    mixing(b)
                    q_turn(b, slot, 0)
                    if more:
                        q_proj(b + 1, nxt, 1)
                    output(b)
                pe.wait_ge(row_set, 2)
                pe.wait_ge(bank_cleared, 1)
                turn_y(0, 0)
                k_proj(0, 0, 0)
                k_proj(0, 0, 1)
                q_proj(0, 0, 0)
                q_proj(0, 0, 1)
                steps(pe, B, 2, rounds)

            @block.vector
            def _(dve):
                def split_y(b, slot):
                    dve.wait_ge(rounded, b + 1)
                    split_cols(dve, y_lo[:, slot, :], y_hi[:, slot, :], PA).then_inc(used[A], 1)

                def k_peak(b, j):
                    dve.wait_ge(k_done, b * 2 + (j + 1))
                    dve.tensor_reduce(k_neg[:, j:j + 1], (PA, PB)[j][:, :, 0:HALF], AX.XY, ALU.max, negate=True
                                      ).then_inc(k_negated, 1)
                    dve.wait_ge(k_negated, b * 2 + (j + 1))
                    if at_least(b, 1):
                        dve.wait_ge(used[(A, B_)[j]], place(f"k{j}", b)[1])
                    dve.scalar_tensor_tensor(out=k_shift[:, j:j + 1], in0=k_neg[:, j:j + 1], scalar=bias_k[:, j:j + 1],
                                             in1=bias_k[:, j:j + 1], op0=ALU.subtract, op1=ALU.add
                                             ).then_inc(k_shifted, 1)

                def q_centre(b, slot, part):
                    dve.wait_ge(q_done, b * 2 + (part + 1))
                    c, n = Q_PARTS[part]
                    at = slice(c * S_HEADS, (c + n) * S_HEADS)
                    src = Q_BANKS[part].rearrange("p a (h s) -> p (a h) s", s=SLICES)
                    dve.tensor_reduce(q_peak[:, at], src, AX.X, ALU.max).then_inc(q_peaked, 1)
                    dve.wait_ge(q_peaked, b * 2 + (part + 1))
                    if at_least(b, 2):
                        dve.wait_ge(q_turned, b * 2 - 2)
                    dve.tensor_tensor(q_sb[:, slot, at, :], src, q_peak[:, at].unsqueeze(2).broadcast_to(
                        [P, n * S_HEADS, SLICES]), ALU.subtract).then_inc(used[(D, C)[part]], 1)

                def q_total(b, slot, part):
                    c, n = Q_PARTS[part]
                    at = slice(c * S_HEADS, (c + n) * S_HEADS)
                    dve.wait_ge(q_exped, b * 2 + (part + 1))
                    dve.tensor_reduce(q_sum[:, slot, at], q_sb[:, slot, at, :], AX.X, ALU.add).then_inc(q_summed, 1)
                    dve.wait_ge(q_summed, b * 2 + (part + 1))
                    dve.reciprocal(q_sum[:, slot, at], q_sum[:, slot, at]).then_inc(q_inverted, 1)

                def mix_out(b, slot):
                    over(dve, "k0", b)
                    over(dve, "k1", b)
                    dve.reciprocal(k_inv[:, :], k_sum[:, slot, :]).then_inc(k_inverted, 1)
                    dve.wait_ge(k_inverted, b + 1)
                    dve.wait_ge(mix_done, b + 1)
                    if at_least(b, 1):
                        dve.wait_ge(out_done, b)
                    for j in range(2):
                        last = dve.scalar_tensor_tensor(out=mix[:, j, :], in0=p_mix[:, j, :], scalar=k_inv[:, j:j + 1],
                                                        in1=bias_out[:, j, :], op0=ALU.mult, op1=ALU.add)
                    last.then_inc(mix_ready, 1)

                def add(b):
                    dve.wait_ge(out_done, b + 1)
                    for c0, c1, n in [(0, 4, P), (4, 5, P), (5, 6, LAST)]:
                        h = g.h[0:n, bass.ds(b * TILES + c0, c1 - c0), :]
                        src = PA[0:n, c0 // 4, (c0 % 4) * P:((c1 - 1) % 4 + 1) * P].rearrange("p (c d) -> p c d", d=P)
                        last = dve.tensor_tensor(h, src, h, ALU.add)
                    last.then_inc(used[A], 1)

                def statistics(b):
                    over(dve, "out", b)
                    take_statistics(dve, g, b, range(TILES))

                def rounds(b, slot):
                    nxt, more = 1 - slot, before(b, B - 1)
                    if more:
                        split_y(b + 1, nxt)
                        k_peak(b + 1, 0)
                        k_peak(b + 1, 1)
                    if at_least(b, 1):
                        statistics(b - 1)
                    if more:
                        q_centre(b + 1, nxt, 0)
                    mix_out(b, slot)
                    if more:
                        q_total(b + 1, nxt, 0)
                        q_centre(b + 1, nxt, 1)
                    add(b)
                    if more:
                        q_total(b + 1, nxt, 1)
                dve.memset(PD[:, :], 0.0).then_inc(bank_cleared, 1)
                split_y(0, 0)
                for j in range(2):
                    k_peak(0, j)
                for part in range(2):
                    q_centre(0, 0, part)
                for part in range(2):
                    q_total(0, 0, part)
                steps(dve, B, 2, rounds)
                statistics(B - 1)

            @block.scalar
            def _(act):
                def round_y(b, slot):
                    act.wait_ge(turned, b + 1)
                    if at_least(b, 2):
                        act.wait_ge(q_done, b * 2 - 2)
                    round_cols(act, y_hi[:, slot, :], PA).then_inc(rounded, 1)

                def k_keep(b, part):
                    act.wait_ge(k_turned, b * 2 + (part + 1))
                    if at_least(b, 1):
                        act.wait_ge(ky_done, b)
                    c, n = K_PARTS[part]
                    src = PB[:, :, :] if part == 0 else PC[:, 0:1, :]
                    act.copy(k_tok[:, c:c + n, :].rearrange("p (a c) s -> p a (c s)", c=2), src
                             ).then_inc(used[(B_, C)[part]], 1)

                def k_exps(b, slot, j):
                    act.wait_ge(k_shifted, b * 2 + (j + 1))
                    if at_least(b, 1):
                        act.wait_ge(k_turned, b * 2)
                    act.activation(k_exp[:, j, :].rearrange("p (h n) -> p h n", h=2), (PA, PB)[j][:, :, 0:HALF],
                                   ACT.Exp, bias=k_shift[:, j:j + 1], accum_out=k_sum[:, slot, j:j + 1]
                                   ).then_inc(used[(A, B_)[j]], 1)

                def ky_keep(b):
                    act.wait_ge(ky_done, b + 1)
                    if at_least(b, 1):
                        act.wait_ge(mix_done, b)
                    act.copy(ky[:, :], p_ky).then_inc(ky_kept, 1)

                def q_exps(b, slot, part):
                    over(act, f"q{part}", b)
                    c, n = Q_PARTS[part]
                    q = q_sb[:, slot, c * S_HEADS:(c + n) * S_HEADS, :]
                    act.activation(q, q, ACT.Exp).then_inc(q_exped, 1)

                def q_keep(b, j):
                    act.wait_ge(q_turned, b * 2 + (2 - j))
                    if at_least(b, 1):
                        act.wait_ge(out_done, b)
                    act.copy(q_cols[:, j, 0:512], (PB, PC)[j][:, 0, :])
                    act.copy(q_cols[:, j, 512:T], (PB, PC)[j][:, 1, 0:T - 512]).then_inc(used[(B_, C)[j]], 1)

                def rounds(b, slot):
                    nxt, more = 1 - slot, before(b, B - 1)
                    if more:
                        round_y(b + 1, nxt)
                    k_keep(b, 0)
                    k_keep(b, 1)
                    if more:
                        k_exps(b + 1, nxt, 0)
                        k_exps(b + 1, nxt, 1)
                    ky_keep(b)
                    q_keep(b, 1)
                    q_keep(b, 0)
                    if more:
                        q_exps(b + 1, nxt, 0)
                        q_exps(b + 1, nxt, 1)
                round_y(0, 0)
                for j in range(2):
                    k_exps(0, 0, j)
                for part in range(2):
                    q_exps(0, 0, part)
                steps(act, B, 2, rounds)


def mixture(nc, g, w, out):
    HID = 512
    BLOCKS = HID // P
    SHARED = 2
    TOP = 2
    ALL = SHARED + E_N
    with ExitStack() as ctx:
        def sb(name, shape, dt=F32):
            return ctx.enter_context(nc.sbuf_tensor(name, shape, dt))

        gates = nc.dram_tensor("e_gates", (P, T), F32, kind="Internal").ap()
        w1_hi = sb("e_w1_hi", [P, ALL * BLOCKS, P], F32R)
        w1_lo = sb("e_w1_lo", [P, ALL * BLOCKS, P], F32R)
        w2_hi = sb("e_w2_hi", [P, ALL * BLOCKS, P], F32R)
        w2_lo = sb("e_w2_lo", [P, ALL * BLOCKS, P], F32R)
        b1 = sb("e_b1", [P, 1, ALL * BLOCKS])
        b2 = sb("e_b2", [P, 1, E_N])
        shared_b2 = sb("e_sb2", [P, 1, SHARED])
        gate_bias = sb("e_gate_b", [P, E_N])
        with ExitStack() as inner:
            wg_hi = inner.enter_context(nc.sbuf_tensor("e_wg_hi", [P, 1, WIDE], F32R))
            wg_lo = inner.enter_context(nc.sbuf_tensor("e_wg_lo", [P, 1, WIDE], F32R))
            logits = inner.enter_context(nc.sbuf_tensor("e_logits", [P, TILES, B, E_N], F32))

            def ups(name, first, n):
                return [(w1_hi[:, (first + e) * BLOCKS:(first + e + 1) * BLOCKS, :],
                         w1_lo[:, (first + e) * BLOCKS:(first + e + 1) * BLOCKS, :],
                         w[name][e].rearrange("(j f) d -> f j d", f=P), True) for e in range(n)]

            def downs(name, first, n):
                return [(w2_hi[:, (first + e) * BLOCKS:(first + e + 1) * BLOCKS, :],
                         w2_lo[:, (first + e) * BLOCKS:(first + e + 1) * BLOCKS, :],
                         w[name][e].rearrange("d (j f) -> d j f", f=P), True) for e in range(n)]

            def bias_columns(name, first, n):
                return (b1[:, :, first * BLOCKS:(first + n) * BLOCKS], None,
                        w[name].rearrange("e (j o f) -> (e j) o f", o=1, f=P), True)

            weights_and_statistics(nc, g, [
                (wg_hi[:, :, AT:AT + E_N], wg_lo[:, :, AT:AT + E_N], w["L1_ffn_gate_w"].rearrange("e (o d) -> e o d", o=1), True),
                *ups("L1_ffn_sw1", 0, SHARED), *ups("L1_ffn_rw1", SHARED, E_N),
                *downs("L1_ffn_sw2", 0, SHARED), *downs("L1_ffn_rw2", SHARED, E_N),
                (b2[:, :, :], None, w["L1_ffn_rb2"].rearrange("e (o d) -> e o d", o=1), True),
                (shared_b2[:, :, :], None, w["L1_ffn_sb2"].rearrange("e (o d) -> e o d", o=1), True),
                bias_columns("L1_ffn_sb1", 0, SHARED), bias_columns("L1_ffn_rb1", SHARED, E_N)], "e", True)
            load_small(nc, [
                (gate_bias[:, :], w["L1_ffn_gate_b"].unsqueeze(0).broadcast_to([P, E_N]), None)], "e")
            with nc.Block() as block:
                @block.vector
                def _(dve):
                    dve.tensor_tensor(shared_b2[:, :, 0], shared_b2[:, :, 0], shared_b2[:, :, 1], ALU.add)
            router_logits(nc, g, wg_hi, wg_lo, gate_bias, logits, "e")
            route(nc, g, logits, gates, None, TOP, "e")
        gated_ffn(nc, g, w1_hi, w1_lo, b1, w2_hi, w2_lo, b2, shared_b2[:, 0, 0:1], BLOCKS, SHARED, gates, out, "e")


def audio_tower(nc, w, out):
    with ExitStack() as ctx:
        g = Shared()
        g.h = ctx.enter_context(nc.sbuf_tensor("h", [P, B * TILES, P], F32))
        g.mean = ctx.enter_context(nc.sbuf_tensor("mean", [P, B * TILES], F32))
        g.rstd = ctx.enter_context(nc.sbuf_tensor("rstd", [P, B * TILES], F32))
        g.stats = ctx.enter_context(nc.sbuf_tensor("stats", [P, B * TILES, 6], F32))
        constants(nc, ctx, g)
        quasi_recurrent(nc, g, w["x"], w["L0_tok_kernel"])
        cross_attention(nc, g, w)
        expert_choice(nc, g, w)
        slice_attention(nc, g, w)
        mixture(nc, g, w, out)


_INS = ['x', 'L0_tok_kernel', 'L0_attn_q_w', 'L0_attn_kv_w', 'L0_ffn_Wg', 'L0_ffn_W1', 'L0_ffn_b1', 'L0_ffn_W2',
        'L0_ffn_b2', 'L1_attn_W_in', 'L1_attn_b_in', 'L1_attn_Wq', 'L1_attn_Wk', 'L1_attn_Wv', 'L1_attn_W_out',
        'L1_attn_b_out', 'L1_ffn_gate_w', 'L1_ffn_gate_b', 'L1_ffn_sw1', 'L1_ffn_sb1', 'L1_ffn_sw2', 'L1_ffn_sb2',
        'L1_ffn_rw1', 'L1_ffn_rb1', 'L1_ffn_rw2', 'L1_ffn_rb2']


def kernel(**inputs):
    import numpy as _np
    import concourse.bacc as _bacc
    from concourse import mybir as _mybir
    from concourse.bass_utils import run_bass_kernel_spmd as _run

    nc = _bacc.Bacc("TRN2", target_bir_lowering=False, num_devices=1)
    arrays, aps = {}, {}
    for name in _INS:
        a = _np.ascontiguousarray(inputs[name])
        arrays[f"in_{name}_dram"] = a
        aps[name] = nc.dram_tensor(f"in_{name}_dram", a.shape, _mybir.dt.from_np(a.dtype), kind="ExternalInput").ap()
    out = nc.dram_tensor("out_0_dram", (B, T, P), _mybir.dt.float32, kind="ExternalOutput").ap()
    audio_tower(nc, aps, out)
    r = _run(nc, [arrays], core_ids=[0])
    return r.results[0]["out_0_dram"]
```
